# Optimizing a Trainium2 kernel written in Bass

```python
import numpy as np
import jax
import jax.numpy as jnp

def _softmax(x, axis=-1):
    return jax.nn.softmax(x, axis=axis)

def _gelu(x):
    return jax.nn.gelu(x, approximate=True)

def _silu(x):
    return jax.nn.silu(x)

def _sigmoid(x):
    return jax.nn.sigmoid(x)

def _layernorm(x, axis=-1, eps=1e-05):
    m = jnp.mean(x, axis=axis, keepdims=True)
    v = jnp.var(x, axis=axis, keepdims=True)
    return (x - m) / jnp.sqrt(v + eps)

def _scatter_add(tgt, idx, src, axis=0):
    return tgt.at[idx].add(src)

def _segment_sum(src, seg, n):
    return jax.ops.segment_sum(src, seg, n)
kernel_name = 'mk_seq_preln_d1_jaxref_r8_ceba30'

def setup_inputs(seed: int=0):
    np.random.seed(seed)
    _w = jnp.asarray

    def _L0_attn_setup():
        import jax, jax.numpy as jnp
        import numpy as np
        H = 16
        EPS_DEN = 1e-06

        def _decay_scan(x, decay, init):
            xT = jnp.moveaxis(x, 2, 0)

            def step(s, xt):
                s = decay * s + xt
                return (s, s)
            _, ys = jax.lax.scan(step, init, xT)
            return jnp.moveaxis(ys, 0, 2)

        def _phi(z):
            return jax.nn.elu(z) + 1.0

        def _reference_tuple_inner(x, w_qkv, w_out, decay_param):
            B, T, Hid = x.shape
            D = Hid // H
            qkv = x @ w_qkv
            q, k, v = jnp.split(qkv, 3, axis=-1)

            def to_bhtd(t):
                return t.reshape(B, T, H, D).transpose(0, 2, 1, 3)
            q = _phi(to_bhtd(q))
            k = _phi(to_bhtd(k))
            v = to_bhtd(v)
            decay = jax.nn.sigmoid(decay_param).reshape(1, H, 1)
            init = jnp.zeros((B, H, D), dtype=x.dtype)
            running_kv = _decay_scan(k * v, decay, init)
            running_ksum = _decay_scan(k, decay, init)
            den = jnp.clip(jnp.sum(q * running_ksum, axis=-1, keepdims=True), EPS_DEN, None)
            out = q * running_kv / den
            out = out.transpose(0, 2, 1, 3).reshape(B, T, Hid) @ w_out
            new_kv = running_kv[:, :, -1, :]
            new_ksum = running_ksum[:, :, -1, :]
            return (out, new_kv, new_ksum)
        key = jax.random.key(seed)
        k1, k2, k3 = jax.random.split(key, 3)
        x = jax.random.normal(k1, (2, 512, 256), dtype=jnp.float32)
        w_qkv = jax.random.normal(k2, (256, 768), dtype=jnp.float32) * 0.02
        w_out = jax.random.normal(k3, (256, 256), dtype=jnp.float32) * 0.02
        decay_param = jnp.full((H,), 0.95, dtype=jnp.float32)
        return {'x': x, 'w_qkv': w_qkv, 'w_out': w_out, 'decay_param': decay_param}
    _L0_attn_in = _L0_attn_setup()

    def _L0_ffn_setup():
        import jax, jax.numpy as jnp
        import numpy as np
        B, S, H = (1, 64, 256)
        I = 192
        E = 32
        K = 4
        SCALE = 1.8
        key = jax.random.key(seed)
        ks = jax.random.split(key, 9)
        init = lambda k, shape: jax.random.normal(k, shape, jnp.float32) * (1.0 / np.sqrt(shape[-1]))
        return {'x': jax.random.normal(ks[0], (B, S, H), jnp.float32), 'router_w': init(ks[1], (E, H)), 'router_b': jnp.zeros((E,), jnp.float32), 'gate_w': init(ks[2], (E, I, H)), 'up_w': init(ks[3], (E, I, H)), 'down_w': init(ks[4], (E, H, I)), 'shared_gate_w': init(ks[5], (I, H)), 'shared_up_w': init(ks[6], (I, H)), 'shared_down_w': init(ks[7], (H, I))}
    _L0_ffn_in = _L0_ffn_setup()
    _d = {'L0_attn_x': _L0_attn_in['x'], 'L0_attn_w_qkv': _L0_attn_in['w_qkv'], 'L0_attn_w_out': _L0_attn_in['w_out'], 'L0_attn_decay_param': _L0_attn_in['decay_param'], 'L0_ffn_router_w': _L0_ffn_in['router_w'], 'L0_ffn_router_b': _L0_ffn_in['router_b'], 'L0_ffn_gate_w': _L0_ffn_in['gate_w'], 'L0_ffn_up_w': _L0_ffn_in['up_w'], 'L0_ffn_down_w': _L0_ffn_in['down_w'], 'L0_ffn_shared_gate_w': _L0_ffn_in['shared_gate_w'], 'L0_ffn_shared_up_w': _L0_ffn_in['shared_up_w'], 'L0_ffn_shared_down_w': _L0_ffn_in['shared_down_w']}
    _x0 = _d['L0_attn_x']
    _d['L0_attn_x'] = jax.random.normal(jax.random.fold_in(jax.random.key(seed), 1), (8, 512, 256), dtype=_x0.dtype)
    del _x0
    return _d

def reference(L0_attn_x, L0_attn_w_qkv, L0_attn_w_out, L0_attn_decay_param, L0_ffn_router_w, L0_ffn_router_b, L0_ffn_gate_w, L0_ffn_up_w, L0_ffn_down_w, L0_ffn_shared_gate_w, L0_ffn_shared_up_w, L0_ffn_shared_down_w):

    def _L0_attn_ref(x, w_qkv, w_out, decay_param):
        import jax, jax.numpy as jnp
        import numpy as np
        H = 16
        EPS_DEN = 1e-06

        def _decay_scan(x, decay, init):
            xT = jnp.moveaxis(x, 2, 0)

            def step(s, xt):
                s = decay * s + xt
                return (s, s)
            _, ys = jax.lax.scan(step, init, xT)
            return jnp.moveaxis(ys, 0, 2)

        def _phi(z):
            return jax.nn.elu(z) + 1.0

        def _reference_tuple_inner(x, w_qkv, w_out, decay_param):
            B, T, Hid = x.shape
            D = Hid // H
            qkv = x @ w_qkv
            q, k, v = jnp.split(qkv, 3, axis=-1)

            def to_bhtd(t):
                return t.reshape(B, T, H, D).transpose(0, 2, 1, 3)
            q = _phi(to_bhtd(q))
            k = _phi(to_bhtd(k))
            v = to_bhtd(v)
            decay = jax.nn.sigmoid(decay_param).reshape(1, H, 1)
            init = jnp.zeros((B, H, D), dtype=x.dtype)
            running_kv = _decay_scan(k * v, decay, init)
            running_ksum = _decay_scan(k, decay, init)
            den = jnp.clip(jnp.sum(q * running_ksum, axis=-1, keepdims=True), EPS_DEN, None)
            out = q * running_kv / den
            out = out.transpose(0, 2, 1, 3).reshape(B, T, Hid) @ w_out
            new_kv = running_kv[:, :, -1, :]
            new_ksum = running_ksum[:, :, -1, :]
            return (out, new_kv, new_ksum)
        return _reference_tuple_inner(x, w_qkv, w_out, decay_param)[0]

    def _L0_ffn_ref(x, router_w, router_b, gate_w, up_w, down_w, shared_gate_w, shared_up_w, shared_down_w):
        import jax, jax.numpy as jnp
        import numpy as np
        B, S, H = (1, 64, 256)
        I = 192
        E = 32
        K = 4
        SCALE = 1.8
        b, s, h = x.shape
        xf = x.reshape(-1, h).astype(jnp.float32)
        logits = xf @ router_w.T + router_b
        top_vals, top_idx = jax.lax.top_k(logits, K)
        rw = jax.nn.softmax(top_vals, axis=-1) * SCALE
        combine = jnp.einsum('tke,tk->te', jax.nn.one_hot(top_idx, E, dtype=xf.dtype), rw)
        g = jax.nn.silu(jnp.einsum('th,eih->tei', xf, gate_w))
        u = jnp.einsum('th,eih->tei', xf, up_w)
        routed = jnp.einsum('tei,ehi,te->th', g * u, down_w, combine)
        sg = jax.nn.silu(xf @ shared_gate_w.T)
        su = xf @ shared_up_w.T
        shared = sg * su @ shared_down_w.T
        return (routed + shared).reshape(b, s, h)
    x = L0_attn_x
    x = x + _L0_attn_ref(_layernorm(x, axis=-1), L0_attn_w_qkv, L0_attn_w_out, L0_attn_decay_param)
    x = x + _L0_ffn_ref(_layernorm(x, axis=-1), L0_ffn_router_w, L0_ffn_router_b, L0_ffn_gate_w, L0_ffn_up_w, L0_ffn_down_w, L0_ffn_shared_gate_w, L0_ffn_shared_up_w, L0_ffn_shared_down_w)
    return x

_drawn_inputs = setup_inputs


def setup_inputs(seed=0):
    import zlib

    import numpy as np

    out = dict(_drawn_inputs(seed))
    spreads = {'L0_attn_decay_param': (0.949999988079071, 0.6), 'L0_ffn_router_b': (0.0, 0.1)}
    factors = {'L0_attn_w_qkv': 3.524, 'L0_attn_w_out': 3.43}
    for name, (base, spread) in spreads.items():
        noise = np.random.default_rng([zlib.crc32(name.encode()), seed]).standard_normal(out[name].shape)
        drawn = base * np.exp(spread * noise) if base else spread * noise
        out[name] = jnp.asarray(drawn.astype(out[name].dtype))
    for name, factor in factors.items():
        out[name] = (out[name] * factor).astype(out[name].dtype)
    return out
```

```python
import concourse.bass as bass
from concourse import mybir
from contextlib import ExitStack


def moe_block(nc, x, w_qkv, w_out, decay_param, router_w, router_b, gate_w, up_w, down_w,
              shared_gate_w, shared_up_w, shared_down_w, out):
    f32, f16, i32, u32 = mybir.dt.float32, mybir.dt.float16, mybir.dt.int32, mybir.dt.uint32
    ALU = mybir.AluOpType
    ACT = mybir.ActivationFunctionType
    AX = mybir.AxisListType

    P = 128
    NB, S, H = x.shape
    T = NB * S
    NT = T // P
    TS = S // P
    HC = H // P
    HEADS = decay_param.shape[0]
    D = H // HEADS
    E, I, _ = gate_w.shape
    K = 4
    LN_EPS = 1e-5
    DEN_EPS = 1e-6
    IC = I - P
    GU = 2 * I
    GUW = HC * 2 * GU
    DNW = 4 * H
    EW = GUW + DNW
    NE = E + 1
    PREP = 3
    EARLY = PREP * NB

    ROUTED = T * K // P + E
    TILES = ROUTED + NT
    ROUND = 4
    SCALE = 1.8

    xv = x.rearrange("b (j p) h -> b p j h", p=P)

    ctx = ExitStack()
    with ctx:
        def sb(name, shape, dt):
            return ctx.enter_context(nc.sbuf_tensor(name, shape, dt))

        def ps(name, shape, dt=f32):
            return ctx.enter_context(nc.psum_tensor(name, shape, dt))

        def sem(name):
            return ctx.enter_context(nc.semaphore(name))

        xn2_dram = nc.dram_tensor("xn2_scratch", [T, 2 * H], f16, kind="Internal").ap()
        x1_dram = nc.dram_tensor("x1_scratch", [T, H], f32, kind="Internal").ap()
        y_dram = nc.dram_tensor("y_scratch", [T * K + ROUTED * P, H], f32, kind="Internal").ap()
        y_v = y_dram[0:T * K].rearrange("(j p k) h -> j p k h", p=P, k=K)
        x1_tiles = x1_dram.rearrange("(j p) h -> j p h", p=P)
        xn2_tiles = xn2_dram.rearrange("(j p) h -> j p h", p=P)
        out_tiles = out.rearrange("b t h -> (b t) h").rearrange("(j p) h -> j p h", p=P)
        x1_v = x1_dram.rearrange("(b j p) h -> b p j h", j=TS, p=P)
        xn2_v = xn2_dram.rearrange("(b j p) h -> b p j h", j=TS, p=P)

        W = sb("W", [P, NE * EW], f16)
        LATE = (NE - EARLY) * EW // 2
        late = W[:, EARLY * EW:NE * EW].bitcast(f32)
        ARENA = 8960
        arena = sb("arena", [P, ARENA], f32)[:, :]

        def carver(region, size):
            at = [0]

            def carve(words):
                a = at[0]
                at[0] += words
                assert at[0] <= size, (at[0], size)
                return region[:, a:at[0]]
            return carve

        carve = carver(late, LATE)
        xnT = carve(HC * S).rearrange("p (c t) -> p c t", c=HC)
        wqkv_sb = carve(HC * 3 * H).rearrange("p (c n) -> p c n", c=HC)
        wout_sb = carve(HC * H).rearrange("p (c n) -> p c n", c=HC)
        kv = [carve(S) for _ in range(HC)]
        kphi = [carve(S) for _ in range(HC)]
        qks = [carve(S) for _ in range(HC)]
        qphi = [carve(S) for _ in range(HC)]
        ksum = [carve(S) for _ in range(HC)]
        kvsum = [carve(S) for _ in range(HC)]
        attnT = carve(HC * S).rearrange("p (c t) -> p c t", c=HC)
        xn = carve(TS * H).rearrange("p (j h) -> p j h", j=TS)

        blockones_at = carve(P)

        carve = carver(arena, ARENA)
        gu_nat = carve(PREP * 3 * H).rearrange("p (e m h) -> p e m h", e=PREP, m=3)
        dn_nat = carve(PREP * HC * (I + IC)).rearrange("p (e c i) -> p e c i", e=PREP, c=HC)
        x_sb = [carve(TS * H).rearrange("p (j h) -> p j h", j=TS) for _ in range(2)]
        x1_sb = carve(TS * H).rearrange("p (j h) -> p j h", j=TS)
        xn2 = xn
        xn2_split = carve(TS * H).bitcast(f16).rearrange("p (j s h) -> p j s h", j=TS, s=2)
        xT2 = [carve(H).bitcast(f16).rearrange("p (s c t) -> p s c t", s=2, c=HC) for _ in range(2)]

        STAGED = PREP * (3 * H + HC * (I + IC))
        carve = carver(arena[:, STAGED:], ARENA - STAGED)
        chosen = [carve(E * NT // 2).bitcast(f16) for _ in range(K)]
        dest = carve(E * NT)
        picked = carve(E * NT)
        wide = [carve(2 * H) for _ in range(2)]
        carve = carver(arena[:, STAGED + 3 * E * NT:], E * NT)
        RING = K
        lo_hot = [carve(P // 2).bitcast(f16) for _ in range(RING)]
        hi_hot = [carve(ROUTED).bitcast(f16).rearrange("p (v s) -> p v s", v=2) for _ in range(RING)]

        carve = carver(arena, ARENA)
        xg = [carve(H).bitcast(f16) for _ in range(ROUND)]
        xT = [carve(H).bitcast(f16).rearrange("p (s c t) -> p s c t", s=2, c=HC) for _ in range(2)]
        gate = [carve(I) for _ in range(2)]
        act32 = [carve(I) for _ in range(2)]
        aT_hi = [carve(P // 2).bitcast(f16) for _ in range(2)]
        aT_lo = [carve(P // 2).bitcast(f16) for _ in range(2)]
        aT_tail = [carve(P // 2).bitcast(f16) for _ in range(2)]
        y_sb = [carve(H) for _ in range(ROUND)]
        y4 = [carve(K * H).rearrange("p (k h) -> p k h", k=K) for _ in range(ROUND)]
        o_sb = [carve(H) for _ in range(ROUND)]

        ident32 = sb("ident32", [P, P], f32)
        ident16 = sb("ident16", [P, P], f16)
        decay_in = sb("decay_in", [HEADS, 1], f32)
        decay = sb("decay", [P, HC], f32)
        rb_row = sb("rb_row", [1, E], f32)
        rb = sb("rb", [P, E], f32)
        rwT = sb("rwT", [P, HC, 2, E], f16)
        logits = sb("logits", [P, TS, E], f32)
        top8 = sb("top8", [P, TS, 8], f32)
        idx8 = sb("idx8", [P, TS, 8], u32)
        zero = sb("zero", [P, 1], f32)
        carrier = sb("carrier", [P, 1], f32)
        eps = sb("eps", [P, TS], f32)
        topv = sb("topv", [P, NT, K], f32)
        topi = sb("topi", [P, NT, K], f32)
        iota_e = sb("iota_e", [P, E], f32)
        iota_s = sb("iota_s", [P, ROUTED], f16)
        row = sb("row", [P, 3], f32)
        before = sb("before", [P, P], f16)
        ones16 = sb("ones16", [P, P], f16)
        one = sb("one", [P, 1], f32)
        seen = sb("seen", [P, E], f32)
        counts = sb("counts", [P, E], f32)
        counts_i = sb("counts_i", [P, E], i32)
        tile_end = sb("tile_end", [P, E], f32)
        shift = sb("shift", [P, E], f32)
        owner = sb("owner", [P, 2], f32)
        owner_i = sb("owner_i", [1, ROUTED], i32)
        number = sb("number", [P, K * NT], f32)
        gtab = sb("gtab", [P, ROUTED], i32)
        stab = sb("stab", [P, ROUTED], i32)
        iota_i = stab
        slot_i = gtab[:, 0:K * NT]
        place, place_i = dest[:, 0:ROUTED], dest[:, ROUTED:2 * ROUTED].bitcast(i32)
        slot_hi = dest[:, 2 * ROUTED:2 * ROUTED + K * NT].rearrange("p (k j) -> p k j", k=K)
        slot_lo = dest[:, 2 * ROUTED + K * NT:2 * ROUTED + 2 * K * NT].rearrange("p (k j) -> p k j", k=K)
        slot = topi[:, :, :].rearrange("p j k -> p (j k)").rearrange("p (k j) -> p k j", k=K)
        share = topv
        gcur = sb("gcur", [P, ROUND], i32)
        scur = sb("scur", [P, ROUND], i32)
        share_sum = sb("share_sum", [P, NT], f32)
        mhalf = sb("mhalf", [P, TS], f32)
        stats = [sb(f"stats{n}", [P, TS, 6], f32) for n in range(2)]
        mv = [sb(f"mv{n}", [P, TS, 2], f32) for n in range(2)]
        vare = [sb(f"vare{n}", [P, TS], f32) for n in range(2)]
        rstd = [sb(f"rstd{n}", [P, TS], f32) for n in range(2)]
        blockones = blockones_at
        headsel = x1_sb[0:HEADS, 1, :]
        ones_row = x1_sb[0:1, 2, 0:P]
        rw_nat = x1_sb[0:E, 0, :]

        psT = [ps(f"psT{n}", [P, 512]) for n in range(3)]
        psK = ps("psK", [P, S])
        psQ = ps("psQ", [P, S])
        psV = ps("psV", [P, S])
        psD = ps("psD", [P, 2, S])
        psX = [psT[0][:, 0:H].bitcast(f16), psT[1][:, 0:H].bitcast(f16)]
        psG = [psK, psQ]
        psA = [psV, psT[2]]
        psY = [psD[:, 0, 0:H], psD[:, 1, 0:H]]

        consts_loaded = sem("consts_loaded")
        wattn_loaded = sem("wattn_loaded")
        x_loaded = [sem(f"x_loaded{n}") for n in range(2)]
        wstage_loaded = sem("wstage_loaded")
        x1_stored = sem("x1_stored")
        xn2_stored = sem("xn2_stored")
        setup_pool = sem("setup_pool")
        consts_made = sem("consts_made")
        setup_mm = sem("setup_mm")
        setup_act = sem("setup_act")
        setup_dve = sem("setup_dve")
        ln_stats = [sem(f"ln_stats{n}") for n in range(2)]
        ln_aggr = [sem(f"ln_aggr{n}") for n in range(2)]
        ln_vare = [sem(f"ln_vare{n}") for n in range(2)]
        ln_rstd = [sem(f"ln_rstd{n}") for n in range(2)]
        xn_ready = sem("xn_ready")
        xn_transposed = sem("xn_transposed")
        xnT_ready = sem("xnT_ready")
        k_ready, q_ready, v_ready = sem("k_ready"), sem("q_ready"), sem("v_ready")
        k_acted, q_acted = sem("k_acted"), sem("q_acted")
        kphi_done, kv_done, ksum_done = sem("kphi_done"), sem("kv_done"), sem("ksum_done")
        qphi_done, kvsum_done = sem("qphi_done"), sem("kvsum_done")
        qks_done, qkv_done = sem("qks_done"), sem("qkv_done")
        den_ready = sem("den_ready")
        den_clipped, den_inverted = sem("den_clipped"), sem("den_inverted")
        attn_done = sem("attn_done")
        proj_ready = sem("proj_ready")
        x1_done = sem("x1_done")
        xn2_ready = sem("xn2_ready")
        hi_done = sem("hi_done")
        split_done = sem("split_done")
        xn2_transposed = sem("xn2_transposed")
        xT2_ready = sem("xT2_ready")
        logits_ready = sem("logits_ready")
        logits_done = sem("logits_done")
        top_done = sem("top_done")
        topi_done = sem("topi_done")
        prep_transposed = sem("prep_transposed")
        tail_doubled = sem("tail_doubled")
        prep_hi = sem("prep_hi")
        prep_lo = sem("prep_lo")

        route_made = sem("route_made")
        chosen_done = sem("chosen_done")
        ranks_ready = sem("ranks_ready")
        chain = sem("chain")
        adjusted = sem("adjusted")
        picked_done = sem("picked_done")
        hot_done = sem("hot_done")
        placed = sem("placed")
        owner_done, owner_turned, owner_ready = sem("owner_done"), sem("owner_turned"), sem("owner_ready")
        tables_done = sem("tables_done")
        share_shifted, share_exp, share_done = sem("share_shifted"), sem("share_exp"), sem("share_done")
        gcur_done, scur_done = sem("gcur_done"), sem("scur_done")
        xg_loaded = [sem(f"xg_loaded{c}") for c in range(ROUND)]
        xs_loaded = [sem(f"xs_loaded{c}") for c in range(ROUND)]
        y_stored = [sem(f"y_stored{c}") for c in range(ROUND)]
        y4_loaded = [sem(f"y4_loaded{c}") for c in range(ROUND)]
        out_stored = [sem(f"out_stored{c}") for c in range(ROUND)]
        x_turned, xT_done = sem("x_turned"), sem("xT_done")
        gu_ready, silu_done, a_done = sem("gu_ready"), sem("silu_done"), sem("a_done")
        a_turned, aT_hi_done, aT_lo_done = sem("a_turned"), sem("aT_hi_done"), sem("aT_lo_done")
        y_ready, y_done, o_done, o_started = sem("y_ready"), sem("y_done"), sem("o_done"), sem("o_started")

        block = ctx.enter_context(nc.Block())

        R_ROUNDS, S_ROUNDS = ROUTED // ROUND, NT // ROUND
        ALL_ROUNDS = R_ROUNDS + S_ROUNDS

        def kind_of(tile, i, kind):
            if kind:
                return kind
            return None if tile < 0 or tile >= TILES else "routed" if tile < ROUTED else "shared"

        def rounds(eng, do):
            do(0, None)
            do(1, None)
            with eng.Fori(2, R_ROUNDS - 1) as i:
                do(i, "routed")
            do(R_ROUNDS - 1, None)
            do(R_ROUNDS, None)
            with eng.Fori(R_ROUNDS + 1, ALL_ROUNDS - 1) as i:
                do(i, "shared")
            do(ALL_ROUNDS - 1, None)
            do(ALL_ROUNDS, None)

        class Step:
            def __init__(self, b, parity, half, before=True, now=True, after=True):
                self.b, self.parity, self.half = b, parity, half
                self.before, self.now, self.after = before, now, after

        def steps(eng, do):
            do(Step(0, 0, 0, before=False))
            with eng.Fori(0, (NB - 2) // 2) as i:
                do(Step(2 * i + 1, 1, i))
                do(Step(2 * i + 2, 0, i + 1))
            do(Step(NB - 1, (NB - 1) % 2, (NB - 1) // 2, after=False))
            do(Step(NB, NB % 2, NB // 2, now=False, after=False))

        def wait_apart(eng, semaphore, value):
            eng.wait_ge(semaphore, value)
            nc.vector.memset(carrier[:, :], 0.0)

        SLOTS = [("prep", n) for n in range(6)] + [("xn2", j) for j in range(TS)] \
            + [("xn", c) for c in range(HC)] + [("prep", n) for n in range(6, 9)]
        assert len(SLOTS) % 3 == 0 and len(SLOTS) == 15

        def evacuated(kind, n, b):
            if kind == "prep":
                return prep_lo, 9 * b + n + 1
            if kind == "xn2":
                return xT2_ready, TS * (b - 1) + n + 1
            return xnT_ready, HC * (b + 1) + n + 1

        def there(kind, st):
            return {"prep": st.now, "xn2": st.before, "xn": st.after}[kind]

        def wait_bank(eng, slot, st):
            s = slot - 3
            while s >= 0:
                if there(SLOTS[s][0], st):
                    eng.wait_ge(*evacuated(*SLOTS[s], st.b))
                    return
                s -= 3
            if st.before:
                s += 15
                if there("prep", Step(0, 0, 0)) and not (st.now is False and False):
                    eng.wait_ge(*evacuated(*SLOTS[s], st.b - 1))
            elif s + 15 - 3 >= 10:
                eng.wait_ge(*evacuated(*SLOTS[s + 12], -1))

        def load_experts(eng, which):
            routed = PREP if which is not None else E % PREP
            if which is None:
                which = bass.ds(E - routed, routed)
            for src, dst in ((gate_w[which, 0:P], gu_nat[:, 0:routed, 0]), (gate_w[which, P:I], gu_nat[0:IC, 0:routed, 1]),
                             (up_w[which, 0:P - IC], gu_nat[IC:P, 0:routed, 1]), (up_w[which, P - IC:I], gu_nat[:, 0:routed, 2])):
                eng.dma_start(dst, src.rearrange("e p h -> p e h")).then_inc(wstage_loaded, 16)
            for q in range(routed):
                eng.dma_start(dn_nat[:, q, :, 0:I], down_w[which][q:q + 1].rearrange("e (c p) i -> p (e c) i", p=P)).then_inc(wstage_loaded, 16)
            if routed < PREP:
                for src, dst in ((shared_gate_w[0:P], gu_nat[:, routed, 0]), (shared_gate_w[P:I], gu_nat[0:IC, routed, 1]),
                                 (shared_up_w[0:P - IC], gu_nat[IC:P, routed, 1]), (shared_up_w[P - IC:I], gu_nat[:, routed, 2])):
                    eng.dma_start(dst, src).then_inc(wstage_loaded, 16)
                eng.dma_start(dn_nat[:, routed, :, 0:I], shared_down_w.rearrange("(c p) i -> p c i", p=P)).then_inc(wstage_loaded, 16)
        WSTAGE = 16 * (4 + PREP)
        LATE_STEPS = range(NB, -(-NE // PREP))
        LAST_WSTAGE = WSTAGE * LATE_STEPS[-1] + WSTAGE + 16 * 4

        def staged(b):
            return LAST_WSTAGE if isinstance(b, int) and b == LATE_STEPS[-1] else WSTAGE * b + WSTAGE

        WS = 256.0

        @block.sync
        def _(sp):
            def sp_round(i, kind):
                def tokens(c):
                    t = ROUND * i + c
                    if kind_of(t + ROUND, i, kind) == "shared":
                        sp.wait_ge(x_turned, t + 1)
                        sp.dma_start(xg[c], xn2_tiles[bass.ds(t + ROUND - ROUTED, 1)].rearrange("o p h -> p (o h)")).then_inc(xs_loaded[c], 16)

                def given(c):
                    t = ROUND * i + c
                    if kind_of(t, i, kind) == "shared":
                        if not first:
                            sp.wait_ge(out_stored[c], 16 * (i - R_ROUNDS))
                        sp.dma_start(y4[c], y_v[bass.ds(t - ROUTED, 1)].rearrange("o p k h -> p (o k) h")).then_inc(y4_loaded[c], 16)
                        sp.dma_start(o_sb[c], x1_tiles[bass.ds(t - ROUTED, 1)].rearrange("o p h -> p (o h)")).then_inc(y4_loaded[c], 16)

                first = isinstance(i, int) and i == R_ROUNDS
                if first:
                    for c in range(ROUND):
                        tokens(c)
                    for c in range(ROUND):
                        sp.wait_ge(y_stored[c], 16 * R_ROUNDS)
                    for c in range(ROUND):
                        given(c)
                else:
                    for c in range(ROUND):
                        tokens(c)
                        given(c)
                if isinstance(i, int) and i == ALL_ROUNDS:
                    for c in range(ROUND):
                        sp.wait_ge(out_stored[c], 16 * S_ROUNDS)

            sp.dma_start(x_sb[0], xv[0]).then_inc(x_loaded[0], 16)
            sp.dma_start(wqkv_sb, w_qkv.rearrange("(c p) n -> p c n", p=P)).then_inc(wattn_loaded, 16)
            sp.dma_start(x_sb[1], xv[1]).then_inc(x_loaded[1], 16)
            load_experts(sp, bass.ds(0, PREP))

            def step(st):
                if st.before:
                    sp.wait_ge(x1_done, 2 * st.b)
                    sp.dma_start(x1_v[bass.ds(st.b - 1, 1)].rearrange("o p j h -> p (o j) h"), x1_sb).then_inc(x1_stored, 16)
                    if st.after:
                        sp.wait_ge(x1_stored, 16 * st.b)
                        sp.dma_start(x_sb[1 - st.parity], xv[bass.ds(st.b + 1, 1)].rearrange("o p j h -> p (o j) h")).then_inc(x_loaded[1 - st.parity], 16)
                    sp.wait_ge(split_done, st.b)
                    sp.dma_start(xn2_v[bass.ds(st.b - 1, 1)].rearrange("o p j h -> p (o j) h"),
                                 xn2_split.rearrange("p j s h -> p j (s h)")).then_inc(xn2_stored, 16)
                if st.now:
                    if st.before:
                        sp.wait_ge(xn2_stored, 16 * st.b)
                    sp.wait_ge(prep_transposed, 9 * st.b + 9)
                    load_experts(sp, bass.ds(PREP * st.b + PREP, PREP))
            steps(sp, step)
            for b in LATE_STEPS[1:]:
                sp.wait_ge(prep_transposed, 9 * b)
                load_experts(sp, bass.ds(PREP * b, PREP) if b < LATE_STEPS[-1] else None)
            sp.wait_ge(x1_stored, 16 * NB)
            sp.wait_ge(xn2_stored, 16 * NB)
            rounds(sp, sp_round)

        def w_halves(e, part):
            off = 2 * part * GU if part < HC else GUW
            width = GU if part < HC else 2 * H
            return W[:, bass.ds(e * EW + off, width)], W[:, bass.ds(e * EW + off + width, width)], width

        @block.gpsimd
        def _(pool):
            nc.gpsimd.memset(ident32[:, :], 0.0).then_inc(setup_pool, 1)
            nc.gpsimd.memset(headsel, 0.0).then_inc(setup_pool, 1)
            nc.gpsimd.memset(ones_row, 1.0).then_inc(consts_made, 1)
            nc.gpsimd.memset(mhalf[:, :], -0.5).then_inc(consts_made, 1)
            nc.gpsimd.memset(zero[:, :], 0.0).then_inc(consts_made, 1)
            nc.gpsimd.memset(eps[:, :], LN_EPS).then_inc(consts_made, 1)
            pool.wait_ge(setup_pool, 2)
            nc.gpsimd.affine_select(out=ident32[:, :], in_=ident32[:, :], compare_op=ALU.not_equal, fill=1.0,
                                    base=0, pattern=[[-1, P]], channel_multiplier=1).then_inc(consts_made, 1)
            hv = headsel.rearrange("p (h d) -> p h d", d=D)
            nc.gpsimd.affine_select(out=hv, in_=hv, compare_op=ALU.not_equal, fill=1.0,
                                    base=0, pattern=[[-1, HEADS], [0, D]], channel_multiplier=1).then_inc(consts_made, 1)
            pool.wait_ge(consts_made, 6)
            nc.gpsimd.tensor_copy(ident16[:, :], ident32[:, :]).then_inc(consts_made, 1)

            nc.gpsimd.iota(iota_i[:, :], [[1, ROUTED]], base=0, channel_multiplier=0).then_inc(setup_pool, 1)
            nc.gpsimd.memset(before[:, :], -1.0).then_inc(setup_pool, 1)
            nc.gpsimd.memset(ones16[:, :], 1.0).then_inc(route_made, 1)
            nc.gpsimd.memset(one[:, :], 1.0).then_inc(route_made, 1)
            nc.gpsimd.iota(counts_i[:, 0:3], [[1, 3]], base=0, channel_multiplier=1).then_inc(setup_pool, 1)
            pool.wait_ge(setup_pool, 5)
            nc.gpsimd.tensor_copy(iota_e[:, :], iota_i[:, 0:E]).then_inc(route_made, 1)
            nc.gpsimd.tensor_copy(iota_s[:, :], iota_i[:, :]).then_inc(route_made, 1)
            nc.gpsimd.tensor_scalar(number[:, :], iota_i[:, 0:K * NT], float(P), float(P), ALU.mult, ALU.add).then_inc(route_made, 1)
            nc.gpsimd.affine_select(out=before[:, :], in_=before[:, :], compare_op=ALU.is_ge, fill=0.0,
                                    base=0, pattern=[[-1, P]], channel_multiplier=1).then_inc(route_made, 1)
            nc.gpsimd.tensor_scalar(row[:, 0:1], counts_i[:, 0:1], 0.0, None, ALU.add).then_inc(route_made, 1)
            nc.gpsimd.tensor_scalar(row[:, 1:2], counts_i[:, 0:1], float(P), None, ALU.add).then_inc(route_made, 1)
            nc.gpsimd.tensor_scalar(row[:, 2:3], counts_i[:, 0:1], float(T * K), None, ALU.add).then_inc(route_made, 1)

            def hold(semaphore, value):
                if not isinstance(value, int):
                    value = pool.to_reg(value)
                    pool.wait_ge(route_made, 9)
                pool.wait_ge(semaphore, value)

            def pool_round(i, kind):
                for c in range(ROUND):
                    t = ROUND * i + c
                    if kind_of(t + ROUND, i, kind) == "routed":
                        hold(x_turned, t + 1)
                        nc.gpsimd.tensor_copy(gcur[:, c:c + 1], gtab[:, bass.ds(t + ROUND, 1)]).then_inc(gcur_done, 1)
                        hold(gcur_done, t + 2)
                        gather(c)
                    if kind_of(t - ROUND, i, kind) == "routed":
                        hold(y_done, t - ROUND + 1)
                        nc.gpsimd.tensor_copy(scur[:, c:c + 1], stab[:, bass.ds(t - ROUND, 1)]).then_inc(scur_done, 1)
                        hold(scur_done, t - ROUND + 1)
                        nc.gpsimd.indirect_dma_start(y_dram[:, :], bass.IndirectOffsetOnAxis(ap=scur[:, c:c + 1], axis=0), y_sb[c], None).then_inc(y_stored[c], 16)
                for c in range(ROUND):
                    t = ROUND * i + c
                    if kind_of(t - 2, i, kind) == "shared":
                        j, r = t - 2 - ROUTED, (c - 2) % ROUND
                        hold(o_done, j + 1)
                        pool.dma_start(out_tiles[bass.ds(j, 1)].rearrange("o p h -> p (o h)"), o_sb[r]).then_inc(out_stored[r], 16)

            def gather(c):
                nc.gpsimd.indirect_dma_start(xg[c], None, xn2_dram[:, :], bass.IndirectOffsetOnAxis(ap=gcur[:, c:c + 1], axis=0)).then_inc(xg_loaded[c], 16)

            def root(n, b):
                pool.wait_ge(ln_aggr[n], TS * b + TS)
                nc.gpsimd.tensor_tensor(vare[n][:, :], mv[n][:, :, 1], eps[:, :], ALU.add).then_inc(ln_vare[n], 1)
                pool.wait_ge(ln_vare[n], b + 1)
                nc.gpsimd.tensor_tensor(rstd[n][:, :], vare[n][:, :], mhalf[:, :], ALU.pow).then_inc(ln_rstd[n], 1)

            def double_tail(b):
                pool.wait_ge(wstage_loaded, staged(b))
                nc.gpsimd.tensor_tensor(dn_nat[:, :, :, I:I + IC], dn_nat[:, :, :, P:I],
                                        zero[:, :].unsqueeze(1).unsqueeze(1).to_broadcast([P, PREP, HC, IC]), ALU.add).then_inc(tail_doubled, 1)

            def q_products(b, c):
                pool.wait_ge(qphi_done, HC * b + c + 1)
                pool.wait_ge(ksum_done, HC * b + c + 1)
                nc.gpsimd.tensor_tensor(qks[c], qphi[c], ksum[c], ALU.mult).then_inc(qks_done, 1)
                pool.wait_ge(kvsum_done, HC * b + c + 1)
                nc.gpsimd.tensor_tensor(kvsum[c], qphi[c], kvsum[c], ALU.mult).then_inc(qkv_done, 1)

            def step(st):
                b = st.b
                if st.now:
                    double_tail(b)
                if st.before:
                    root(1, b - 1)
                if st.now:
                    q_products(b, 0)
                if st.before:
                    pool.wait_ge(xn2_ready, TS * b)
                    if not st.now:
                        pool.wait_ge(xn2_stored, 16 * (b - 1))
                    nc.gpsimd.tensor_tensor(xn2_split[:, :, 0], xn2, zero[:, :].unsqueeze(1).to_broadcast([P, TS, H]), ALU.add).then_inc(hi_done, 1)
                    pool.wait_ge(hi_done, b)
                    nc.gpsimd.tensor_tensor(xn2_split[:, :, 1], xn2, xn2_split[:, :, 0], ALU.subtract).then_inc(split_done, 1)
                if st.after:
                    root(0, b + 1)
                if st.now:
                    q_products(b, 1)

            root(0, 0)
            steps(pool, step)
            for b in LATE_STEPS:
                double_tail(b)
                for n in range(9):
                    m = 9 * b + n
                    hi, lo, width = w_halves(PREP * b + n // 3, n % 3)
                    pool.wait_ge(prep_hi, m + 1)
                    nc.gpsimd.tensor_tensor(lo, wide[m % 2][:, 0:width], hi, ALU.subtract).then_inc(prep_lo, 1)
            pool.wait_ge(tables_done, 2)
            nc.gpsimd.tensor_copy(gcur[:, :], gtab[:, 0:ROUND]).then_inc(gcur_done, 1)
            pool.wait_ge(xn2_stored, 16 * NB)
            pool.wait_ge(prep_transposed, 9 * (LATE_STEPS[-1] + 1))
            hold(gcur_done, 1)
            for c in range(ROUND):
                gather(c)
            rounds(pool, pool_round)

        @block.scalar
        def _(act):
            act.dma_start(decay_in[:, :], decay_param.rearrange("(h o) -> h o", o=1)).then_inc(consts_loaded, 16)
            act.dma_start(rb_row[:, :], router_b.rearrange("(o e) -> o e", o=1)).then_inc(consts_loaded, 16)
            act.dma_start(rw_nat, router_w).then_inc(consts_loaded, 16)
            act.dma_start(wout_sb, w_out.rearrange("(c p) n -> p c n", p=P)).then_inc(wattn_loaded, 16)
            act.wait_ge(setup_mm, 1)
            nc.scalar.activation(decay[:, :], psK[:, 0:HC], ACT.Exp, scale=-1.0).then_inc(setup_act, 1)
            nc.scalar.activation(blockones, psQ[:, 0:P], ACT.Copy).then_inc(setup_act, 1)
            nc.scalar.activation(rb[:, :], psV[:, 0:E], ACT.Copy).then_inc(setup_act, 1)
            nc.scalar.activation(rwT[:, :, 0, :], psD[:, 0, 0:HC * E].rearrange("p (c e) -> p c e", c=HC), ACT.Copy).then_inc(setup_act, 1)

            def act_round(i, kind):
                for c in range(ROUND):
                    t = ROUND * i + c
                    if kind_of(t, i, kind):
                        act.wait_ge(gu_ready, t + 1)
                        nc.scalar.activation(gate[c % 2], psG[c % 2][:, 0:I], ACT.Silu, scale=1 / WS).then_inc(silu_done, 1)
                    if kind_of(t - 1, i, kind):
                        u = (c - 1) % 2
                        act.wait_ge(a_turned, t)
                        nc.scalar.activation(aT_hi[u], psA[u][:, 0:P], ACT.Copy).then_inc(aT_hi_done, 1)
                        nc.scalar.activation(aT_tail[u][0:IC], psA[u][0:IC, P:2 * P], ACT.Copy).then_inc(aT_hi_done, 1)
                    if kind_of(t - 2, i, kind) == "routed":
                        u = c % 2
                        y = (c - 2) % ROUND
                        act.wait_ge(y_ready, t - 1)
                        if kind or t - 2 >= ROUND:
                            act.wait_ge(y_stored[y], 16 * (i if c >= 2 else i - 1))
                        nc.scalar.activation(y_sb[y], psY[u], ACT.Copy, scale=1 / WS).then_inc(y_done, 1)

            def xn_out(b):
                for c in range(HC):
                    act.wait_ge(xn_transposed, HC * b + c + 1)
                    nc.scalar.activation(xnT[:, c, :], psT[(10 + c) % 3][:, :], ACT.Copy).then_inc(xnT_ready, 1)

            def prep_out(b, n):
                act.wait_ge(prep_transposed, 9 * b + n + 1)
                dst, _, width = w_halves(PREP * b + n // 3, n % 3)
                nc.scalar.activation(dst, psT[n % 3][:, 0:width], ACT.Copy, scale=WS).then_inc(prep_hi, 1)

            def k_parts(b, c):
                act.wait_ge(k_ready, HC * b + c + 1)
                nc.scalar.activation(kv[c], psK[:, :], ACT.Exp)
                nc.scalar.activation(kphi[c], psK[:, :], ACT.Relu).then_inc(k_acted, 1)

            def q_parts(b, c):
                act.wait_ge(q_ready, HC * b + c + 1)
                nc.scalar.activation(qks[c], psQ[:, :], ACT.Exp)
                nc.scalar.activation(qphi[c], psQ[:, :], ACT.Relu).then_inc(q_acted, 1)

            def step(st):
                b = st.b
                if st.now:
                    k_parts(b, 0)
                    prep_out(b, 0)
                    q_parts(b, 0)
                    prep_out(b, 1)
                    prep_out(b, 2)
                    k_parts(b, 1)
                    prep_out(b, 3)
                    q_parts(b, 1)
                    prep_out(b, 4)
                    prep_out(b, 5)
                if st.before:
                    for j in range(TS):
                        act.wait_ge(xn2_transposed, TS * (b - 1) + j + 1)
                        nc.scalar.activation(xT2[j % 2].rearrange("p s c t -> p (s c t)"),
                                             psT[(6 + j) % 3][:, 0:H].bitcast(f16), ACT.Copy).then_inc(xT2_ready, 1)
                if st.after:
                    xn_out(b + 1)
                if st.now:
                    for n in range(6, 9):
                        prep_out(b, n)

            xn_out(0)
            steps(act, step)
            act.wait_ge(share_shifted, 1)
            nc.scalar.activation(share[:, :, :], share[:, :, :], ACT.Exp).then_inc(share_exp, 1)
            for b in LATE_STEPS:
                for n in range(9):
                    m = 9 * b + n
                    hi, _, width = w_halves(PREP * b + n // 3, n % 3)
                    act.wait_ge(prep_transposed, m + 1)
                    if m >= 9 * LATE_STEPS[0] + 2:
                        act.wait_ge(prep_lo, m - 1)
                    nc.scalar.activation(wide[m % 2][:, 0:width], psT[n % 3][:, 0:width], ACT.Copy, scale=WS)
                    nc.scalar.activation(hi, psT[n % 3][:, 0:width], ACT.Copy, scale=WS).then_inc(prep_hi, 1)
            rounds(act, act_round)

        @block.vector
        def _(dve):
            dve.wait_ge(setup_act, 4)
            nc.vector.tensor_scalar(decay[:, :], decay[:, :], 1.0, None, ALU.add).then_inc(setup_dve, 1)
            nc.vector.tensor_tensor(rwT[:, :, 1, :], psD[:, 0, 0:HC * E].rearrange("p (c e) -> p c e", c=HC),
                                    rwT[:, :, 0, :], ALU.subtract).then_inc(setup_dve, 1)
            dve.wait_ge(setup_dve, 2)
            nc.vector.reciprocal(decay[:, :], decay[:, :]).then_inc(setup_dve, 1)
            dve.wait_ge(setup_dve, 3)

            def norm_stats(n, src, b):
                for j in range(TS):
                    nc.vector.bn_stats(stats[n][:, j], src[:, j]).then_inc(ln_stats[n], 1)
                wait_apart(dve, ln_stats[n], TS * b + TS)
                for j in range(TS):
                    nc.vector.bn_aggr(mv[n][:, j], stats[n][:, j]).then_inc(ln_aggr[n], 1)

            def norm(n, dst, src, b, done):
                dve.wait_ge(ln_rstd[n], b + 1)
                for j in range(TS):
                    nc.vector.tensor_scalar(dst[:, j], src[:, j], mv[n][:, j, 0:1], rstd[n][:, j:j + 1],
                                            ALU.subtract, ALU.mult).then_inc(done, 1)

            def unit(b, c):
                n = HC * b + c
                dve.wait_ge(k_acted, n + 1)
                nc.vector.scalar_tensor_tensor(kphi[c], kv[c], 1.0, kphi[c], ALU.min, ALU.add).then_inc(kphi_done, 1)
                dve.wait_ge(q_acted, n + 1)
                nc.vector.scalar_tensor_tensor(qphi[c], qks[c], 1.0, qphi[c], ALU.min, ALU.add).then_inc(qphi_done, 1)
                dve.wait_ge(kphi_done, n + 1)
                dve.wait_ge(v_ready, n + 1)
                nc.vector.tensor_tensor(kv[c], psV[:, :], kphi[c], ALU.mult).then_inc(kv_done, 1)
                dec = decay[:, c:c + 1].to_broadcast([P, S])
                nc.vector.tensor_tensor_scan(ksum[c], dec, kphi[c], 0.0, ALU.mult, ALU.add).then_inc(ksum_done, 1)
                dve.wait_ge(kv_done, n + 1)
                nc.vector.tensor_tensor_scan(kvsum[c], dec, kv[c], 0.0, ALU.mult, ALU.add).then_inc(kvsum_done, 1)

            def prep_out(b, n):
                dve.wait_ge(prep_hi, 9 * b + n + 1)
                hi, dst, width = w_halves(PREP * b + n // 3, n % 3)
                nc.vector.scalar_tensor_tensor(dst, psT[n % 3][:, 0:width], WS, hi, ALU.mult, ALU.subtract).then_inc(prep_lo, 1)

            def step(st):
                b = st.b
                if st.before:
                    if not st.now:
                        dve.wait_ge(x1_stored, 16 * (b - 1))
                    for h in range(2):
                        dve.wait_ge(proj_ready, 2 * (b - 1) + h + 1)
                        nc.vector.tensor_tensor(x1_sb[:, 2 * h:2 * h + 2], psD[:, h, :].rearrange("p (j h) -> p j h", h=H),
                                                x_sb[1 - st.parity][:, 2 * h:2 * h + 2], ALU.add).then_inc(x1_done, 1)
                    dve.wait_ge(x1_done, 2 * b)
                    norm_stats(1, x1_sb, b - 1)
                if st.now:
                    unit(b, 0)
                    for n in range(3):
                        prep_out(b, n)
                if st.before:
                    if st.now:
                        dve.wait_ge(xn_transposed, HC * b + HC)
                    norm(1, xn2, x1_sb, b - 1, xn2_ready)
                if st.after:
                    dve.wait_ge(x_loaded[1 - st.parity], 16 * ((st.half if st.parity == 0 else st.half + 1) + 1))
                    norm_stats(0, x_sb[1 - st.parity], b + 1)
                if st.now:
                    unit(b, 1)
                    for n in range(3, 6):
                        prep_out(b, n)
                if st.after:
                    if st.before:
                        dve.wait_ge(split_done, b)
                    dve.wait_ge(xn_transposed, HC * b + HC)
                    norm(0, xn, x_sb[1 - st.parity], b + 1, xn_ready)
                if st.before:
                    dve.wait_ge(logits_ready, TS * b)
                    nc.vector.tensor_tensor(logits[:, :, :], psD[:, 0, 0:TS * E].rearrange("p (j e) -> p j e", e=E),
                                            rb[:, :].unsqueeze(1).to_broadcast([P, TS, E]), ALU.add).then_inc(logits_done, 1)
                    wait_apart(dve, logits_done, b)
                    for j in range(TS):
                        nc.vector.max(top8[:, j], logits[:, j]).then_inc(top_done, 1)
                    wait_apart(dve, top_done, TS * b)
                    for j in range(TS):
                        nc.vector.max_index(idx8[:, j], top8[:, j], logits[:, j]).then_inc(topi_done, 1)
                    dve.wait_ge(topi_done, (TS + 2) * (b - 1) + TS)
                    nc.vector.tensor_copy(topv[:, bass.ds(TS * (b - 1), TS), :], top8[:, :, 0:K]).then_inc(topi_done, 1)
                    nc.vector.tensor_copy(topi[:, bass.ds(TS * (b - 1), TS), :], idx8[:, :, 0:K]).then_inc(topi_done, 1)
                if st.now:
                    for n in range(6, 9):
                        prep_out(b, n)
                    for c in range(HC):
                        dve.wait_ge(den_ready, HC * b + c + 1)
                        nc.vector.tensor_scalar(ksum[c], psD[:, c, :], DEN_EPS, None, ALU.max).then_inc(den_clipped, 1)
                    for c in range(HC):
                        dve.wait_ge(den_clipped, HC * b + c + 1)
                        nc.vector.reciprocal(ksum[c], ksum[c]).then_inc(den_inverted, 1)
                    for c in range(HC):
                        dve.wait_ge(den_inverted, HC * b + c + 1)
                        dve.wait_ge(qkv_done, HC * b + c + 1)
                        nc.vector.tensor_tensor(attnT[:, c, :], kvsum[c], ksum[c], ALU.mult).then_inc(attn_done, 1)

            links = [0]

            def link(instruction):
                links[0] += 1
                instruction.then_inc(chain, 1)
                dve.wait_ge(chain, links[0])

            def dispatch():
                v = nc.vector
                dve.wait_ge(route_made, 9)
                dve.wait_ge(x1_stored, 16 * NB)
                dve.wait_ge(xn2_stored, 16 * NB)
                dve.wait_ge(topi_done, (TS + 2) * NB)
                link(v.tensor_copy(share_sum[:, :], topv[:, :, 0]))
                v.tensor_tensor(share[:, :, :], topv[:, :, :], share_sum[:, :].unsqueeze(2).to_broadcast([P, NT, K]), ALU.subtract).then_inc(share_shifted, 1)
                for k in range(K):
                    v.tensor_tensor(chosen[k].rearrange("p (e j) -> p e j", e=E), topi[:, :, k].unsqueeze(1).to_broadcast([P, E, NT]),
                                    iota_e[:, :].unsqueeze(2).to_broadcast([P, E, NT]), ALU.is_equal).then_inc(chosen_done, 1)
                dve.wait_ge(ranks_ready, 1)
                link(v.tensor_tensor_scan(dest, one[:, :].to_broadcast([P, E * NT]), psD[:, :, :].rearrange("p a b -> p (a b)"), 0.0, ALU.mult, ALU.add))
                dest_v = dest.rearrange("p (e j) -> p e j", e=E)
                v.memset(seen[:, 0:1], 0.0)
                link(v.tensor_copy(seen[:, 1:E], dest_v[:, 0:E - 1, NT - 1]))
                link(v.tensor_tensor(counts[:, :], dest_v[:, :, NT - 1], seen[:, :], ALU.subtract))
                link(v.tensor_scalar(counts_i[:, :], counts[:, :], float(P - 1), None, ALU.add))
                link(v.tensor_scalar(counts_i[:, :], counts_i[:, :], P.bit_length() - 1, None, ALU.arith_shift_right))
                link(v.tensor_copy(counts[:, :], counts_i[:, :]))
                link(v.tensor_tensor_scan(tile_end[:, :], one[:, :].to_broadcast([P, E]), counts[:, :], 0.0, ALU.mult, ALU.add))
                link(v.tensor_tensor(shift[:, :], tile_end[:, :], counts[:, :], ALU.subtract))
                link(v.scalar_tensor_tensor(shift[:, :], shift[:, :], float(P), seen[:, :], ALU.mult, ALU.subtract))
                half = E * NT // 2
                for n, bank in enumerate((psK, psQ)):
                    last = v.tensor_tensor(dest[:, n * half:(n + 1) * half], bank[:, :], dest[:, n * half:(n + 1) * half], ALU.add)
                link(last)
                link(v.tensor_tensor(dest_v, dest_v, shift[:, :].unsqueeze(2).to_broadcast([P, E, NT]), ALU.add))
                for k in range(K):
                    link(v.tensor_tensor(picked, chosen[k], dest, ALU.mult))
                    link(v.tensor_reduce(slot[:, k, :], picked.rearrange("p (e j) -> p j e", e=E), AX.X, ALU.add))
                flat = slot[:, :, :].rearrange("p k j -> p (k j)")
                hi, lo = slot_hi[:, :, :].rearrange("p k j -> p (k j)"), slot_lo[:, :, :].rearrange("p k j -> p (k j)")
                link(v.tensor_copy(slot_i, flat))
                link(v.tensor_scalar(slot_i, slot_i, P.bit_length() - 1, None, ALU.arith_shift_right))
                link(v.tensor_copy(hi, slot_i))
                link(v.scalar_tensor_tensor(lo, hi, -float(P), flat, ALU.mult, ALU.add))
                for n in range(2):
                    v.tensor_scalar((counts, shift)[n][:, :], tile_end[:, :], row[:, n:n + 1], None, ALU.is_le, ALU.add, accum_out=owner[:, n:n + 1]).then_inc(owner_done, 1)
                dve.wait_ge(owner_turned, 1)
                v.tensor_scalar(owner_i[:, :], psD[0:1, 0, 0:ROUTED], float(E - 1), None, ALU.min).then_inc(owner_ready, 1)

                def hot(j):
                    for k in range(K):
                        n = K * j + k
                        col = bass.ds(j, 1)
                        if not isinstance(j, int):
                            dve.wait_ge(placed, n - RING + 1)
                        v.tensor_scalar(lo_hot[k], iota_s[:, 0:P], slot_lo[:, k, col], None, ALU.is_equal)
                        v.tensor_scalar(hi_hot[k][:, 0], iota_s[:, :], slot_hi[:, k, col], number[:, bass.ds(n, 1)], ALU.is_equal, ALU.mult)
                        v.tensor_scalar(hi_hot[k][:, 1], iota_s[:, :], slot_hi[:, k, col], row[:, 0:1], ALU.is_equal, ALU.mult).then_inc(hot_done, 1)

                hot(0)
                with dve.Fori(1, NT) as j:
                    hot(j)
                dve.wait_ge(placed, K * NT)
                table = psV[:, 0:ROUTED]
                link(v.tensor_scalar(place, table, -float(P), 0.0, ALU.add, ALU.max))
                link(v.tensor_copy(place_i, place))
                v.tensor_scalar(gtab[:, :], place_i, (P * K).bit_length() - 1, P.bit_length() - 1, ALU.arith_shift_right, ALU.logical_shift_left)
                link(v.tensor_scalar(stab[:, :], place_i, P.bit_length() - 1, K - 1, ALU.arith_shift_right, ALU.bitwise_and))
                link(v.tensor_scalar(place_i, place_i, P - 1, None, ALU.bitwise_and))
                link(v.tensor_tensor(gtab[:, :], gtab[:, :], place_i, ALU.add))
                link(v.tensor_scalar(place, iota_s[:, :], float(P), row[:, 2:3], ALU.mult, ALU.add))
                v.scalar_tensor_tensor(place, table, 0.0, place, ALU.is_equal, ALU.mult)
                link(v.tensor_copy(place_i, gtab[:, :]))
                link(v.tensor_scalar(place_i, place_i, K.bit_length() - 1, None, ALU.logical_shift_left))
                link(v.tensor_tensor(stab[:, :], stab[:, :], place_i, ALU.add))
                link(v.tensor_copy(place_i, place))
                v.tensor_tensor(stab[:, :], stab[:, :], place_i, ALU.add).then_inc(tables_done, 2)
                dve.wait_ge(share_exp, 1)
                link(v.tensor_reduce(share_sum[:, :], share[:, :, :], AX.X, ALU.add))
                link(v.reciprocal(share_sum[:, :], share_sum[:, :]))
                v.scalar_tensor_tensor(share[:, :, :], share[:, :, :], SCALE, share_sum[:, :].unsqueeze(2).to_broadcast([P, NT, K]), ALU.mult, ALU.mult).then_inc(share_done, 1)
                dve.wait_ge(share_done, 1)

            def turn_out(tile, c):
                dve.wait_ge(x_turned, tile + 1)
                nc.vector.tensor_copy(xT[c % 2].rearrange("p s c t -> p (s c t)"), psX[c % 2]).then_inc(xT_done, 1)

            def dve_round(i, kind):
                if isinstance(i, int) and i == 0:
                    turn_out(0, 0)
                for c in range(ROUND):
                    t = ROUND * i + c
                    if kind_of(t + 1, i, kind):
                        turn_out(t + 1, c + 1)
                    if kind_of(t, i, kind):
                        dve.wait_ge(silu_done, t + 1)
                        nc.vector.scalar_tensor_tensor(act32[c % 2], psG[c % 2][:, I:GU], 1 / WS, gate[c % 2], ALU.mult, ALU.mult).then_inc(a_done, 1)
                    if kind_of(t - 1, i, kind):
                        u = (c - 1) % 2
                        dve.wait_ge(aT_hi_done, 2 * t)
                        nc.vector.tensor_tensor(aT_lo[u], psA[u][:, 0:P], aT_hi[u], ALU.subtract)
                        nc.vector.tensor_tensor(aT_tail[u][IC:P], psA[u][0:IC, P:2 * P], aT_tail[u][0:IC], ALU.subtract).then_inc(aT_lo_done, 1)
                    if kind_of(t - 2, i, kind) == "shared":
                        d = t - 2
                        r = (c - 2) % ROUND
                        j = d - ROUTED
                        rnd = i - R_ROUNDS if c >= 2 else i - R_ROUNDS - 1
                        dve.wait_ge(y4_loaded[r], 32 * (rnd + 1))
                        dve.wait_ge(y_ready, d + 1)
                        nc.vector.scalar_tensor_tensor(o_sb[r], psY[c % 2], 1 / WS, o_sb[r], ALU.mult, ALU.add).then_inc(y_done, 1)
                        for k in range(K):
                            if k == 0:
                                dve.wait_ge(y_done, d + 1)
                            else:
                                dve.wait_ge(o_started, (K - 1) * j + k)
                            ins = nc.vector.scalar_tensor_tensor(o_sb[r], y4[r][:, k], share[:, bass.ds(j, 1), k], o_sb[r], ALU.mult, ALU.add)
                            ins.then_inc(o_started if k < K - 1 else o_done, 1)

            dve.wait_ge(x_loaded[0], 16)
            norm_stats(0, x_sb[0], 0)
            norm(0, xn, x_sb[0], 0, xn_ready)
            steps(dve, step)
            dispatch()
            rounds(dve, dve_round)

        @block.tensor
        def _(pe):
            pe.wait_ge(consts_made, 7)
            pe.wait_ge(consts_loaded, 48)
            for c in range(HC):
                nc.tensor.matmul(psK[:, c:c + 1], headsel[:, c * P:(c + 1) * P], decay_in[:, :], start=True, stop=True)
            nc.tensor.matmul(psQ[:, 0:P], headsel[:, 0:P], headsel[:, 0:P], start=True, stop=True)
            nc.tensor.matmul(psV[:, 0:E], ones_row, rb_row[:, :], start=True, stop=True)
            for c in range(HC):
                last = nc.tensor.transpose(psD[:, 0, c * E:(c + 1) * E], rw_nat[:, c * P:(c + 1) * P], ident32[0:E, 0:E])
            last.then_inc(setup_mm, 1)

            def xn_in(b):
                pe.wait_ge(xn_ready, TS * b + TS)
                for c in range(HC):
                    if isinstance(b, int) and b == 0:
                        pass
                    for j in range(TS):
                        last = nc.tensor.transpose(psT[(10 + c) % 3][:, j * P:(j + 1) * P], xn[:, j, c * P:(c + 1) * P], ident32[:, :])
                    last.then_inc(xn_transposed, 1)

            def prep_in(st, slot, n=None):
                if n is None:
                    n = SLOTS[slot][1]
                if n == 0:
                    pe.wait_ge(wstage_loaded, staged(st.b))
                if n == 2:
                    pe.wait_ge(tail_doubled, st.b + 1)
                if slot is not None:
                    wait_bank(pe, slot, st)
                else:
                    if 9 * st.b + n >= 9 * LATE_STEPS[0] + 3:
                        pe.wait_ge(prep_hi, 9 * st.b + n - 2)
                bank, q, part = psT[n % 3], n // 3, n % 3
                if part < HC:
                    for m in range(3):
                        last = nc.tensor.transpose(bank[:, m * P:(m + 1) * P], gu_nat[:, q, m, part * P:(part + 1) * P], ident32[:, :])
                else:
                    for c in range(HC):
                        nc.tensor.transpose(bank[:, c * P:(c + 1) * P], dn_nat[:, q, c, 0:P], ident32[:, :])
                        last = nc.tensor.transpose(bank[:, H + c * P:H + (c + 1) * P],
                                                   dn_nat[:, q, c, P:I + IC], ident32[:, :])
                last.then_inc(prep_transposed, 1)

            def late_and_dispatch():
                pe.wait_ge(route_made, 9)
                pe.wait_ge(topi_done, (TS + 2) * NB)
                half = E * NT // 2
                for k in range(K):
                    pe.wait_ge(chosen_done, k + 1)
                    for n, bank in enumerate((psK, psQ)):
                        nc.tensor.matmul(bank[:, :], before[:, :], chosen[k][:, n * half:(n + 1) * half], start=(k == 0), stop=(k == K - 1))
                        last = nc.tensor.matmul(psD[:, n, :], ones16[:, :], chosen[k][:, n * half:(n + 1) * half], start=(k == 0), stop=(k == K - 1))
                last.then_inc(ranks_ready, 1)
                pe.wait_ge(xT2_ready, NT)
                for b in LATE_STEPS:
                    for n in range(9):
                        prep_in(Step(b, 0, 0), None, n)
                pe.wait_ge(owner_done, 2)
                for w in range(2):
                    last = nc.tensor.transpose(psD[0:1, 0, w * P:(w + 1) * P], owner[:, w:w + 1], ident32[:, :])
                last.then_inc(owner_turned, 1)

                def hot(j):
                    for k in range(K):
                        n = K * j + k
                        pe.wait_ge(hot_done, n + 1)
                        for v in range(2):
                            last = nc.tensor.matmul(psV[:, 0:ROUTED], lo_hot[k], hi_hot[k][:, v], start=(isinstance(j, int) and j == 0 and k == 0 and v == 0),
                                                    stop=(isinstance(j, int) and j == NT - 1 and k == K - 1 and v == 1))
                        last.then_inc(placed, 1)

                hot(0)
                with pe.Fori(1, NT - 1) as j:
                    hot(j)
                hot(NT - 1)
                pe.wait_ge(owner_ready, 1)
                pe.wait_ge(tables_done, 2)
                pe.wait_ge(prep_lo, 9 * (LATE_STEPS[-1] + 1))

            def turn_in(tile, c, i, kind):
                if kind == "routed":
                    pe.wait_ge(xg_loaded[c % ROUND], 16 * (i + 1 + c // ROUND))
                else:
                    pe.wait_ge(xs_loaded[c % ROUND], 16 * (i + 1 + c // ROUND - R_ROUNDS))
                if not (isinstance(tile, int) and tile < 2):
                    pe.wait_ge(xT_done, tile - 1)
                for n in range(2 * HC):
                    last = nc.tensor.transpose(psX[c % 2][:, n * P:(n + 1) * P], xg[c % ROUND][:, n * P:(n + 1) * P], ident16[:, :])
                last.then_inc(x_turned, 1)

            def expert(tile, kind):
                if kind == "shared":
                    return E * EW
                if isinstance(tile, int):
                    return pe.value_load(owner_i[0:1, tile:tile + 1], min_val=0, max_val=E - 1) * EW
                return pe.value_load(owner_i[0:1, bass.ds(tile, 1)], min_val=0, max_val=E - 1) * EW

            def pe_round(i, kind):
                if isinstance(i, int) and i == 0:
                    turn_in(0, 0, 0, "routed")
                for c in range(ROUND):
                    t = ROUND * i + c
                    now, last_kind = kind_of(t, i, kind), kind_of(t - 2, i, kind)
                    if now:
                        at = expert(t, now)
                        pe.wait_ge(xT_done, t + 1)
                        if kind or t >= 2:
                            pe.wait_ge(a_done, t - 1)
                        n = 0
                        for sx, sw in ((0, 0), (0, 1), (1, 0)):
                            for h in range(HC):
                                last = nc.tensor.matmul(psG[c % 2][:, 0:GU], xT[c % 2][:, sx, h], W[:, bass.ds(at + (2 * h + sw) * GU, GU)],
                                                        start=(n == 0), stop=(n == 3 * HC - 1))
                                n += 1
                        last.then_inc(gu_ready, 1)
                    if kind_of(t + 1, i, kind):
                        turn_in(t + 1, c + 1, i, kind_of(t + 1, i, kind))
                    if kind_of(t - 1, i, kind):
                        u = (c - 1) % 2
                        pe.wait_ge(a_done, t)
                        if kind or t >= 3:
                            pe.wait_ge(aT_lo_done, t - 2)
                        nc.tensor.transpose(psA[u][:, 0:P], act32[u][:, 0:P], ident32[:, :])
                        nc.tensor.transpose(psA[u][0:IC, P:2 * P], act32[u][:, P:I], ident32[:, :]).then_inc(a_turned, 1)
                    if last_kind:
                        u = c % 2
                        at = expert(t - 2, last_kind)
                        pe.wait_ge(aT_lo_done, t - 1)
                        if kind or t >= 4:
                            pe.wait_ge(y_done, t - 3)
                        parts = ((aT_hi[u], 0, P), (aT_tail[u], 1, P), (aT_lo[u], 0, P), (aT_hi[u], 2, P), (aT_tail[u], 3, IC))
                        for n, (part, q, rows) in enumerate(parts):
                            last = nc.tensor.matmul(psY[u], part[0:rows], W[0:rows, bass.ds(at + GUW + q * H, H)], start=(n == 0), stop=(n == len(parts) - 1))
                        last.then_inc(y_ready, 1)

            def project(dst, st, c, which, acted, ready):
                n = HC * st.b + c
                if not (isinstance(n, int) and n == 0):
                    pe.wait_ge(acted, n)
                for h in range(HC):
                    last = nc.tensor.matmul(dst[:, :], wqkv_sb[:, h, which * H + c * P:which * H + (c + 1) * P], xnT[:, h, :],
                                            start=(h == 0), stop=(h == HC - 1))
                last.then_inc(ready, 1)

            def step(st):
                b = st.b
                if st.now:
                    pe.wait_ge(xnT_ready, HC * b + HC)
                    for c in range(HC):
                        project(psK, st, c, 1, k_acted, k_ready)
                        prep_in(st, 3 * c)
                        project(psQ, st, c, 0, q_acted, q_ready)
                        prep_in(st, 3 * c + 1)
                        project(psV, st, c, 2, kv_done, v_ready)
                        prep_in(st, 3 * c + 2)
                if st.before:
                    pe.wait_ge(split_done, b)
                    for j in range(TS):
                        wait_bank(pe, 6 + j, st)
                        bank = psT[(6 + j) % 3][:, 0:H].bitcast(f16)
                        for s in range(2):
                            for c in range(HC):
                                last = nc.tensor.transpose(bank[:, (s * HC + c) * P:(s * HC + c + 1) * P],
                                                           xn2_split[:, j, s, c * P:(c + 1) * P], ident16[:, :])
                        last.then_inc(xn2_transposed, 1)
                        if j >= 1:
                            route(b, j - 1)
                    route(b, TS - 1)
                if st.after:
                    for c in range(HC):
                        wait_bank(pe, 10 + c, st)
                    xn_in(b + 1)
                if st.now:
                    den(st, 0)
                    for n in range(6, 9):
                        prep_in(st, 6 + n)
                    den(st, 1)
                    pe.wait_ge(attn_done, HC * b + HC)
                    for j in range(TS):
                        for c in range(HC):
                            last = nc.tensor.matmul(psD[:, j // 2, (j % 2) * H:(j % 2 + 1) * H], attnT[:, c, j * P:(j + 1) * P],
                                                    wout_sb[:, c, :], start=(c == 0), stop=(c == HC - 1))
                        if j % 2:
                            last.then_inc(proj_ready, 1)

            def route(b, j):
                pe.wait_ge(xT2_ready, TS * (b - 1) + j + 1)
                if j == 0:
                    pe.wait_ge(x1_done, 2 * b)
                n = 0
                for sx, sw in ((0, 0), (0, 1), (1, 0)):
                    for c in range(HC):
                        last = nc.tensor.matmul(psD[:, 0, j * E:(j + 1) * E], xT2[j % 2][:, sx, c, :], rwT[:, c, sw, :],
                                                start=(n == 0), stop=(n == 3 * HC - 1))
                        n += 1
                last.then_inc(logits_ready, 1)

            def den(st, c):
                b = st.b
                pe.wait_ge(qks_done, HC * b + c + 1)
                if st.before and c == 0:
                    pe.wait_ge(logits_done, b)
                if st.before and c == 1:
                    pe.wait_ge(x1_done, 2 * b)
                nc.tensor.matmul(psD[:, c, :], blockones, qks[c], start=True, stop=True).then_inc(den_ready, 1)

            pe.wait_ge(setup_dve, 3)
            pe.wait_ge(wattn_loaded, 32)
            xn_in(0)
            steps(pe, step)
            late_and_dispatch()
            rounds(pe, pe_round)


_INS = ['L0_attn_x', 'L0_attn_w_qkv', 'L0_attn_w_out', 'L0_attn_decay_param', 'L0_ffn_router_w', 'L0_ffn_router_b',
        'L0_ffn_gate_w', 'L0_ffn_up_w', 'L0_ffn_down_w', 'L0_ffn_shared_gate_w', 'L0_ffn_shared_up_w', 'L0_ffn_shared_down_w']
_OUTS = [((8, 512, 256), 'float32')]


def kernel(**inputs):
    import numpy as _np
    import concourse.bacc as _bacc
    from concourse import mybir as _mybir
    from concourse.bass_utils import run_bass_kernel_spmd as _run

    nc = _bacc.Bacc("TRN2", target_bir_lowering=False, num_devices=1)
    arrays, args = {}, []
    for name in _INS:
        a = _np.ascontiguousarray(inputs[name])
        arrays[f"in_{name}_dram"] = a
        args.append(nc.dram_tensor(f"in_{name}_dram", a.shape, _mybir.dt.from_np(a.dtype), kind="ExternalInput").ap())
    for i, (shape, dtype) in enumerate(_OUTS):
        dt = _mybir.dt.from_np(_np.dtype(dtype))
        args.append(nc.dram_tensor(f"out_{i}_dram", shape, dt, kind="ExternalOutput").ap())
    moe_block(nc, *args)
    r = _run(nc, [arrays], core_ids=[0])
    got = tuple(r.results[0][f"out_{i}_dram"] for i in range(len(_OUTS)))
    return got[0]
```

```python
import concourse.bass as bass
from concourse import mybir
from contextlib import ExitStack


def moe_block(nc, x, w_qkv, w_out, decay_param, router_w, router_b, gate_w, up_w, down_w,
              shared_gate_w, shared_up_w, shared_down_w, out):
    f32, f16, i32, u32 = mybir.dt.float32, mybir.dt.float16, mybir.dt.int32, mybir.dt.uint32
    ALU = mybir.AluOpType
    ACT = mybir.ActivationFunctionType
    AX = mybir.AxisListType

    P = 128
    NB, S, H = x.shape
    T = NB * S
    NT = T // P
    TS = S // P
    HC = H // P
    HEADS = decay_param.shape[0]
    D = H // HEADS
    E, I, _ = gate_w.shape
    K = 4
    LN_EPS = 1e-5
    DEN_EPS = 1e-6
    IC = I - P
    GU = 2 * I
    GUW = HC * 2 * GU
    DNW = 4 * H
    EW = GUW + DNW
    NE = E + 1
    PREP = 3
    EARLY = PREP * NB

    ROUTED = T * K // P + E
    TILES = ROUTED + NT
    ROUND = 4
    SCALE = 1.8

    xv = x.rearrange("b (j p) h -> b p j h", p=P)

    ctx = ExitStack()
    with ctx:
        def sb(name, shape, dt):
            return ctx.enter_context(nc.sbuf_tensor(name, shape, dt))

        def ps(name, shape, dt=f32):
            return ctx.enter_context(nc.psum_tensor(name, shape, dt))

        def sem(name):
            return ctx.enter_context(nc.semaphore(name))

        xn2_dram = nc.dram_tensor("xn2_scratch", [T, 2 * H], f16, kind="Internal").ap()
        TERMS = K + 1
        y_dram = nc.dram_tensor("y_scratch", [T * TERMS + ROUTED * P, H], f32, kind="Internal").ap()
        y_v = y_dram[0:T * TERMS].rearrange("(j p k) h -> j p k h", p=P, k=TERMS)
        xn2_tiles = xn2_dram.rearrange("(j p) h -> j p h", p=P)
        out_tiles = out.rearrange("b t h -> (b t) h").rearrange("(j p) h -> j p h", p=P)
        x1_v = y_dram[0:T * TERMS].rearrange("(b j p k) h -> b k p j h", j=TS, p=P, k=TERMS)[:, K]
        xn2_v = xn2_dram.rearrange("(b j p) h -> b p j h", j=TS, p=P)

        W = sb("W", [P, NE * EW], f16)
        LATE = (NE - EARLY) * EW // 2
        late = W[:, EARLY * EW:NE * EW].bitcast(f32)
        ARENA = 8960
        arena = sb("arena", [P, ARENA], f32)[:, :]

        def carver(region, size):
            at = [0]

            def carve(words):
                a = at[0]
                at[0] += words
                assert at[0] <= size, (at[0], size)
                return region[:, a:at[0]]
            return carve

        carve = carver(late, LATE)
        xnT = carve(HC * S).rearrange("p (c t) -> p c t", c=HC)
        wqkv_sb = carve(HC * 3 * H).rearrange("p (c n) -> p c n", c=HC)
        wout_sb = carve(HC * H).rearrange("p (c n) -> p c n", c=HC)
        kv = [carve(S) for _ in range(HC)]
        kphi = [carve(S) for _ in range(HC)]
        qks = [carve(S) for _ in range(HC)]
        qphi = [carve(S) for _ in range(HC)]
        ksum = [carve(S) for _ in range(HC)]
        kvsum = [carve(S) for _ in range(HC)]
        attn_words = carve(HC * S)
        attnT = attn_words.rearrange("p (c t) -> p c t", c=HC)
        rden_rows = attn_words.rearrange("p (j h) -> p j h", j=TS)
        xn = carve(TS * H).rearrange("p (j h) -> p j h", j=TS)

        blockones_at = carve(P)
        rden = carve(TS * HEADS)

        carve = carver(arena, ARENA)
        gu_nat = carve(PREP * 3 * H).rearrange("p (e m h) -> p e m h", e=PREP, m=3)
        dn_nat = carve(PREP * HC * (I + IC)).rearrange("p (e c i) -> p e c i", e=PREP, c=HC)
        x_sb = [carve(TS * H).rearrange("p (j h) -> p j h", j=TS) for _ in range(2)]
        x1_sb = carve(TS * H).rearrange("p (j h) -> p j h", j=TS)
        xn2 = xn
        xn2_split = carve(TS * H).bitcast(f16).rearrange("p (j s h) -> p j s h", j=TS, s=2)
        xT2 = [carve(H).bitcast(f16).rearrange("p (s c t) -> p s c t", s=2, c=HC) for _ in range(2)]

        STAGED = PREP * (3 * H + HC * (I + IC))
        carve = carver(arena[:, STAGED:], ARENA - STAGED)
        chosen = [carve(E * NT // 2).bitcast(f16) for _ in range(K)]
        dest = carve(E * NT)
        picked = carve(E * NT)
        wide = [carve(2 * H) for _ in range(2)]
        carve = carver(arena[:, STAGED:], K * E * NT // 2)
        lo_hot = [carve(K * P).rearrange("p (k s) -> p k s", k=K) for _ in range(2)]
        hi_hot = [carve(ROUTED) for _ in range(K)]

        carve = carver(arena, ARENA)
        xg = [carve(H).bitcast(f16) for _ in range(ROUND)]
        xT = [carve(H).bitcast(f16).rearrange("p (s c t) -> p s c t", s=2, c=HC) for _ in range(2)]
        gate = [carve(I) for _ in range(2)]
        act32 = [carve(I) for _ in range(2)]
        aT_hi = [carve(P // 2).bitcast(f16) for _ in range(2)]
        aT_lo = [carve(P // 2).bitcast(f16) for _ in range(2)]
        aT_tail = [carve(P // 2).bitcast(f16) for _ in range(2)]
        y_sb = [carve(H) for _ in range(ROUND)]
        terms = [carve(TERMS * H).rearrange("p (k h) -> p k h", k=TERMS) for _ in range(ROUND)]
        o_sb = y_sb

        ident32 = sb("ident32", [P, P], f32)
        ident16 = sb("ident16", [P, P], f16)
        decay_in = sb("decay_in", [HEADS, 1], f32)
        decay = sb("decay", [P, HC], f32)
        rb_row = sb("rb_row", [1, E], f32)
        rb = sb("rb", [P, E], f32)
        rwT = sb("rwT", [P, HC, 2, E], f16)
        logits = sb("logits", [P, TS, E], f32)
        top8 = sb("top8", [P, TS, 8], f32)
        idx8 = sb("idx8", [P, TS, 8], u32)
        zero = sb("zero", [P, 1], f32)
        carrier = sb("carrier", [P, 1], f32)
        eps = sb("eps", [P, TS], f32)
        topv = sb("topv", [P, NT, K], f32)
        topi = sb("topi", [P, NT, K], f32)
        iota_e = sb("iota_e", [P, E], f32)
        iota_s = sb("iota_s", [P, ROUTED], f16)
        row = sb("row", [P, 3], f32)
        before = sb("before", [P, P], f16)
        ones16 = sb("ones16", [P, P], f16)
        one = sb("one", [P, 1], f32)
        seen = sb("seen", [P, E], f32)
        counts = sb("counts", [P, E], f32)
        counts_i = sb("counts_i", [P, E], i32)
        tile_end = sb("tile_end", [P, E], f32)
        shift = sb("shift", [P, E], f32)
        owner = sb("owner", [P, 2], f32)
        owner_i = sb("owner_i", [1, ROUTED + 2], i32)
        number = sb("number", [P, K * NT], f32)
        gtab = sb("gtab", [P, ROUTED], i32)
        stab = sb("stab", [P, ROUTED], i32)
        iota_i = stab
        slot_i = gtab[:, 0:K * NT]
        place, place_i = dest[:, 0:ROUTED], dest[:, ROUTED:2 * ROUTED].bitcast(i32)
        slot_hi = dest[:, 2 * ROUTED:2 * ROUTED + K * NT].rearrange("p (k j) -> p k j", k=K)
        slot_lo = dest[:, 2 * ROUTED + K * NT:2 * ROUTED + 2 * K * NT].rearrange("p (k j) -> p k j", k=K)
        slot = topi[:, :, :].rearrange("p j k -> p (j k)").rearrange("p (k j) -> p k j", k=K)
        share = topv
        gcur = sb("gcur", [P, ROUND], i32)
        scur = sb("scur", [P, ROUND], i32)
        share_sum = sb("share_sum", [P, NT], f32)
        mhalf = sb("mhalf", [P, TS], f32)
        stats = [sb(f"stats{n}", [P, TS, 6], f32) for n in range(2)]
        mv = [sb(f"mv{n}", [P, TS, 2], f32) for n in range(2)]
        vare = [sb(f"vare{n}", [P, TS], f32) for n in range(2)]
        rstd = [sb(f"rstd{n}", [P, TS], f32) for n in range(2)]
        blockones = blockones_at
        head_sums = blockones.rearrange("p (h d) -> p h d", d=D)[:, :, 0]
        headsel = x1_sb[0:HEADS, 1, :]
        ones_row = x1_sb[0:1, 2, 0:P]
        rw_nat = x1_sb[0:E, 0, :]

        psT = [ps(f"psT{n}", [P, 512]) for n in range(3)]
        psK = ps("psK", [P, S])
        psQ = ps("psQ", [P, S])
        psV = ps("psV", [P, S])
        psD = ps("psD", [P, 2, S])
        psX = [psT[0][:, 0:H].bitcast(f16), psT[1][:, 0:H].bitcast(f16)]
        psG = [psK, psQ]
        psA = [psV, psT[2]]
        psY = [psD[:, 0, 0:H], psD[:, 1, 0:H]]

        consts_loaded = sem("consts_loaded")
        wattn_loaded = sem("wattn_loaded")
        x_loaded = [sem(f"x_loaded{n}") for n in range(2)]
        wstage_loaded = sem("wstage_loaded")
        x1_stored = sem("x1_stored")
        xn2_stored = sem("xn2_stored")
        setup_pool = sem("setup_pool")
        consts_made = sem("consts_made")
        setup_mm = sem("setup_mm")
        setup_act = sem("setup_act")
        setup_dve = sem("setup_dve")
        ln_stats = [sem(f"ln_stats{n}") for n in range(2)]
        ln_aggr = [sem(f"ln_aggr{n}") for n in range(2)]
        ln_vare = [sem(f"ln_vare{n}") for n in range(2)]
        ln_rstd = [sem(f"ln_rstd{n}") for n in range(2)]
        xn_ready = sem("xn_ready")
        xn_transposed = sem("xn_transposed")
        xnT_ready = sem("xnT_ready")
        k_ready, q_ready, v_ready = sem("k_ready"), sem("q_ready"), sem("v_ready")
        k_acted, q_acted = sem("k_acted"), sem("q_acted")
        kphi_done, kv_done, ksum_done = sem("kphi_done"), sem("kv_done"), sem("ksum_done")
        qphi_done, kvsum_done = sem("qphi_done"), sem("kvsum_done")
        qks_done, qkv_done = sem("qks_done"), sem("qkv_done")
        den_ready = sem("den_ready")
        den_clipped, den_inverted = sem("den_clipped"), sem("den_inverted")
        rden_spread, rden_turned = sem("rden_spread"), sem("rden_turned")
        attn_done = sem("attn_done")
        proj_ready = sem("proj_ready")
        x1_done = sem("x1_done")
        xn2_ready = sem("xn2_ready")
        hi_done = sem("hi_done")
        split_done = sem("split_done")
        xn2_transposed = sem("xn2_transposed")
        xT2_ready = sem("xT2_ready")
        logits_ready = sem("logits_ready")
        logits_done = sem("logits_done")
        top_done = sem("top_done")
        topi_done = sem("topi_done")
        prep_transposed = sem("prep_transposed")
        tail_doubled = sem("tail_doubled")
        prep_hi = sem("prep_hi")
        prep_lo = sem("prep_lo")

        route_made = sem("route_made")
        chosen_done = sem("chosen_done")
        ranks_ready = sem("ranks_ready")
        chain = sem("chain")
        adjusted = sem("adjusted")
        picked_done = sem("picked_done")
        hot_done = sem("hot_done")
        placed = sem("placed")
        owner_done, owner_turned, owner_ready = sem("owner_done"), sem("owner_turned"), sem("owner_ready")
        tables_done = sem("tables_done")
        share_shifted, share_exp, share_done = sem("share_shifted"), sem("share_exp"), sem("share_done")
        gcur_done, scur_done = sem("gcur_done"), sem("scur_done")
        xg_loaded = [sem(f"xg_loaded{c}") for c in range(ROUND)]
        xs_loaded = [sem(f"xs_loaded{c}") for c in range(ROUND)]
        y_stored = [sem(f"y_stored{c}") for c in range(ROUND)]
        terms_loaded = [sem(f"terms_loaded{c}") for c in range(ROUND)]
        terms_scaled, pairs_added, terms_added = sem("terms_scaled"), sem("pairs_added"), sem("terms_added")
        out_stored = [sem(f"out_stored{c}") for c in range(ROUND)]
        x_turned, xT_done = sem("x_turned"), sem("xT_done")
        gu_ready, silu_done, a_done = sem("gu_ready"), sem("silu_done"), sem("a_done")
        a_turned, aT_hi_done, aT_lo_done = sem("a_turned"), sem("aT_hi_done"), sem("aT_lo_done")
        y_ready, y_done, o_done, o_started = sem("y_ready"), sem("y_done"), sem("o_done"), sem("o_started")

        block = ctx.enter_context(nc.Block())

        R_ROUNDS, S_ROUNDS = ROUTED // ROUND, NT // ROUND
        ALL_ROUNDS = R_ROUNDS + S_ROUNDS

        def kind_of(tile, i, kind):
            if kind:
                return kind
            return None if tile < 0 or tile >= TILES else "routed" if tile < ROUTED else "shared"

        def rounds(eng, do):
            do(0, None)
            do(1, None)
            with eng.Fori(2, R_ROUNDS - 2) as i:
                do(i, "routed")
            do(R_ROUNDS - 2, None)
            do(R_ROUNDS - 1, None)
            do(R_ROUNDS, None)
            with eng.Fori(R_ROUNDS + 1, ALL_ROUNDS - 1) as i:
                do(i, "shared")
            do(ALL_ROUNDS - 1, None)
            do(ALL_ROUNDS, None)

        class Step:
            def __init__(self, b, parity, half, before=True, now=True, after=True):
                self.b, self.parity, self.half = b, parity, half
                self.before, self.now, self.after = before, now, after
                self.prep = True

        def steps(eng, do):
            do(Step(0, 0, 0, before=False))
            with eng.Fori(0, (NB - 2) // 2) as i:
                do(Step(2 * i + 1, 1, i))
                do(Step(2 * i + 2, 0, i + 1))
            do(Step(NB - 1, (NB - 1) % 2, (NB - 1) // 2, after=False))
            do(Step(NB, NB % 2, NB // 2, now=False, after=False))

        def wait_apart(eng, semaphore, value):
            eng.wait_ge(semaphore, value)
            nc.vector.memset(carrier[:, :], 0.0)

        SLOTS = [("prep", n) for n in range(6)] + [("xn2", j) for j in range(TS)] \
            + [("xn", c) for c in range(HC)] + [("prep", n) for n in range(6, 9)]
        assert len(SLOTS) % 3 == 0 and len(SLOTS) == 15

        def evacuated(kind, n, b):
            if kind == "prep":
                return prep_lo, 9 * b + n + 1
            if kind == "xn2":
                return xT2_ready, TS * (b - 1) + n + 1
            return xnT_ready, HC * (b + 1) + n + 1

        def there(kind, st):
            return {"prep": st.prep, "xn2": st.before, "xn": st.after}[kind]

        def wait_bank(eng, slot, st):
            s = slot - 3
            while s >= 0:
                if there(SLOTS[s][0], st):
                    eng.wait_ge(*evacuated(*SLOTS[s], st.b))
                    return
                s -= 3
            if st.before:
                s += 15
                eng.wait_ge(*evacuated(*SLOTS[s], st.b - 1))
            elif s + 15 - 3 >= 10:
                eng.wait_ge(*evacuated(*SLOTS[s + 12], -1))

        def load_experts(eng, which):
            routed = PREP if which is not None else E % PREP
            if which is None:
                which = bass.ds(E - routed, routed)
            for src, dst in ((gate_w[which, 0:P], gu_nat[:, 0:routed, 0]), (gate_w[which, P:I], gu_nat[0:IC, 0:routed, 1]),
                             (up_w[which, 0:P - IC], gu_nat[IC:P, 0:routed, 1]), (up_w[which, P - IC:I], gu_nat[:, 0:routed, 2])):
                eng.dma_start(dst, src.rearrange("e p h -> p e h")).then_inc(wstage_loaded, 16)
            for q in range(routed):
                eng.dma_start(dn_nat[:, q, :, 0:I], down_w[which][q:q + 1].rearrange("e (c p) i -> p (e c) i", p=P)).then_inc(wstage_loaded, 16)
            if routed < PREP:
                for src, dst in ((shared_gate_w[0:P], gu_nat[:, routed, 0]), (shared_gate_w[P:I], gu_nat[0:IC, routed, 1]),
                                 (shared_up_w[0:P - IC], gu_nat[IC:P, routed, 1]), (shared_up_w[P - IC:I], gu_nat[:, routed, 2])):
                    eng.dma_start(dst, src).then_inc(wstage_loaded, 16)
                eng.dma_start(dn_nat[:, routed, :, 0:I], shared_down_w.rearrange("(c p) i -> p c i", p=P)).then_inc(wstage_loaded, 16)
        WSTAGE = 16 * (4 + PREP)
        LATE_STEPS = range(NB + 1, -(-NE // PREP))
        LAST_WSTAGE = WSTAGE * LATE_STEPS[-1] + WSTAGE + 16 * 4

        def staged(b):
            return LAST_WSTAGE if isinstance(b, int) and b == LATE_STEPS[-1] else WSTAGE * b + WSTAGE

        WS = 256.0

        @block.sync
        def _(sp):
            def sp_round(i, kind):
                def tokens(c):
                    t = ROUND * i + c
                    if kind_of(t + ROUND, i, kind) == "shared":
                        sp.wait_ge(x_turned, t + 1)
                        sp.dma_start(xg[c], xn2_tiles[bass.ds(t + ROUND - ROUTED, 1)].rearrange("o p h -> p (o h)")).then_inc(xs_loaded[c], 16)

                def given(c):
                    t = ROUND * i + c
                    if kind_of(t, i, kind) == "shared":
                        if not first:
                            sp.wait_ge(o_done, t - ROUND - ROUTED + 1)
                        sp.dma_start(terms[c], y_v[bass.ds(t - ROUTED, 1)].rearrange("o p k h -> p (o k) h")).then_inc(terms_loaded[c], 16)

                def result(c):
                    t = ROUND * i + c
                    if kind_of(t - ROUND, i, kind) == "shared":
                        j = t - ROUND - ROUTED
                        sp.wait_ge(o_done, j + 1)
                        sp.dma_start(out_tiles[bass.ds(j, 1)].rearrange("o p h -> p (o h)"), o_sb[c]).then_inc(out_stored[c], 16)

                first = isinstance(i, int) and i == R_ROUNDS
                if first:
                    for c in range(ROUND):
                        tokens(c)
                    for c in range(ROUND):
                        sp.wait_ge(y_stored[c], 16 * R_ROUNDS)
                    for c in range(ROUND):
                        given(c)
                else:
                    for c in range(ROUND):
                        tokens(c)
                        given(c)
                        result(c)
                if isinstance(i, int) and i == ALL_ROUNDS:
                    for c in range(ROUND):
                        sp.wait_ge(out_stored[c], 16 * S_ROUNDS)

            sp.dma_start(x_sb[0], xv[0]).then_inc(x_loaded[0], 16)
            sp.dma_start(wqkv_sb, w_qkv.rearrange("(c p) n -> p c n", p=P)).then_inc(wattn_loaded, 16)
            sp.dma_start(x_sb[1], xv[1]).then_inc(x_loaded[1], 16)
            load_experts(sp, bass.ds(0, PREP))

            def step(st):
                if st.before:
                    sp.wait_ge(x1_done, 2 * st.b)
                    if st.after:
                        sp.dma_start(x_sb[1 - st.parity], xv[bass.ds(st.b + 1, 1)].rearrange("o p j h -> p (o j) h")).then_inc(x_loaded[1 - st.parity], 16)
                    sp.dma_start(x1_v[bass.ds(st.b - 1, 1)].rearrange("o p j h -> p (o j) h"), x1_sb).then_inc(x1_stored, 16)
                    sp.wait_ge(split_done, st.b)
                    sp.dma_start(xn2_v[bass.ds(st.b - 1, 1)].rearrange("o p j h -> p (o j) h"),
                                 xn2_split.rearrange("p j s h -> p j (s h)")).then_inc(xn2_stored, 16)
                if st.prep:
                    if st.before:
                        sp.wait_ge(xn2_stored, 16 * st.b)
                    sp.wait_ge(prep_transposed, 9 * st.b + 9)
                    load_experts(sp, bass.ds(PREP * st.b + PREP, PREP))
            steps(sp, step)
            for b in LATE_STEPS[1:]:
                sp.wait_ge(prep_transposed, 9 * b)
                load_experts(sp, bass.ds(PREP * b, PREP) if b < LATE_STEPS[-1] else None)
            sp.wait_ge(x1_stored, 16 * NB)
            sp.wait_ge(xn2_stored, 16 * NB)
            rounds(sp, sp_round)

        def w_halves(e, part):
            off = 2 * part * GU if part < HC else GUW
            width = GU if part < HC else 2 * H
            return W[:, bass.ds(e * EW + off, width)], W[:, bass.ds(e * EW + off + width, width)], width

        @block.gpsimd
        def _(pool):
            nc.gpsimd.memset(ident32[:, :], 0.0).then_inc(setup_pool, 1)
            nc.gpsimd.memset(headsel, 0.0).then_inc(setup_pool, 1)
            nc.gpsimd.memset(ones_row, 1.0).then_inc(consts_made, 1)
            nc.gpsimd.memset(mhalf[:, :], -0.5).then_inc(consts_made, 1)
            nc.gpsimd.memset(zero[:, :], 0.0).then_inc(consts_made, 1)
            nc.gpsimd.memset(eps[:, :], LN_EPS).then_inc(consts_made, 1)
            pool.wait_ge(setup_pool, 2)
            nc.gpsimd.affine_select(out=ident32[:, :], in_=ident32[:, :], compare_op=ALU.not_equal, fill=1.0,
                                    base=0, pattern=[[-1, P]], channel_multiplier=1).then_inc(consts_made, 1)
            hv = headsel.rearrange("p (h d) -> p h d", d=D)
            nc.gpsimd.affine_select(out=hv, in_=hv, compare_op=ALU.not_equal, fill=1.0,
                                    base=0, pattern=[[-1, HEADS], [0, D]], channel_multiplier=1).then_inc(consts_made, 1)
            pool.wait_ge(consts_made, 6)
            nc.gpsimd.tensor_copy(ident16[:, :], ident32[:, :]).then_inc(consts_made, 1)

            nc.gpsimd.iota(iota_i[:, :], [[1, ROUTED]], base=0, channel_multiplier=0).then_inc(setup_pool, 1)
            nc.gpsimd.memset(before[:, :], -1.0).then_inc(setup_pool, 1)
            nc.gpsimd.memset(ones16[:, :], 1.0).then_inc(route_made, 1)
            nc.gpsimd.memset(one[:, :], 1.0).then_inc(route_made, 1)
            nc.gpsimd.iota(counts_i[:, 0:3], [[1, 3]], base=0, channel_multiplier=1).then_inc(setup_pool, 1)
            nc.gpsimd.iota(gtab[:, 0:K * NT], [[P, K * NT]], base=P, channel_multiplier=1).then_inc(setup_pool, 1)
            pool.wait_ge(setup_pool, 6)
            nc.gpsimd.tensor_copy(iota_e[:, :], iota_i[:, 0:E]).then_inc(route_made, 1)
            nc.gpsimd.tensor_copy(iota_s[:, :], iota_i[:, :]).then_inc(route_made, 1)
            nc.gpsimd.tensor_copy(number[:, :], gtab[:, 0:K * NT]).then_inc(route_made, 1)
            nc.gpsimd.affine_select(out=before[:, :], in_=before[:, :], compare_op=ALU.is_ge, fill=0.0,
                                    base=0, pattern=[[-1, P]], channel_multiplier=1).then_inc(route_made, 1)
            nc.gpsimd.tensor_scalar(row[:, 0:1], counts_i[:, 0:1], 0.0, None, ALU.add).then_inc(route_made, 1)
            nc.gpsimd.tensor_scalar(row[:, 1:2], counts_i[:, 0:1], float(P), None, ALU.add).then_inc(route_made, 1)
            nc.gpsimd.tensor_scalar(row[:, 2:3], counts_i[:, 0:1], float(T * TERMS), None, ALU.add).then_inc(route_made, 1)

            def hold(semaphore, value):
                if not isinstance(value, int):
                    value = pool.to_reg(value)
                    pool.wait_ge(route_made, 9)
                pool.wait_ge(semaphore, value)

            def pool_round(i, kind):
                for c in range(ROUND):
                    t = ROUND * i + c
                    if kind_of(t + ROUND, i, kind) == "routed":
                        hold(gcur_done, t + 2)
                        gather(c)
                    if kind_of(t - ROUND, i, kind) == "routed":
                        hold(scur_done, t - ROUND + 1)
                        nc.gpsimd.indirect_dma_start(y_dram[:, :], bass.IndirectOffsetOnAxis(ap=scur[:, c:c + 1], axis=0), y_sb[c], None).then_inc(y_stored[c], 16)
                for c in range(ROUND):
                    t = ROUND * i + c
                    if kind_of(t - 1, i, kind) == "shared":
                        j, r = t - 1 - ROUTED, (c - 1) % ROUND
                        pool.wait_ge(terms_scaled, j + 1)
                        nc.gpsimd.tensor_tensor(terms[r][:, 1:3], terms[r][:, 1:3], terms[r][:, 3:5], ALU.add).then_inc(pairs_added, 1)
                        pool.wait_ge(pairs_added, j + 1)
                        nc.gpsimd.tensor_tensor(terms[r][:, 1], terms[r][:, 1], terms[r][:, 2], ALU.add).then_inc(terms_added, 1)

            def gather(c):
                nc.gpsimd.indirect_dma_start(xg[c], None, xn2_dram[:, :], bass.IndirectOffsetOnAxis(ap=gcur[:, c:c + 1], axis=0)).then_inc(xg_loaded[c], 16)

            def root(n, b):
                pool.wait_ge(ln_aggr[n], TS * b + TS)
                nc.gpsimd.tensor_tensor(vare[n][:, :], mv[n][:, :, 1], eps[:, :], ALU.add).then_inc(ln_vare[n], 1)
                pool.wait_ge(ln_vare[n], b + 1)
                nc.gpsimd.tensor_tensor(rstd[n][:, :], vare[n][:, :], mhalf[:, :], ALU.pow).then_inc(ln_rstd[n], 1)

            def double_tail(b):
                pool.wait_ge(wstage_loaded, staged(b))
                nc.gpsimd.tensor_tensor(dn_nat[:, :, :, I:I + IC], dn_nat[:, :, :, P:I],
                                        zero[:, :].unsqueeze(1).unsqueeze(1).to_broadcast([P, PREP, HC, IC]), ALU.add).then_inc(tail_doubled, 1)

            def q_products(b, c):
                pool.wait_ge(qphi_done, HC * b + c + 1)
                pool.wait_ge(ksum_done, HC * b + c + 1)
                nc.gpsimd.tensor_tensor(qks[c], qphi[c], ksum[c], ALU.mult).then_inc(qks_done, 1)
                pool.wait_ge(kvsum_done, HC * b + c + 1)
                nc.gpsimd.tensor_tensor(kvsum[c], qphi[c], kvsum[c], ALU.mult).then_inc(qkv_done, 1)

            def step(st):
                b = st.b
                if st.prep:
                    double_tail(b)
                if st.now:
                    q_products(b, 0)
                if st.before:
                    root(1, b - 1)
                    pool.wait_ge(hi_done, b)
                    nc.gpsimd.tensor_tensor(xn2_split[:, :, 1], xn2, xn2_split[:, :, 0], ALU.subtract).then_inc(split_done, 1)
                if st.after:
                    root(0, b + 1)
                if st.now:
                    q_products(b, 1)

            root(0, 0)
            steps(pool, step)
            for b in LATE_STEPS:
                double_tail(b)
                for n in range(9):
                    m = 9 * b + n
                    hi, lo, width = w_halves(PREP * b + n // 3, n % 3)
                    pool.wait_ge(prep_hi, m + 1)
                    nc.gpsimd.tensor_tensor(lo, wide[m % 2][:, 0:width], hi, ALU.subtract).then_inc(prep_lo, 1)
            pool.wait_ge(xn2_stored, 16 * NB)
            pool.wait_ge(prep_transposed, 9 * (LATE_STEPS[-1] + 1))
            hold(gcur_done, 1)
            for c in range(ROUND):
                gather(c)
            rounds(pool, pool_round)

        @block.scalar
        def _(act):
            act.dma_start(decay_in[:, :], decay_param.rearrange("(h o) -> h o", o=1)).then_inc(consts_loaded, 16)
            act.dma_start(rb_row[:, :], router_b.rearrange("(o e) -> o e", o=1)).then_inc(consts_loaded, 16)
            act.dma_start(rw_nat, router_w).then_inc(consts_loaded, 16)
            act.dma_start(wout_sb, w_out.rearrange("(c p) n -> p c n", p=P)).then_inc(wattn_loaded, 16)
            act.wait_ge(setup_mm, 1)
            nc.scalar.activation(decay[:, :], psK[:, 0:HC], ACT.Exp, scale=-1.0).then_inc(setup_act, 1)
            nc.scalar.activation(blockones, psQ[:, 0:P], ACT.Copy).then_inc(setup_act, 1)
            nc.scalar.activation(rb[:, :], psV[:, 0:E], ACT.Copy).then_inc(setup_act, 1)
            nc.scalar.activation(rwT[:, :, 0, :], psD[:, 0, 0:HC * E].rearrange("p (c e) -> p c e", c=HC), ACT.Copy).then_inc(setup_act, 1)

            def act_round(i, kind):
                for c in range(ROUND):
                    t = ROUND * i + c
                    if kind_of(t, i, kind):
                        act.wait_ge(gu_ready, t + 1)
                        nc.scalar.activation(gate[c % 2], psG[c % 2][:, 0:I], ACT.Silu, scale=1 / WS).then_inc(silu_done, 1)
                    if kind_of(t - 1, i, kind):
                        u = (c - 1) % 2
                        act.wait_ge(a_turned, t)
                        nc.scalar.activation(aT_hi[u], psA[u][:, 0:P], ACT.Copy).then_inc(aT_hi_done, 1)
                        nc.scalar.activation(aT_tail[u][0:IC], psA[u][0:IC, P:2 * P], ACT.Copy).then_inc(aT_hi_done, 1)
                    if kind_of(t - 2, i, kind) == "routed":
                        u = c % 2
                        y = (c - 2) % ROUND
                        act.wait_ge(y_ready, t - 1)
                        if kind or t - 2 >= ROUND:
                            act.wait_ge(y_stored[y], 16 * (i if c >= 2 else i - 1))
                        nc.scalar.activation(y_sb[y], psY[u], ACT.Copy, scale=1 / WS).then_inc(y_done, 1)
                        nc.scalar.activation(scur[:, y:y + 1], stab[:, bass.ds(t - 2, 1)], ACT.Copy).then_inc(scur_done, 1)
                    if kind_of(t - 1, i, kind) == "shared":
                        j, r = t - 1 - ROUTED, (c - 1) % ROUND
                        act.wait_ge(terms_loaded[r], 16 * ((i if c >= 1 else i - 1) - R_ROUNDS + 1))
                        for k in range(1, K):
                            last = nc.scalar.activation(terms[r][:, k], terms[r][:, k], ACT.Copy, scale=share[:, bass.ds(j, 1), k])
                        last.then_inc(terms_scaled, 1)

            def xn_out(b):
                for c in range(HC):
                    act.wait_ge(xn_transposed, HC * b + c + 1)
                    nc.scalar.activation(xnT[:, c, :], psT[(10 + c) % 3][:, :], ACT.Copy).then_inc(xnT_ready, 1)

            def prep_out(b, n):
                act.wait_ge(prep_transposed, 9 * b + n + 1)
                dst, _, width = w_halves(PREP * b + n // 3, n % 3)
                nc.scalar.activation(dst, psT[n % 3][:, 0:width], ACT.Copy, scale=WS).then_inc(prep_hi, 1)

            def k_parts(b, c):
                act.wait_ge(k_ready, HC * b + c + 1)
                nc.scalar.activation(kv[c], psK[:, :], ACT.Exp)
                nc.scalar.activation(kphi[c], psK[:, :], ACT.Relu).then_inc(k_acted, 1)

            def q_parts(b, c):
                act.wait_ge(q_ready, HC * b + c + 1)
                nc.scalar.activation(qks[c], psQ[:, :], ACT.Exp)
                nc.scalar.activation(qphi[c], psQ[:, :], ACT.Relu).then_inc(q_acted, 1)

            def step(st):
                b = st.b
                if st.now:
                    k_parts(b, 0)
                    q_parts(b, 0)
                prep_out(b, 0)
                if st.now:
                    k_parts(b, 1)
                prep_out(b, 1)
                prep_out(b, 2)
                if st.now:
                    q_parts(b, 1)
                prep_out(b, 3)
                if st.before:
                    act.wait_ge(xn2_ready, TS * b)
                    if not st.now:
                        act.wait_ge(xn2_stored, 16 * (b - 1))
                    nc.scalar.activation(xn2_split[:, :, 0], xn2, ACT.Copy).then_inc(hi_done, 1)
                prep_out(b, 4)
                prep_out(b, 5)
                if st.before:
                    for j in range(TS):
                        act.wait_ge(xn2_transposed, TS * (b - 1) + j + 1)
                        nc.scalar.activation(xT2[j % 2].rearrange("p s c t -> p (s c t)"),
                                             psT[(6 + j) % 3][:, 0:H].bitcast(f16), ACT.Copy).then_inc(xT2_ready, 1)
                if st.after:
                    xn_out(b + 1)
                if st.now:
                    act.wait_ge(den_inverted, b + 1)
                    nc.scalar.activation(attn_words.rearrange("p (n d) -> p n d", d=D), rden[:, :].unsqueeze(2).to_broadcast([P, TS * HEADS, D]), ACT.Copy).then_inc(rden_spread, 1)
                for n in range(6, 9):
                    prep_out(b, n)

            xn_out(0)
            steps(act, step)
            act.wait_ge(share_shifted, 1)
            nc.scalar.activation(share[:, :, :], share[:, :, :], ACT.Exp).then_inc(share_exp, 1)
            for b in LATE_STEPS:
                for n in range(9):
                    m = 9 * b + n
                    hi, _, width = w_halves(PREP * b + n // 3, n % 3)
                    act.wait_ge(prep_transposed, m + 1)
                    if m >= 9 * LATE_STEPS[0] + 2:
                        act.wait_ge(prep_lo, m - 1)
                    nc.scalar.activation(wide[m % 2][:, 0:width], psT[n % 3][:, 0:width], ACT.Copy, scale=WS)
                    nc.scalar.activation(hi, psT[n % 3][:, 0:width], ACT.Copy, scale=WS).then_inc(prep_hi, 1)
            rounds(act, act_round)

        @block.vector
        def _(dve):
            dve.wait_ge(setup_act, 4)
            nc.vector.tensor_scalar(decay[:, :], decay[:, :], 1.0, None, ALU.add).then_inc(setup_dve, 1)
            nc.vector.tensor_tensor(rwT[:, :, 1, :], psD[:, 0, 0:HC * E].rearrange("p (c e) -> p c e", c=HC),
                                    rwT[:, :, 0, :], ALU.subtract).then_inc(setup_dve, 1)
            dve.wait_ge(setup_dve, 2)
            nc.vector.reciprocal(decay[:, :], decay[:, :]).then_inc(setup_dve, 1)
            dve.wait_ge(setup_dve, 3)

            def norm_stats(n, src, b):
                for j in range(TS):
                    nc.vector.bn_stats(stats[n][:, j], src[:, j]).then_inc(ln_stats[n], 1)
                wait_apart(dve, ln_stats[n], TS * b + TS)
                for j in range(TS):
                    nc.vector.bn_aggr(mv[n][:, j], stats[n][:, j]).then_inc(ln_aggr[n], 1)

            def norm(n, dst, src, b, done):
                dve.wait_ge(ln_rstd[n], b + 1)
                for j in range(TS):
                    nc.vector.tensor_scalar(dst[:, j], src[:, j], mv[n][:, j, 0:1], rstd[n][:, j:j + 1],
                                            ALU.subtract, ALU.mult).then_inc(done, 1)

            def unit(b, c):
                n = HC * b + c
                dve.wait_ge(k_acted, n + 1)
                nc.vector.scalar_tensor_tensor(kphi[c], kv[c], 1.0, kphi[c], ALU.min, ALU.add).then_inc(kphi_done, 1)
                dve.wait_ge(q_acted, n + 1)
                nc.vector.scalar_tensor_tensor(qphi[c], qks[c], 1.0, qphi[c], ALU.min, ALU.add).then_inc(qphi_done, 1)
                dve.wait_ge(kphi_done, n + 1)
                dve.wait_ge(v_ready, n + 1)
                if not (isinstance(b, int) and b == 0):
                    dve.wait_ge(attn_done, HC * b)
                nc.vector.tensor_tensor(kv[c], psV[:, :], kphi[c], ALU.mult).then_inc(kv_done, 1)
                dec = decay[:, c:c + 1].to_broadcast([P, S])
                nc.vector.tensor_tensor_scan(ksum[c], dec, kphi[c], 0.0, ALU.mult, ALU.add).then_inc(ksum_done, 1)
                dve.wait_ge(kv_done, n + 1)
                nc.vector.tensor_tensor_scan(kvsum[c], dec, kv[c], 0.0, ALU.mult, ALU.add).then_inc(kvsum_done, 1)

            def prep_out(b, n):
                dve.wait_ge(prep_hi, 9 * b + n + 1)
                hi, dst, width = w_halves(PREP * b + n // 3, n % 3)
                nc.vector.scalar_tensor_tensor(dst, psT[n % 3][:, 0:width], WS, hi, ALU.mult, ALU.subtract).then_inc(prep_lo, 1)

            def step(st):
                b = st.b
                if st.now:
                    unit(b, 0)
                if st.before:
                    if not (isinstance(b, int) and b == 1):
                        dve.wait_ge(x1_stored, 16 * (b - 1))
                    for h in range(2):
                        dve.wait_ge(proj_ready, 2 * (b - 1) + h + 1)
                        nc.vector.tensor_tensor(x1_sb[:, 2 * h:2 * h + 2], psD[:, h, :].rearrange("p (j h) -> p j h", h=H),
                                                x_sb[1 - st.parity][:, 2 * h:2 * h + 2], ALU.add).then_inc(x1_done, 1)
                    dve.wait_ge(x1_done, 2 * b)
                    norm_stats(1, x1_sb, b - 1)
                for n in range(3):
                    prep_out(b, n)
                if st.before:
                    if st.now:
                        dve.wait_ge(xn_transposed, HC * b + HC)
                    norm(1, xn2, x1_sb, b - 1, xn2_ready)
                if st.after:
                    dve.wait_ge(x_loaded[1 - st.parity], 16 * ((st.half if st.parity == 0 else st.half + 1) + 1))
                    norm_stats(0, x_sb[1 - st.parity], b + 1)
                for n in range(3, 6):
                    prep_out(b, n)
                if st.now:
                    unit(b, 1)
                if st.after:
                    if st.before:
                        dve.wait_ge(split_done, b)
                    dve.wait_ge(xn_transposed, HC * b + HC)
                    norm(0, xn, x_sb[1 - st.parity], b + 1, xn_ready)
                if st.before:
                    dve.wait_ge(logits_ready, TS * b)
                    nc.vector.tensor_tensor(logits[:, :, :], psD[:, 0, 0:TS * E].rearrange("p (j e) -> p j e", e=E),
                                            rb[:, :].unsqueeze(1).to_broadcast([P, TS, E]), ALU.add).then_inc(logits_done, 1)
                if st.now:
                    dve.wait_ge(den_ready, b + 1)
                    nc.vector.tensor_scalar(rden[:, :], psD[:, 0, 0:TS * HEADS], DEN_EPS, None, ALU.max).then_inc(den_clipped, 1)
                    dve.wait_ge(den_clipped, b + 1)
                    nc.vector.reciprocal(rden[:, :], rden[:, :]).then_inc(den_inverted, 1)
                if st.before:
                    wait_apart(dve, logits_done, b)
                    for j in range(TS):
                        nc.vector.max(top8[:, j], logits[:, j]).then_inc(top_done, 1)
                    wait_apart(dve, top_done, TS * b)
                    for j in range(TS):
                        nc.vector.max_index(idx8[:, j], top8[:, j], logits[:, j]).then_inc(topi_done, 1)
                    dve.wait_ge(topi_done, (TS + 2) * (b - 1) + TS)
                    nc.vector.tensor_copy(topv[:, bass.ds(TS * (b - 1), TS), :], top8[:, :, 0:K]).then_inc(topi_done, 1)
                    nc.vector.tensor_copy(topi[:, bass.ds(TS * (b - 1), TS), :], idx8[:, :, 0:K]).then_inc(topi_done, 1)
                for n in range(6, 9):
                    prep_out(b, n)
                if st.now:
                    for c in range(HC):
                        if c == 0:
                            dve.wait_ge(rden_turned, b + 1)
                            dve.wait_ge(qkv_done, HC * b + HC)
                        nc.vector.tensor_tensor(attnT[:, c, :], kvsum[c], psD[:, c, :], ALU.mult).then_inc(attn_done, 1)

            links = [0]

            def link(instruction):
                links[0] += 1
                instruction.then_inc(chain, 1)
                dve.wait_ge(chain, links[0])

            def dispatch():
                v = nc.vector
                dve.wait_ge(route_made, 9)
                dve.wait_ge(x1_stored, 16 * NB)
                dve.wait_ge(xn2_stored, 16 * NB)
                dve.wait_ge(topi_done, (TS + 2) * NB)
                link(v.tensor_copy(share_sum[:, :], topv[:, :, 0]))
                v.tensor_tensor(share[:, :, :], topv[:, :, :], share_sum[:, :].unsqueeze(2).to_broadcast([P, NT, K]), ALU.subtract).then_inc(share_shifted, 1)
                for k in range(K):
                    v.tensor_tensor(chosen[k].rearrange("p (e j) -> p e j", e=E), topi[:, :, k].unsqueeze(1).to_broadcast([P, E, NT]),
                                    iota_e[:, :].unsqueeze(2).to_broadcast([P, E, NT]), ALU.is_equal).then_inc(chosen_done, 1)
                dve.wait_ge(ranks_ready, 1)
                link(v.tensor_tensor_scan(dest, one[:, :].to_broadcast([P, E * NT]), psD[:, :, :].rearrange("p a b -> p (a b)"), 0.0, ALU.mult, ALU.add))
                dest_v = dest.rearrange("p (e j) -> p e j", e=E)
                v.memset(seen[:, 0:1], 0.0)
                link(v.tensor_copy(seen[:, 1:E], dest_v[:, 0:E - 1, NT - 1]))
                link(v.tensor_tensor(counts[:, :], dest_v[:, :, NT - 1], seen[:, :], ALU.subtract))
                link(v.tensor_scalar(counts_i[:, :], counts[:, :], float(P - 1), None, ALU.add))
                link(v.tensor_scalar(counts_i[:, :], counts_i[:, :], P.bit_length() - 1, None, ALU.arith_shift_right))
                link(v.tensor_copy(counts[:, :], counts_i[:, :]))
                link(v.tensor_tensor_scan(tile_end[:, :], one[:, :].to_broadcast([P, E]), counts[:, :], 0.0, ALU.mult, ALU.add))
                link(v.tensor_tensor(shift[:, :], tile_end[:, :], counts[:, :], ALU.subtract))
                link(v.scalar_tensor_tensor(shift[:, :], shift[:, :], float(P), seen[:, :], ALU.mult, ALU.subtract))
                half = E * NT // 2
                for n, bank in enumerate((psK, psQ)):
                    last = v.tensor_tensor(dest[:, n * half:(n + 1) * half], bank[:, :], dest[:, n * half:(n + 1) * half], ALU.add)
                link(last)
                link(v.tensor_tensor(dest_v, dest_v, shift[:, :].unsqueeze(2).to_broadcast([P, E, NT]), ALU.add))
                for k in range(K):
                    link(v.tensor_tensor(picked, chosen[k], dest, ALU.mult))
                    link(v.tensor_reduce(slot[:, k, :], picked.rearrange("p (e j) -> p j e", e=E), AX.X, ALU.add))
                flat = slot[:, :, :].rearrange("p k j -> p (k j)")
                hi, lo = slot_hi[:, :, :].rearrange("p k j -> p (k j)"), slot_lo[:, :, :].rearrange("p k j -> p (k j)")
                link(v.tensor_copy(slot_i, flat))
                link(v.tensor_scalar(slot_i, slot_i, P.bit_length() - 1, None, ALU.arith_shift_right))
                link(v.tensor_copy(hi, slot_i))
                link(v.scalar_tensor_tensor(lo, hi, -float(P), flat, ALU.mult, ALU.add))
                for n in range(2):
                    v.tensor_scalar((counts, shift)[n][:, :], tile_end[:, :], row[:, n:n + 1], None, ALU.is_le, ALU.add, accum_out=owner[:, n:n + 1]).then_inc(owner_done, 1)
                dve.wait_ge(owner_turned, 1)
                v.memset(owner_i[:, 0:2], 0)
                v.tensor_scalar(owner_i[:, 2:], psD[0:1, 0, 0:ROUTED], float(E - 1), float(EW), ALU.min, ALU.mult).then_inc(owner_ready, 1)

                def hot(j, parity, first):
                    col = bass.ds(j, 1)
                    if not first:
                        dve.wait_ge(placed, K * j - K)
                    v.tensor_tensor(lo_hot[parity], iota_s[:, 0:P].unsqueeze(1).to_broadcast([P, K, P]),
                                    slot_lo[:, :, col].to_broadcast([P, K, P]), ALU.is_equal)
                    for k in range(K):
                        n = K * j + k
                        if not (first and j == 0):
                            dve.wait_ge(placed, n - K + 1)
                        v.tensor_scalar(hi_hot[k], iota_s[:, :], slot_hi[:, k, col], number[:, bass.ds(n, 1)], ALU.is_equal, ALU.mult).then_inc(hot_done, 1)

                hot(0, 0, True)
                hot(1, 1, True)
                with dve.Fori(1, NT // 2) as i:
                    hot(2 * i, 0, False)
                    hot(2 * i + 1, 1, False)
                dve.wait_ge(placed, K * NT)
                table = psV[:, 0:ROUTED]
                link(v.tensor_scalar(place, table, -float(P), 0.0, ALU.add, ALU.max))
                link(v.tensor_copy(place_i, place))
                v.tensor_scalar(gtab[:, :], place_i, (P * K).bit_length() - 1, P.bit_length() - 1, ALU.arith_shift_right, ALU.logical_shift_left)
                link(v.tensor_scalar(stab[:, :], place_i, P.bit_length() - 1, K - 1, ALU.arith_shift_right, ALU.bitwise_and))
                link(v.tensor_scalar(place_i, place_i, P - 1, None, ALU.bitwise_and))
                link(v.tensor_tensor(gtab[:, :], gtab[:, :], place_i, ALU.add))
                link(v.tensor_scalar(place, iota_s[:, :], float(P), row[:, 2:3], ALU.mult, ALU.add))
                v.scalar_tensor_tensor(place, table, 0.0, place, ALU.is_equal, ALU.mult)
                link(v.tensor_copy(place_i, gtab[:, :]))
                link(v.tensor_scalar(place_i, place_i, K.bit_length() - 1, None, ALU.logical_shift_left))
                link(v.tensor_tensor(stab[:, :], stab[:, :], place_i, ALU.add))
                link(v.tensor_tensor(stab[:, :], stab[:, :], gtab[:, :], ALU.add))
                link(v.tensor_copy(place_i, place))
                v.tensor_tensor(stab[:, :], stab[:, :], place_i, ALU.add).then_inc(tables_done, 1)
                v.tensor_copy(gcur[:, :], gtab[:, 0:ROUND]).then_inc(gcur_done, 1)
                dve.wait_ge(share_exp, 1)
                link(v.tensor_reduce(share_sum[:, :], share[:, :, :], AX.X, ALU.add))
                link(v.reciprocal(share_sum[:, :], share_sum[:, :]))
                v.scalar_tensor_tensor(share[:, :, :], share[:, :, :], SCALE, share_sum[:, :].unsqueeze(2).to_broadcast([P, NT, K]), ALU.mult, ALU.mult).then_inc(share_done, 1)
                dve.wait_ge(share_done, 1)

            def turn_out(tile, c, kind):
                dve.wait_ge(x_turned, tile + 1)
                nc.vector.tensor_copy(xT[c % 2].rearrange("p s c t -> p (s c t)"), psX[c % 2]).then_inc(xT_done, 1)
                if kind_of(tile + ROUND, None, kind) == "routed":
                    nc.vector.tensor_copy(gcur[:, c % ROUND:c % ROUND + 1], gtab[:, bass.ds(tile + ROUND, 1)]).then_inc(gcur_done, 1)

            def dve_round(i, kind):
                if isinstance(i, int) and i == 0:
                    turn_out(0, 0, None)
                for c in range(ROUND):
                    t = ROUND * i + c
                    if kind_of(t + 1, i, kind):
                        turn_out(t + 1, c + 1, kind)
                    if kind_of(t - 2, i, kind) == "shared":
                        j, r = t - 2 - ROUTED, (c - 2) % ROUND
                        dve.wait_ge(terms_added, j + 1)
                        nc.vector.scalar_tensor_tensor(terms[r][:, 0], terms[r][:, 0], share[:, bass.ds(j, 1), 0], terms[r][:, 1], ALU.mult, ALU.add).then_inc(o_started, 1)
                    if kind_of(t, i, kind):
                        dve.wait_ge(silu_done, t + 1)
                        nc.vector.scalar_tensor_tensor(act32[c % 2], psG[c % 2][:, I:GU], 1 / WS, gate[c % 2], ALU.mult, ALU.mult).then_inc(a_done, 1)
                    if kind_of(t - 1, i, kind):
                        u = (c - 1) % 2
                        dve.wait_ge(aT_hi_done, 2 * t)
                        nc.vector.tensor_tensor(aT_lo[u], psA[u][:, 0:P], aT_hi[u], ALU.subtract)
                        nc.vector.tensor_tensor(aT_tail[u][IC:P], psA[u][0:IC, P:2 * P], aT_tail[u][0:IC], ALU.subtract).then_inc(aT_lo_done, 1)
                    if kind_of(t - 2, i, kind) == "shared":
                        j, r = t - 2 - ROUTED, (c - 2) % ROUND
                        if kind or j >= ROUND:
                            dve.wait_ge(out_stored[r], 16 * ((i if c >= 2 else i - 1) - R_ROUNDS))
                        dve.wait_ge(o_started, j + 1)
                        dve.wait_ge(y_ready, t - 1)
                        nc.vector.scalar_tensor_tensor(o_sb[r], psY[c % 2], 1 / WS, terms[r][:, 0], ALU.mult, ALU.add).then_inc(o_done, 1)

            dve.wait_ge(x_loaded[0], 16)
            norm_stats(0, x_sb[0], 0)
            norm(0, xn, x_sb[0], 0, xn_ready)
            steps(dve, step)
            dispatch()
            rounds(dve, dve_round)

        @block.tensor
        def _(pe):
            pe.wait_ge(consts_made, 7)
            pe.wait_ge(consts_loaded, 48)
            for c in range(HC):
                nc.tensor.matmul(psK[:, c:c + 1], headsel[:, c * P:(c + 1) * P], decay_in[:, :], start=True, stop=True)
            nc.tensor.matmul(psQ[:, 0:P], headsel[:, 0:P], headsel[:, 0:P], start=True, stop=True)
            nc.tensor.matmul(psV[:, 0:E], ones_row, rb_row[:, :], start=True, stop=True)
            for c in range(HC):
                last = nc.tensor.transpose(psD[:, 0, c * E:(c + 1) * E], rw_nat[:, c * P:(c + 1) * P], ident32[0:E, 0:E])
            last.then_inc(setup_mm, 1)

            def xn_in(b):
                pe.wait_ge(xn_ready, TS * b + TS)
                for c in range(HC):
                    for j in range(TS):
                        last = nc.tensor.transpose(psT[(10 + c) % 3][:, j * P:(j + 1) * P], xn[:, j, c * P:(c + 1) * P], ident32[:, :])
                    last.then_inc(xn_transposed, 1)

            def prep_in(st, slot, n=None):
                if n is None:
                    n = SLOTS[slot][1]
                if n == 0:
                    pe.wait_ge(wstage_loaded, staged(st.b))
                if n == 2:
                    pe.wait_ge(tail_doubled, st.b + 1)
                if slot is not None:
                    wait_bank(pe, slot, st)
                else:
                    pe.wait_ge(prep_lo if st.b == LATE_STEPS[0] and n < 3 else prep_hi, 9 * st.b + n - 2)
                bank, q, part = psT[n % 3], n // 3, n % 3
                if part < HC:
                    for m in range(3):
                        last = nc.tensor.transpose(bank[:, m * P:(m + 1) * P], gu_nat[:, q, m, part * P:(part + 1) * P], ident32[:, :])
                else:
                    for c in range(HC):
                        nc.tensor.transpose(bank[:, c * P:(c + 1) * P], dn_nat[:, q, c, 0:P], ident32[:, :])
                        last = nc.tensor.transpose(bank[:, H + c * P:H + (c + 1) * P],
                                                   dn_nat[:, q, c, P:I + IC], ident32[:, :])
                last.then_inc(prep_transposed, 1)

            def late_and_dispatch():
                pe.wait_ge(route_made, 9)
                pe.wait_ge(topi_done, (TS + 2) * NB)
                half = E * NT // 2
                for k in range(K):
                    pe.wait_ge(chosen_done, k + 1)
                    for n, bank in enumerate((psK, psQ)):
                        nc.tensor.matmul(bank[:, :], before[:, :], chosen[k][:, n * half:(n + 1) * half], start=(k == 0), stop=(k == K - 1))
                        last = nc.tensor.matmul(psD[:, n, :], ones16[:, :], chosen[k][:, n * half:(n + 1) * half], start=(k == 0), stop=(k == K - 1))
                last.then_inc(ranks_ready, 1)
                pe.wait_ge(xT2_ready, NT)
                for n in range(9):
                    prep_in(Step(LATE_STEPS[0], 0, 0), None, n)
                pe.wait_ge(owner_done, 2)
                for w in range(2):
                    last = nc.tensor.transpose(psD[0:1, 0, w * P:(w + 1) * P], owner[:, w:w + 1], ident32[:, :])
                last.then_inc(owner_turned, 1)

                def hot(j, parity, first=False, last=False):
                    for k in range(K):
                        pe.wait_ge(hot_done, K * j + k + 1)
                        nc.tensor.matmul(psV[:, 0:ROUTED], lo_hot[parity][:, k], hi_hot[k], start=(first and k == 0), stop=(last and k == K - 1)).then_inc(placed, 1)

                hot(0, 0, first=True)
                assert len(LATE_STEPS) == 2
                for n in range(9):
                    prep_in(Step(LATE_STEPS[1], 0, 0), None, n)
                    hot(n + 1, (n + 1) % 2)
                with pe.Fori(5, NT // 2 - 1) as i:
                    hot(2 * i, 0)
                    hot(2 * i + 1, 1)
                hot(NT - 2, 0)
                hot(NT - 1, 1, last=True)
                pe.wait_ge(owner_ready, 1)
                pe.wait_ge(tables_done, 1)
                pe.wait_ge(prep_lo, 9 * (LATE_STEPS[-1] + 1))

            def turn_in(tile, c, i, kind):
                if kind == "routed":
                    pe.wait_ge(xg_loaded[c % ROUND], 16 * (i + 1 + c // ROUND))
                else:
                    pe.wait_ge(xs_loaded[c % ROUND], 16 * (i + 1 + c // ROUND - R_ROUNDS))
                for n in range(2 * HC):
                    last = nc.tensor.transpose(psX[c % 2][:, n * P:(n + 1) * P], xg[c % ROUND][:, n * P:(n + 1) * P], ident16[:, :])
                last.then_inc(x_turned, 1)

            expert_at = [pe.alloc_register(f"expert_at{n}") for n in range(ROUND + 2)]

            def experts_of(i):
                pe.load(expert_at, owner_i[0:1, bass.ds(ROUND * i, ROUND + 2)])
                return [pe.snap(r, min_val=0, max_val=(E - 1) * EW) for r in expert_at]

            last_at = [0] * 2

            def pe_round(i, kind):
                if isinstance(i, int) and i == 0:
                    turn_in(0, 0, 0, "routed")
                routed = kind == "routed" if kind else i < R_ROUNDS
                at_of = experts_of(i) if routed else last_at[-2:] + [E * EW] * ROUND
                last_at[:] = at_of
                for c in range(ROUND):
                    t = ROUND * i + c
                    now, last_kind = kind_of(t, i, kind), kind_of(t - 2, i, kind)
                    if now:
                        at = at_of[c + 2]
                        pe.wait_ge(xT_done, t + 1)
                        n = 0
                        for sx, sw in ((0, 0), (0, 1), (1, 0)):
                            for h in range(HC):
                                last = nc.tensor.matmul(psG[c % 2][:, 0:GU], xT[c % 2][:, sx, h], W[:, bass.ds(at + (2 * h + sw) * GU, GU)],
                                                        start=(n == 0), stop=(n == 3 * HC - 1))
                                n += 1
                        last.then_inc(gu_ready, 1)
                    if kind_of(t + 1, i, kind):
                        turn_in(t + 1, c + 1, i, kind_of(t + 1, i, kind))
                    if kind_of(t - 1, i, kind):
                        u = (c - 1) % 2
                        pe.wait_ge(a_done, t)
                        nc.tensor.transpose(psA[u][:, 0:P], act32[u][:, 0:P], ident32[:, :])
                        nc.tensor.transpose(psA[u][0:IC, P:2 * P], act32[u][:, P:I], ident32[:, :]).then_inc(a_turned, 1)
                    if last_kind:
                        u = c % 2
                        at = at_of[c]
                        pe.wait_ge(aT_lo_done, t - 1)
                        parts = ((aT_hi[u], 0, P), (aT_tail[u], 1, P), (aT_lo[u], 0, P), (aT_hi[u], 2, P), (aT_tail[u], 3, IC))
                        for n, (part, q, rows) in enumerate(parts):
                            last = nc.tensor.matmul(psY[u], part[0:rows], W[0:rows, bass.ds(at + GUW + q * H, H)], start=(n == 0), stop=(n == len(parts) - 1))
                        last.then_inc(y_ready, 1)

            def project(dst, st, c, which, acted, ready):
                n = HC * st.b + c
                if not (isinstance(n, int) and n == 0):
                    pe.wait_ge(acted, n)
                for h in range(HC):
                    last = nc.tensor.matmul(dst[:, :], wqkv_sb[:, h, which * H + c * P:which * H + (c + 1) * P], xnT[:, h, :],
                                            start=(h == 0), stop=(h == HC - 1))
                last.then_inc(ready, 1)

            def step(st):
                b = st.b
                if st.now:
                    pe.wait_ge(xnT_ready, HC * b + HC)
                    project(psK, st, 0, 1, k_acted, k_ready)
                    project(psQ, st, 0, 0, q_acted, q_ready)
                    project(psV, st, 0, 2, kv_done, v_ready)
                if st.before:
                    pe.wait_ge(attn_done, HC * b)
                    for j in range(TS):
                        for c in range(HC):
                            last = nc.tensor.matmul(psD[:, j // 2, (j % 2) * H:(j % 2 + 1) * H], attnT[:, c, j * P:(j + 1) * P],
                                                    wout_sb[:, c, :], start=(c == 0), stop=(c == HC - 1))
                        if j % 2:
                            last.then_inc(proj_ready, 1)
                prep_in(st, 0)
                if st.now:
                    project(psK, st, 1, 1, k_acted, k_ready)
                prep_in(st, 1)
                prep_in(st, 2)
                if st.now:
                    project(psQ, st, 1, 0, q_acted, q_ready)
                prep_in(st, 3)
                if st.now:
                    project(psV, st, 1, 2, kv_done, v_ready)
                prep_in(st, 4)
                prep_in(st, 5)
                if st.before:
                    pe.wait_ge(split_done, b)
                    for j in range(TS):
                        wait_bank(pe, 6 + j, st)
                        bank = psT[(6 + j) % 3][:, 0:H].bitcast(f16)
                        for s in range(2):
                            for c in range(HC):
                                last = nc.tensor.transpose(bank[:, (s * HC + c) * P:(s * HC + c + 1) * P],
                                                           xn2_split[:, j, s, c * P:(c + 1) * P], ident16[:, :])
                        last.then_inc(xn2_transposed, 1)
                        if j >= 1:
                            route(b, j - 1)
                    route(b, TS - 1)
                if st.after:
                    for c in range(HC):
                        wait_bank(pe, 10 + c, st)
                    xn_in(b + 1)
                if st.now:
                    den(st)
                for n in range(6, 9):
                    prep_in(st, 6 + n)
                if st.now:
                    pe.wait_ge(rden_spread, b + 1)
                    for c in range(HC):
                        for j in range(TS):
                            last = nc.tensor.transpose(psD[:, c, j * P:(j + 1) * P], rden_rows[:, j, c * P:(c + 1) * P], ident32[:, :])
                    last.then_inc(rden_turned, 1)

            def route(b, j):
                pe.wait_ge(xT2_ready, TS * (b - 1) + j + 1)
                if j == 0:
                    pe.wait_ge(x1_done, 2 * b)
                n = 0
                for sx, sw in ((0, 0), (0, 1), (1, 0)):
                    for c in range(HC):
                        last = nc.tensor.matmul(psD[:, 0, j * E:(j + 1) * E], xT2[j % 2][:, sx, c, :], rwT[:, c, sw, :],
                                                start=(n == 0), stop=(n == 3 * HC - 1))
                        n += 1
                last.then_inc(logits_ready, 1)

            def den(st):
                b = st.b
                pe.wait_ge(qks_done, HC * b + HC)
                if st.before:
                    pe.wait_ge(logits_done, b)
                for c in range(HC):
                    for j in range(TS):
                        n = j * HEADS + c * P // D
                        last = nc.tensor.matmul(psD[:, 0, n:n + P // D], qks[c][:, j * P:(j + 1) * P], head_sums, start=True, stop=True)
                last.then_inc(den_ready, 1)

            pe.wait_ge(setup_dve, 3)
            pe.wait_ge(wattn_loaded, 32)
            xn_in(0)
            steps(pe, step)
            late_and_dispatch()
            rounds(pe, pe_round)


_INS = ['L0_attn_x', 'L0_attn_w_qkv', 'L0_attn_w_out', 'L0_attn_decay_param', 'L0_ffn_router_w', 'L0_ffn_router_b',
        'L0_ffn_gate_w', 'L0_ffn_up_w', 'L0_ffn_down_w', 'L0_ffn_shared_gate_w', 'L0_ffn_shared_up_w', 'L0_ffn_shared_down_w']
_OUTS = [((8, 512, 256), 'float32')]


def kernel(**inputs):
    import numpy as _np
    import concourse.bacc as _bacc
    from concourse import mybir as _mybir
    from concourse.bass_utils import run_bass_kernel_spmd as _run

    nc = _bacc.Bacc("TRN2", target_bir_lowering=False, num_devices=1)
    arrays, args = {}, []
    for name in _INS:
        a = _np.ascontiguousarray(inputs[name])
        arrays[f"in_{name}_dram"] = a
        args.append(nc.dram_tensor(f"in_{name}_dram", a.shape, _mybir.dt.from_np(a.dtype), kind="ExternalInput").ap())
    for i, (shape, dtype) in enumerate(_OUTS):
        dt = _mybir.dt.from_np(_np.dtype(dtype))
        args.append(nc.dram_tensor(f"out_{i}_dram", shape, dt, kind="ExternalOutput").ap())
    moe_block(nc, *args)
    r = _run(nc, [arrays], core_ids=[0])
    got = tuple(r.results[0][f"out_{i}_dram"] for i in range(len(_OUTS)))
    return got[0]
```

```python
import concourse.bass as bass
from concourse import mybir
from contextlib import ExitStack


def moe_block(nc, x, w_qkv, w_out, decay_param, router_w, router_b, gate_w, up_w, down_w,
              shared_gate_w, shared_up_w, shared_down_w, out):
    f32, f16, i32, u32 = mybir.dt.float32, mybir.dt.float16, mybir.dt.int32, mybir.dt.uint32
    ALU = mybir.AluOpType
    ACT = mybir.ActivationFunctionType
    AX = mybir.AxisListType

    P = 128
    NB, S, H = x.shape
    T = NB * S
    NT = T // P
    TS = S // P
    HC = H // P
    HEADS = decay_param.shape[0]
    D = H // HEADS
    E, I, _ = gate_w.shape
    K = 4
    LN_EPS = 1e-5
    DEN_EPS = 1e-6
    IC = I - P
    GU = 2 * I
    GUW = HC * 2 * GU
    DNW = 4 * H
    EW = GUW + DNW
    NE = E + 1
    PREP = 3
    EARLY = PREP * NB

    ROUTED = T * K // P + E
    TILES = ROUTED + NT
    ROUND = 4
    SCALE = 1.8

    xv = x.rearrange("b (j p) h -> b p j h", p=P)

    ctx = ExitStack()
    with ctx:
        def sb(name, shape, dt):
            return ctx.enter_context(nc.sbuf_tensor(name, shape, dt))

        def ps(name, shape, dt=f32):
            return ctx.enter_context(nc.psum_tensor(name, shape, dt))

        def sem(name):
            return ctx.enter_context(nc.semaphore(name))

        xn2_dram = nc.dram_tensor("xn2_scratch", [T, 2 * H], f16, kind="Internal").ap()
        TERMS = K + 1
        y_dram = nc.dram_tensor("y_scratch", [T * TERMS + ROUTED * P, H], f32, kind="Internal").ap()
        y_v = y_dram[0:T * TERMS].rearrange("(j p k) h -> j p k h", p=P, k=TERMS)
        xn2_tiles = xn2_dram.rearrange("(j p) h -> j p h", p=P)
        out_tiles = out.rearrange("b t h -> (b t) h").rearrange("(j p) h -> j p h", p=P)
        x1_v = y_dram[0:T * TERMS].rearrange("(b j p k) h -> b k p j h", j=TS, p=P, k=TERMS)[:, K]
        xn2_v = xn2_dram.rearrange("(b j p) h -> b p j h", j=TS, p=P)

        W = sb("W", [P, NE * EW], f16)
        LATE = (NE - EARLY) * EW // 2
        late = W[:, EARLY * EW:NE * EW].bitcast(f32)
        ARENA = 8960
        arena = sb("arena", [P, ARENA], f32)[:, :]

        def carver(region, size):
            at = [0]

            def carve(words):
                a = at[0]
                at[0] += words
                assert at[0] <= size, (at[0], size)
                return region[:, a:at[0]]
            return carve

        carve = carver(late, LATE)
        xnT = carve(HC * S).rearrange("p (c t) -> p c t", c=HC)
        wqkv_sb = carve(HC * 3 * H).rearrange("p (c n) -> p c n", c=HC)
        wout_sb = carve(HC * H).rearrange("p (c n) -> p c n", c=HC)
        kv = [carve(S) for _ in range(HC)]
        kphi = [carve(S) for _ in range(HC)]
        qks = [carve(S) for _ in range(HC)]
        qphi = [carve(S) for _ in range(HC)]
        ksum = [carve(S) for _ in range(HC)]
        kvsum = [carve(S) for _ in range(HC)]
        attn_words = carve(HC * S)
        attnT = attn_words.rearrange("p (c t) -> p c t", c=HC)
        rden_rows = attn_words.rearrange("p (j h) -> p j h", j=TS)
        xn = carve(TS * H).rearrange("p (j h) -> p j h", j=TS)

        blockones = carve(P)
        rden = carve(TS * HEADS)

        carve = carver(arena, ARENA)
        gu_nat = carve(PREP * 3 * H).rearrange("p (e m h) -> p e m h", e=PREP, m=3)
        dn_nat = carve(PREP * HC * (I + IC)).rearrange("p (e c i) -> p e c i", e=PREP, c=HC)
        x_sb = [carve(TS * H).rearrange("p (j h) -> p j h", j=TS) for _ in range(2)]
        x1_sb = carve(TS * H).rearrange("p (j h) -> p j h", j=TS)
        xn2 = x1_sb
        xn2_split = carve(TS * H).bitcast(f16).rearrange("p (j s h) -> p j s h", j=TS, s=2)
        xT2 = [carve(H).bitcast(f16).rearrange("p (s c t) -> p s c t", s=2, c=HC) for _ in range(2)]

        STAGED = PREP * (3 * H + HC * (I + IC))
        carve = carver(arena[:, STAGED:], ARENA - STAGED)
        chosen = [carve(E * NT // 2).bitcast(f16) for _ in range(K)]
        dest = carve(E * NT)
        picked = carve(E * NT)
        wide = [carve(2 * H) for _ in range(2)]
        carve = carver(arena[:, STAGED:], K * E * NT // 2)
        lo_hot = [carve(K * P).rearrange("p (k s) -> p k s", k=K) for _ in range(2)]
        DVE_HOT = K - 1
        hi_hot = [carve(ROUTED) for _ in range(DVE_HOT)]
        last_hi_hot = [carve(ROUTED) for _ in range(2)]

        carve = carver(arena, ARENA)
        xg = [carve(H).bitcast(f16) for _ in range(ROUND)]
        xT = [carve(H).bitcast(f16).rearrange("p (s c t) -> p s c t", s=2, c=HC) for _ in range(2)]
        gate = [carve(I) for _ in range(2)]
        act32 = [carve(I) for _ in range(2)]
        aT_hi = [carve(P // 2).bitcast(f16) for _ in range(2)]
        aT_lo = [carve(P // 2).bitcast(f16) for _ in range(2)]
        aT_tail = [carve(P // 2).bitcast(f16) for _ in range(2)]
        y_sb = [carve(H) for _ in range(ROUND)]
        terms = [carve(TERMS * H).rearrange("p (k h) -> p k h", k=TERMS) for _ in range(ROUND)]
        o_sb = y_sb

        ident32 = sb("ident32", [P, P], f32)
        ident16 = sb("ident16", [P, P], f16)
        decay_in = sb("decay_in", [HEADS, 1], f32)
        decay = sb("decay", [P, HC], f32)
        rb_row = sb("rb_row", [1, E], f32)
        rb = sb("rb", [P, E], f32)
        rwT = sb("rwT", [P, HC, 2, E], f16)
        logits = sb("logits", [P, TS, E], f32)
        top8 = sb("top8", [P, TS, 8], f32)
        idx8 = sb("idx8", [P, TS, 8], u32)
        zero = sb("zero", [P, 1], f32)
        carrier = sb("carrier", [P, 1], f32)
        eps = sb("eps", [P, TS], f32)
        topv = sb("topv", [P, NT, K], f32)
        topi = sb("topi", [P, NT, K], f32)
        iota_e = sb("iota_e", [P, E], f32)
        iota_s = sb("iota_s", [P, ROUTED], f16)
        row = sb("row", [P, 3], f32)
        before = sb("before", [P, P], f16)
        ones16 = sb("ones16", [P, P], f16)
        one = sb("one", [P, 1], f32)
        seen = sb("seen", [P, E], f32)
        counts = sb("counts", [P, E], f32)
        counts_i = sb("counts_i", [P, E], i32)
        tile_end = sb("tile_end", [P, E], f32)
        shift = sb("shift", [P, E], f32)
        owner = sb("owner", [P, 2], f32)
        owner_i = sb("owner_i", [1, ROUTED + 2], i32)
        number = sb("number", [P, K * NT], f32)
        gtab = sb("gtab", [P, ROUTED], i32)
        stab = sb("stab", [P, ROUTED], i32)
        iota_i = stab
        slot_i = gtab[:, 0:K * NT]
        place, place_i = dest[:, 0:ROUTED], dest[:, ROUTED:2 * ROUTED].bitcast(i32)
        slot_hi = dest[:, 2 * ROUTED:2 * ROUTED + K * NT].rearrange("p (k j) -> p k j", k=K)
        slot_lo = dest[:, 2 * ROUTED + K * NT:2 * ROUTED + 2 * K * NT].rearrange("p (k j) -> p k j", k=K)
        rest = dest[:, 2 * ROUTED + 2 * K * NT:2 * ROUTED + 4 * K * NT]
        minus_hi = rest[:, 0:K * NT].rearrange("p (k j) -> p k j", k=K)
        minus_number = rest[:, K * NT:2 * K * NT]
        slot = topi[:, :, :].rearrange("p j k -> p (j k)").rearrange("p (k j) -> p k j", k=K)
        share = topv
        gcur = sb("gcur", [P, ROUND], i32)
        scur = sb("scur", [P, ROUND], i32)
        share_sum = sb("share_sum", [P, NT], f32)
        mhalf = sb("mhalf", [P, TS], f32)
        stats = [sb(f"stats{n}", [P, TS, 6], f32) for n in range(2)]
        mv = [sb(f"mv{n}", [P, TS, 2], f32) for n in range(2)]
        vare = [sb(f"vare{n}", [P, TS], f32) for n in range(2)]
        rstd = [sb(f"rstd{n}", [P, TS], f32) for n in range(2)]
        head_sums = blockones.rearrange("p (h d) -> p h d", d=D)[:, :, 0]
        headsel = x1_sb[0:HEADS, 1, :]
        ones_row = x1_sb[0:1, 2, 0:P]
        rw_nat = x1_sb[0:E, 0, :]

        psT = [ps(f"psT{n}", [P, 512]) for n in range(3)]
        psK = ps("psK", [P, S])
        psQ = ps("psQ", [P, S])
        psV = ps("psV", [P, S])
        psD = ps("psD", [P, 2, S])
        psX = [psT[0][:, 0:H].bitcast(f16), psT[1][:, 0:H].bitcast(f16)]
        psG = [psK, psQ]
        psA = [psV, psT[2]]
        psY = [psD[:, 0, 0:H], psD[:, 1, 0:H]]

        consts_loaded = sem("consts_loaded")
        wattn_loaded = sem("wattn_loaded")
        x_loaded = [sem(f"x_loaded{n}") for n in range(2)]
        residual_loaded = sem("residual_loaded")
        wstage_loaded = sem("wstage_loaded")
        x1_stored = sem("x1_stored")
        xn2_stored = sem("xn2_stored")
        setup_pool = sem("setup_pool")
        consts_made = sem("consts_made")
        setup_mm = sem("setup_mm")
        setup_act = sem("setup_act")
        setup_dve = sem("setup_dve")
        ln_stats = [sem(f"ln_stats{n}") for n in range(2)]
        ln_aggr = [sem(f"ln_aggr{n}") for n in range(2)]
        ln_vare = [sem(f"ln_vare{n}") for n in range(2)]
        ln_rstd = [sem(f"ln_rstd{n}") for n in range(2)]
        xn_ready = sem("xn_ready")
        xn_transposed = sem("xn_transposed")
        xnT_ready = sem("xnT_ready")
        k_ready, q_ready, v_ready = sem("k_ready"), sem("q_ready"), sem("v_ready")
        k_acted, q_acted = sem("k_acted"), sem("q_acted")
        kphi_done, kv_done, ksum_done = sem("kphi_done"), sem("kv_done"), sem("ksum_done")
        qphi_done, kvsum_done = sem("qphi_done"), sem("kvsum_done")
        qks_done, qkv_done = sem("qks_done"), sem("qkv_done")
        den_ready = sem("den_ready")
        den_clipped, den_inverted = sem("den_clipped"), sem("den_inverted")
        rden_spread, rden_turned = sem("rden_spread"), sem("rden_turned")
        attn_done = sem("attn_done")
        proj_ready = sem("proj_ready")
        x1_done = sem("x1_done")
        xn2_ready = sem("xn2_ready")
        hi_done = sem("hi_done")
        split_done = sem("split_done")
        xn2_transposed = sem("xn2_transposed")
        xT2_ready = sem("xT2_ready")
        logits_ready = sem("logits_ready")
        logits_done = sem("logits_done")
        top_done = sem("top_done")
        topi_done = sem("topi_done")
        prep_transposed = sem("prep_transposed")
        tail_doubled = sem("tail_doubled")
        prep_hi = sem("prep_hi")
        prep_lo = sem("prep_lo")

        route_made = sem("route_made")
        chosen_done = sem("chosen_done")
        ranks_ready = sem("ranks_ready")
        chain = sem("chain")
        hot_done, slots_ready, distances, act_hot_done = sem("hot_done"), sem("slots_ready"), sem("distances"), sem("act_hot_done")
        placed = sem("placed")
        owner_done, owner_turned, owner_ready = sem("owner_done"), sem("owner_turned"), sem("owner_ready")
        tables_done = sem("tables_done")
        share_shifted, share_exp, share_done = sem("share_shifted"), sem("share_exp"), sem("share_done")
        gcur_done, scur_done = sem("gcur_done"), sem("scur_done")
        xg_loaded = [sem(f"xg_loaded{c}") for c in range(ROUND)]
        xs_loaded = [sem(f"xs_loaded{c}") for c in range(ROUND)]
        y_stored = [sem(f"y_stored{c}") for c in range(ROUND)]
        terms_loaded = [sem(f"terms_loaded{c}") for c in range(ROUND)]
        terms_scaled, pairs_added, terms_added = sem("terms_scaled"), sem("pairs_added"), sem("terms_added")
        out_stored = [sem(f"out_stored{c}") for c in range(ROUND)]
        x_turned, xT_done = sem("x_turned"), sem("xT_done")
        gu_ready, silu_done, a_done = sem("gu_ready"), sem("silu_done"), sem("a_done")
        a_turned, aT_hi_done, aT_lo_done = sem("a_turned"), sem("aT_hi_done"), sem("aT_lo_done")
        y_ready, y_done, o_done, o_started = sem("y_ready"), sem("y_done"), sem("o_done"), sem("o_started")

        block = ctx.enter_context(nc.Block())

        R_ROUNDS, S_ROUNDS = ROUTED // ROUND, NT // ROUND
        ALL_ROUNDS = R_ROUNDS + S_ROUNDS

        def kind_of(tile, i, kind):
            if kind:
                return kind
            return None if tile < 0 or tile >= TILES else "routed" if tile < ROUTED else "shared"

        def rounds(eng, do):
            do(0, None)
            do(1, None)
            with eng.Fori(2, R_ROUNDS - 2) as i:
                do(i, "routed")
            do(R_ROUNDS - 2, None)
            do(R_ROUNDS - 1, None)
            do(R_ROUNDS, None)
            do(R_ROUNDS + 1, None)
            with eng.Fori(R_ROUNDS + 2, ALL_ROUNDS - 1) as i:
                do(i, "shared")
            do(ALL_ROUNDS - 1, None)
            do(ALL_ROUNDS, None)

        class Step:
            def __init__(self, b, parity, half, before=True, now=True, after=True):
                self.b, self.parity, self.half = b, parity, half
                self.before, self.now, self.after = before, now, after

        def steps(eng, do):
            do(Step(0, 0, 0, before=False))
            with eng.Fori(0, (NB - 2) // 2) as i:
                do(Step(2 * i + 1, 1, i))
                do(Step(2 * i + 2, 0, i + 1))
            do(Step(NB - 1, (NB - 1) % 2, (NB - 1) // 2, after=False))
            do(Step(NB, NB % 2, NB // 2, now=False, after=False))

        def wait_apart(eng, semaphore, value):
            eng.wait_ge(semaphore, value)
            nc.vector.memset(carrier[:, :], 0.0)

        SLOTS = [("prep", n) for n in range(3)] + [("xn", c) for c in range(HC)] + [("prep", n) for n in range(3, 6)] \
            + [("xn2", j) for j in range(TS)] + [("prep", n) for n in range(6, 9)]
        assert len(SLOTS) == 15

        def bank_of(kind, n):
            return psT[SLOTS.index((kind, n)) % 3]

        def evacuated(kind, n, b):
            if kind == "prep":
                return prep_lo, 9 * b + n + 1
            if kind == "xn2":
                return xT2_ready, TS * (b - 1) + n + 1
            return xnT_ready, HC * (b + 1) + n + 1

        def there(kind, st):
            return {"prep": True, "xn2": st.before, "xn": st.after}[kind]

        def wait_bank(eng, kind, n, st):
            slot = SLOTS.index((kind, n))
            for s in range(slot - 3, -1, -3):
                if there(SLOTS[s][0], st):
                    eng.wait_ge(*evacuated(*SLOTS[s], st.b))
                    return
            if st.before:
                eng.wait_ge(*evacuated(*SLOTS[slot % 3 + len(SLOTS) - 3], st.b - 1))
            elif slot % 3 < HC:
                eng.wait_ge(*evacuated("xn", slot % 3, -1))

        def load_experts(eng, which):
            routed = PREP if which is not None else E % PREP
            if which is None:
                which = bass.ds(E - routed, routed)
            for src, dst in ((gate_w[which, 0:P], gu_nat[:, 0:routed, 0]), (gate_w[which, P:I], gu_nat[0:IC, 0:routed, 1]),
                             (up_w[which, 0:P - IC], gu_nat[IC:P, 0:routed, 1]), (up_w[which, P - IC:I], gu_nat[:, 0:routed, 2])):
                eng.dma_start(dst, src.rearrange("e p h -> p e h")).then_inc(wstage_loaded, 16)
            for q in range(routed):
                eng.dma_start(dn_nat[:, q, :, 0:I], down_w[which][q:q + 1].rearrange("e (c p) i -> p (e c) i", p=P)).then_inc(wstage_loaded, 16)
            if routed < PREP:
                for src, dst in ((shared_gate_w[0:P], gu_nat[:, routed, 0]), (shared_gate_w[P:I], gu_nat[0:IC, routed, 1]),
                                 (shared_up_w[0:P - IC], gu_nat[IC:P, routed, 1]), (shared_up_w[P - IC:I], gu_nat[:, routed, 2])):
                    eng.dma_start(dst, src).then_inc(wstage_loaded, 16)
                eng.dma_start(dn_nat[:, routed, :, 0:I], shared_down_w.rearrange("(c p) i -> p c i", p=P)).then_inc(wstage_loaded, 16)
        WSTAGE = 16 * (4 + PREP)
        LATE_STEPS = range(NB + 1, -(-NE // PREP))
        LAST_WSTAGE = WSTAGE * LATE_STEPS[-1] + WSTAGE + 16 * 4

        def staged(b):
            return LAST_WSTAGE if isinstance(b, int) and b == LATE_STEPS[-1] else WSTAGE * b + WSTAGE

        WS = 256.0

        @block.sync
        def _(sp):
            def sp_round(i, kind):
                def tokens(c):
                    t = ROUND * i + c
                    if kind_of(t + ROUND, i, kind) == "shared":
                        sp.wait_ge(x_turned, t + 1)
                        sp.dma_start(xg[c], xn2_tiles[bass.ds(t + ROUND - ROUTED, 1)].rearrange("o p h -> p (o h)")).then_inc(xs_loaded[c], 16)

                def given(c):
                    t = ROUND * i + c
                    if kind_of(t, i, kind) == "shared":
                        if not first:
                            sp.wait_ge(o_done, t - ROUND - ROUTED + 1)
                        sp.dma_start(terms[c], y_v[bass.ds(t - ROUTED, 1)].rearrange("o p k h -> p (o k) h")).then_inc(terms_loaded[c], 16)

                def result(c):
                    t = ROUND * i + c
                    if kind_of(t - ROUND, i, kind) == "shared":
                        j = t - ROUND - ROUTED
                        sp.wait_ge(o_done, j + 1)
                        sp.dma_start(out_tiles[bass.ds(j, 1)].rearrange("o p h -> p (o h)"), o_sb[c]).then_inc(out_stored[c], 16)

                first = isinstance(i, int) and i == R_ROUNDS
                if first:
                    for c in range(ROUND):
                        tokens(c)
                    for c in range(ROUND):
                        sp.wait_ge(y_stored[c], 16 * R_ROUNDS)
                    for c in range(ROUND):
                        given(c)
                else:
                    for c in range(ROUND):
                        tokens(c)
                        given(c)
                        result(c)
                if isinstance(i, int) and i == ALL_ROUNDS:
                    for c in range(ROUND):
                        sp.wait_ge(out_stored[c], 16 * S_ROUNDS)

            sp.dma_start(x_sb[0], xv[0]).then_inc(x_loaded[0], 16)
            sp.dma_start(wqkv_sb, w_qkv.rearrange("(c p) n -> p c n", p=P)).then_inc(wattn_loaded, 16)
            sp.dma_start(x_sb[1], xv[1]).then_inc(x_loaded[1], 16)
            load_experts(sp, bass.ds(0, PREP))

            def step(st):
                b = st.b
                if st.before:
                    sp.wait_ge(x1_done, 2 * b)
                    sp.dma_start(x1_v[bass.ds(b - 1, 1)].rearrange("o p j h -> p (o j) h"), x1_sb).then_inc(x1_stored, 16)
                    sp.wait_ge(split_done, 2 * b)
                    sp.dma_start(xn2_v[bass.ds(b - 1, 1)].rearrange("o p j h -> p (o j) h"),
                                 xn2_split.rearrange("p j s h -> p j (s h)")).then_inc(xn2_stored, 16)
                if st.now:
                    if not st.before:
                        sp.wait_ge(setup_mm, 1)
                    sp.dma_start(x1_sb, xv[bass.ds(b, 1)].rearrange("o p j h -> p (o j) h")).then_inc(residual_loaded, 16)
                if st.before:
                    sp.wait_ge(xn2_stored, 16 * b)
                sp.wait_ge(prep_transposed, 9 * b + 9)
                load_experts(sp, bass.ds(PREP * b + PREP, PREP))
            steps(sp, step)
            for b in LATE_STEPS[1:]:
                sp.wait_ge(prep_transposed, 9 * b)
                load_experts(sp, bass.ds(PREP * b, PREP) if b < LATE_STEPS[-1] else None)
            sp.wait_ge(x1_stored, 16 * NB)
            sp.wait_ge(xn2_stored, 16 * NB)
            rounds(sp, sp_round)

        def w_halves(e, part):
            off = 2 * part * GU if part < HC else GUW
            width = GU if part < HC else 2 * H
            return W[:, bass.ds(e * EW + off, width)], W[:, bass.ds(e * EW + off + width, width)], width

        @block.gpsimd
        def _(pool):
            nc.gpsimd.memset(ident32[:, :], 0.0).then_inc(setup_pool, 1)
            nc.gpsimd.memset(headsel, 0.0).then_inc(setup_pool, 1)
            nc.gpsimd.memset(ones_row, 1.0).then_inc(consts_made, 1)
            nc.gpsimd.memset(mhalf[:, :], -0.5).then_inc(consts_made, 1)
            nc.gpsimd.memset(zero[:, :], 0.0).then_inc(consts_made, 1)
            nc.gpsimd.memset(eps[:, :], LN_EPS).then_inc(consts_made, 1)
            pool.wait_ge(setup_pool, 2)
            nc.gpsimd.affine_select(out=ident32[:, :], in_=ident32[:, :], compare_op=ALU.not_equal, fill=1.0,
                                    base=0, pattern=[[-1, P]], channel_multiplier=1).then_inc(consts_made, 1)
            hv = headsel.rearrange("p (h d) -> p h d", d=D)
            nc.gpsimd.affine_select(out=hv, in_=hv, compare_op=ALU.not_equal, fill=1.0,
                                    base=0, pattern=[[-1, HEADS], [0, D]], channel_multiplier=1).then_inc(consts_made, 1)
            pool.wait_ge(consts_made, 6)
            nc.gpsimd.tensor_copy(ident16[:, :], ident32[:, :]).then_inc(consts_made, 1)

            nc.gpsimd.iota(iota_i[:, :], [[1, ROUTED]], base=0, channel_multiplier=0).then_inc(setup_pool, 1)
            nc.gpsimd.memset(before[:, :], -1.0).then_inc(setup_pool, 1)
            nc.gpsimd.memset(ones16[:, :], 1.0).then_inc(route_made, 1)
            nc.gpsimd.memset(one[:, :], 1.0).then_inc(route_made, 1)
            nc.gpsimd.iota(counts_i[:, 0:3], [[1, 3]], base=0, channel_multiplier=1).then_inc(setup_pool, 1)
            nc.gpsimd.iota(gtab[:, 0:K * NT], [[P, K * NT]], base=P, channel_multiplier=1).then_inc(setup_pool, 1)
            pool.wait_ge(setup_pool, 6)
            nc.gpsimd.tensor_copy(iota_e[:, :], iota_i[:, 0:E]).then_inc(route_made, 1)
            nc.gpsimd.tensor_copy(iota_s[:, :], iota_i[:, :]).then_inc(route_made, 1)
            nc.gpsimd.tensor_copy(number[:, :], gtab[:, 0:K * NT]).then_inc(route_made, 1)
            nc.gpsimd.affine_select(out=before[:, :], in_=before[:, :], compare_op=ALU.is_ge, fill=0.0,
                                    base=0, pattern=[[-1, P]], channel_multiplier=1).then_inc(route_made, 1)
            nc.gpsimd.tensor_scalar(row[:, 0:1], counts_i[:, 0:1], 0.0, None, ALU.add).then_inc(route_made, 1)
            nc.gpsimd.tensor_scalar(row[:, 1:2], counts_i[:, 0:1], float(P), None, ALU.add).then_inc(route_made, 1)
            nc.gpsimd.tensor_scalar(row[:, 2:3], counts_i[:, 0:1], float(T * TERMS), None, ALU.add).then_inc(route_made, 1)

            def hold(semaphore, value):
                if not isinstance(value, int):
                    value = pool.to_reg(value)
                    pool.wait_ge(route_made, 9)
                pool.wait_ge(semaphore, value)

            def pool_round(i, kind):
                for c in range(ROUND):
                    t = ROUND * i + c
                    if kind_of(t + ROUND, i, kind) == "routed":
                        hold(gcur_done, t + 2)
                        gather(c)
                    if kind_of(t - ROUND, i, kind) == "routed":
                        hold(scur_done, t - ROUND + 1)
                        nc.gpsimd.indirect_dma_start(y_dram[:, :], bass.IndirectOffsetOnAxis(ap=scur[:, c:c + 1], axis=0), y_sb[c], None).then_inc(y_stored[c], 16)
                for c in range(ROUND):
                    t = ROUND * i + c
                    if kind_of(t - 1, i, kind) == "shared":
                        j, r = t - 1 - ROUTED, (c - 1) % ROUND
                        pool.wait_ge(terms_scaled, j + 1)
                        nc.gpsimd.tensor_tensor(terms[r][:, 1:3], terms[r][:, 1:3], terms[r][:, 3:5], ALU.add).then_inc(pairs_added, 1)
                        pool.wait_ge(pairs_added, j + 1)
                        nc.gpsimd.tensor_tensor(terms[r][:, 1], terms[r][:, 1], terms[r][:, 2], ALU.add).then_inc(terms_added, 1)

            def gather(c):
                nc.gpsimd.indirect_dma_start(xg[c], None, xn2_dram[:, :], bass.IndirectOffsetOnAxis(ap=gcur[:, c:c + 1], axis=0)).then_inc(xg_loaded[c], 16)

            def root(n, b):
                pool.wait_ge(ln_aggr[n], TS * b + TS)
                nc.gpsimd.tensor_tensor(vare[n][:, :], mv[n][:, :, 1], eps[:, :], ALU.add).then_inc(ln_vare[n], 1)
                pool.wait_ge(ln_vare[n], b + 1)
                nc.gpsimd.tensor_tensor(rstd[n][:, :], vare[n][:, :], mhalf[:, :], ALU.pow).then_inc(ln_rstd[n], 1)

            def double_tail(b):
                pool.wait_ge(wstage_loaded, staged(b))
                nc.gpsimd.tensor_tensor(dn_nat[:, :, :, I:I + IC], dn_nat[:, :, :, P:I],
                                        zero[:, :].unsqueeze(1).unsqueeze(1).to_broadcast([P, PREP, HC, IC]), ALU.add).then_inc(tail_doubled, 1)

            def k_sum_product(b, c):
                pool.wait_ge(qphi_done, HC * b + c + 1)
                pool.wait_ge(ksum_done, HC * b + c + 1)
                nc.gpsimd.tensor_tensor(qks[c], qphi[c], ksum[c], ALU.mult).then_inc(qks_done, 1)

            def kv_sum_product(b, c):
                pool.wait_ge(kvsum_done, HC * b + c + 1)
                nc.gpsimd.tensor_tensor(kvsum[c], qphi[c], kvsum[c], ALU.mult).then_inc(qkv_done, 1)

            def step(st):
                b = st.b
                if st.after:
                    root(0, b + 1)
                if st.now:
                    k_sum_product(b, 0)
                double_tail(b)
                if st.before:
                    root(1, b - 1)
                if st.now:
                    kv_sum_product(b, 0)
                if st.before:
                    for h in range(2):
                        part = slice(2 * h, 2 * h + 2)
                        pool.wait_ge(hi_done, 2 * (b - 1) + h + 1)
                        nc.gpsimd.tensor_tensor(xn2_split[:, part, 1], xn2[:, part], xn2_split[:, part, 0], ALU.subtract).then_inc(split_done, 1)
                if st.now:
                    k_sum_product(b, 1)
                    kv_sum_product(b, 1)

            root(0, 0)
            steps(pool, step)
            for b in LATE_STEPS:
                double_tail(b)
                for n in range(9):
                    m = 9 * b + n
                    hi, lo, width = w_halves(PREP * b + n // 3, n % 3)
                    pool.wait_ge(prep_hi, m + 1)
                    nc.gpsimd.tensor_tensor(lo, wide[m % 2][:, 0:width], hi, ALU.subtract).then_inc(prep_lo, 1)
            pool.wait_ge(xn2_stored, 16 * NB)
            pool.wait_ge(prep_transposed, 9 * (LATE_STEPS[-1] + 1))
            hold(gcur_done, 1)
            for c in range(ROUND):
                gather(c)
            rounds(pool, pool_round)

        @block.scalar
        def _(act):
            act.dma_start(decay_in[:, :], decay_param.rearrange("(h o) -> h o", o=1)).then_inc(consts_loaded, 16)
            act.dma_start(rb_row[:, :], router_b.rearrange("(o e) -> o e", o=1)).then_inc(consts_loaded, 16)
            act.dma_start(rw_nat, router_w).then_inc(consts_loaded, 16)
            act.dma_start(wout_sb, w_out.rearrange("(c p) n -> p c n", p=P)).then_inc(wattn_loaded, 16)
            act.wait_ge(setup_mm, 1)
            nc.scalar.activation(decay[:, :], psK[:, 0:HC], ACT.Exp, scale=-1.0).then_inc(setup_act, 1)
            nc.scalar.activation(blockones, psQ[:, 0:P], ACT.Copy).then_inc(setup_act, 1)
            nc.scalar.activation(rb[:, :], psV[:, 0:E], ACT.Copy).then_inc(setup_act, 1)
            nc.scalar.activation(rwT[:, :, 0, :], psD[:, 0, 0:HC * E].rearrange("p (c e) -> p c e", c=HC), ACT.Copy, scale=WS).then_inc(setup_act, 1)

            def act_round(i, kind):
                for c in range(ROUND):
                    t = ROUND * i + c
                    if kind_of(t, i, kind):
                        act.wait_ge(gu_ready, t + 1)
                        nc.scalar.activation(gate[c % 2], psG[c % 2][:, 0:I], ACT.Silu, scale=1 / WS).then_inc(silu_done, 1)
                    if kind_of(t - 1, i, kind):
                        u = (c - 1) % 2
                        act.wait_ge(a_turned, t)
                        nc.scalar.activation(aT_hi[u], psA[u][:, 0:P], ACT.Copy).then_inc(aT_hi_done, 1)
                        nc.scalar.activation(aT_tail[u][0:IC], psA[u][0:IC, P:2 * P], ACT.Copy).then_inc(aT_hi_done, 1)
                    if kind_of(t - 2, i, kind) == "routed":
                        u = c % 2
                        y = (c - 2) % ROUND
                        act.wait_ge(y_ready, t - 1)
                        if kind or t - 2 >= ROUND:
                            act.wait_ge(y_stored[y], 16 * (i if c >= 2 else i - 1))
                        nc.scalar.activation(y_sb[y], psY[u], ACT.Copy, scale=1 / WS).then_inc(y_done, 1)
                        nc.scalar.activation(scur[:, y:y + 1], stab[:, bass.ds(t - 2, 1)], ACT.Copy).then_inc(scur_done, 1)
                    if kind_of(t - 1, i, kind) == "shared":
                        j, r = t - 1 - ROUTED, (c - 1) % ROUND
                        act.wait_ge(terms_loaded[r], 16 * ((i if c >= 1 else i - 1) - R_ROUNDS + 1))
                        for k in range(1, K):
                            last = nc.scalar.activation(terms[r][:, k], terms[r][:, k], ACT.Copy, scale=share[:, bass.ds(j, 1), k])
                        last.then_inc(terms_scaled, 1)

            def xn_out(b):
                for c in range(HC):
                    act.wait_ge(xn_transposed, HC * b + c + 1)
                    nc.scalar.activation(xnT[:, c, :], bank_of("xn", c)[:, :], ACT.Copy).then_inc(xnT_ready, 1)

            def prep_out(b, n):
                act.wait_ge(prep_transposed, 9 * b + n + 1)
                dst, _, width = w_halves(PREP * b + n // 3, n % 3)
                nc.scalar.activation(dst, bank_of("prep", n)[:, 0:width], ACT.Copy, scale=WS).then_inc(prep_hi, 1)

            def k_parts(b, c):
                act.wait_ge(k_ready, HC * b + c + 1)
                nc.scalar.activation(kv[c], psK[:, :], ACT.Exp)
                nc.scalar.activation(kphi[c], psK[:, :], ACT.Relu).then_inc(k_acted, 1)

            def q_parts(b, c):
                act.wait_ge(q_ready, HC * b + c + 1)
                nc.scalar.activation(qks[c], psQ[:, :], ACT.Exp)
                nc.scalar.activation(qphi[c], psQ[:, :], ACT.Relu).then_inc(q_acted, 1)

            def step(st):
                b = st.b
                if st.before and st.after:
                    act.wait_ge(xn_ready, TS * b)
                    act.dma_start(x_sb[1 - st.parity], xv[bass.ds(b + 1, 1)].rearrange("o p j h -> p (o j) h")).then_inc(x_loaded[1 - st.parity], 16)
                if st.now:
                    k_parts(b, 0)
                if st.before:
                    act.wait_ge(den_inverted, b)
                    nc.scalar.activation(attn_words.rearrange("p (n d) -> p n d", d=D), rden[:, :].unsqueeze(2).to_broadcast([P, TS * HEADS, D]), ACT.Copy).then_inc(rden_spread, 1)
                if st.now:
                    q_parts(b, 0)
                    k_parts(b, 1)
                prep_out(b, 0)
                if st.now:
                    q_parts(b, 1)
                prep_out(b, 1)
                prep_out(b, 2)
                if st.before:
                    if not st.now:
                        act.wait_ge(xn2_stored, 16 * (b - 1))
                    for h in range(2):
                        act.wait_ge(xn2_ready, TS * (b - 1) + 2 * h + 2)
                        nc.scalar.activation(xn2_split[:, 2 * h:2 * h + 2, 0], xn2[:, 2 * h:2 * h + 2], ACT.Copy).then_inc(hi_done, 1)
                if st.after:
                    xn_out(b + 1)
                prep_out(b, 3)
                prep_out(b, 4)
                prep_out(b, 5)
                if st.before:
                    for j in range(TS):
                        act.wait_ge(xn2_transposed, TS * (b - 1) + j + 1)
                        nc.scalar.activation(xT2[j % 2].rearrange("p s c t -> p (s c t)"),
                                             bank_of("xn2", j)[:, 0:H].bitcast(f16), ACT.Copy).then_inc(xT2_ready, 1)
                for n in range(6, 9):
                    prep_out(b, n)

            xn_out(0)
            steps(act, step)
            act.wait_ge(share_shifted, 1)
            nc.scalar.activation(share[:, :, :], share[:, :, :], ACT.Exp).then_inc(share_exp, 1)
            def late_out(b, n):
                m = 9 * b + n
                hi, _, width = w_halves(PREP * b + n // 3, n % 3)
                act.wait_ge(prep_transposed, m + 1)
                if m >= 9 * LATE_STEPS[0] + 2:
                    act.wait_ge(prep_lo, m - 1)
                nc.scalar.activation(wide[m % 2][:, 0:width], psT[n % 3][:, 0:width], ACT.Copy, scale=WS)
                nc.scalar.activation(hi, psT[n % 3][:, 0:width], ACT.Copy, scale=WS).then_inc(prep_hi, 1)

            def hot(j, parity):
                k = K - 1
                if not (isinstance(j, int) and j < 2):
                    act.wait_ge(placed, K * j - K)
                nc.scalar.activation(last_hi_hot[parity], iota_s[:, :], ACT.Abs, bias=minus_hi[:, k, bass.ds(j, 1)]).then_inc(distances, 1)
                act.wait_ge(distances, j + 1)
                nc.scalar.activation(last_hi_hot[parity], last_hi_hot[parity], ACT.Relu, bias=number[:, bass.ds(K * j + k, 1)],
                                     scale=minus_number[:, bass.ds(K * j + k, 1)]).then_inc(act_hot_done, 1)

            for n in range(9):
                late_out(LATE_STEPS[0], n)
            act.wait_ge(slots_ready, 2)
            hot(0, 0)
            for n in range(9):
                hot(n + 1, (n + 1) % 2)
                late_out(LATE_STEPS[1], n)
            with act.Fori(5, NT // 2) as i:
                hot(2 * i, 0)
                hot(2 * i + 1, 1)
            rounds(act, act_round)

        @block.vector
        def _(dve):
            def norm_stats(n, src, b):
                for j in range(TS):
                    nc.vector.bn_stats(stats[n][:, j], src[:, j]).then_inc(ln_stats[n], 1)
                wait_apart(dve, ln_stats[n], TS * b + TS)
                for j in range(TS):
                    nc.vector.bn_aggr(mv[n][:, j], stats[n][:, j]).then_inc(ln_aggr[n], 1)

            dve.wait_ge(x_loaded[0], 16)
            norm_stats(0, x_sb[0], 0)
            dve.wait_ge(setup_act, 4)
            nc.vector.tensor_scalar(decay[:, :], decay[:, :], 1.0, None, ALU.add).then_inc(setup_dve, 1)
            nc.vector.scalar_tensor_tensor(rwT[:, :, 1, :], psD[:, 0, 0:HC * E].rearrange("p (c e) -> p c e", c=HC), WS,
                                           rwT[:, :, 0, :], ALU.mult, ALU.subtract).then_inc(setup_dve, 1)
            dve.wait_ge(setup_dve, 2)
            nc.vector.memset(logits[:, :, :], 0.0).then_inc(logits_done, 1)
            nc.vector.reciprocal(decay[:, :], decay[:, :]).then_inc(setup_dve, 1)
            dve.wait_ge(setup_dve, 3)

            def norm(n, dst, src, b, done):
                dve.wait_ge(ln_rstd[n], b + 1)
                for j in range(TS):
                    nc.vector.tensor_scalar(dst[:, j], src[:, j], mv[n][:, j, 0:1], rstd[n][:, j:j + 1],
                                            ALU.subtract, ALU.mult).then_inc(done, 1)

            def phi(b, c):
                n = HC * b + c
                dve.wait_ge(k_acted, n + 1)
                nc.vector.scalar_tensor_tensor(kphi[c], kv[c], 1.0, kphi[c], ALU.min, ALU.add).then_inc(kphi_done, 1)
                dve.wait_ge(q_acted, n + 1)
                nc.vector.scalar_tensor_tensor(qphi[c], qks[c], 1.0, qphi[c], ALU.min, ALU.add).then_inc(qphi_done, 1)
                dve.wait_ge(kphi_done, n + 1)
                nc.vector.tensor_tensor_scan(ksum[c], decay[:, c:c + 1].to_broadcast([P, S]), kphi[c], 0.0, ALU.mult, ALU.add).then_inc(ksum_done, 1)

            def k_times_v(b, c):
                dve.wait_ge(v_ready, HC * b + c + 1)
                if not (isinstance(b, int) and b == 0):
                    dve.wait_ge(attn_done, HC * b)
                nc.vector.tensor_tensor(kv[c], psV[:, :], kphi[c], ALU.mult).then_inc(kv_done, 1)

            def kv_sum(b, c):
                dve.wait_ge(kv_done, HC * b + c + 1)
                nc.vector.tensor_tensor_scan(kvsum[c], decay[:, c:c + 1].to_broadcast([P, S]), kv[c], 0.0, ALU.mult, ALU.add).then_inc(kvsum_done, 1)

            def prep_out(b, n):
                dve.wait_ge(prep_hi, 9 * b + n + 1)
                hi, dst, width = w_halves(PREP * b + n // 3, n % 3)
                nc.vector.scalar_tensor_tensor(dst, bank_of("prep", n)[:, 0:width], WS, hi, ALU.mult, ALU.subtract).then_inc(prep_lo, 1)

            def step(st):
                b = st.b
                if st.before:
                    dve.wait_ge(den_ready, b)
                    nc.vector.tensor_scalar(rden[:, :], psD[:, 0, 0:TS * HEADS], DEN_EPS, None, ALU.max).then_inc(den_clipped, 1)
                    dve.wait_ge(den_clipped, b)
                    nc.vector.reciprocal(rden[:, :], rden[:, :]).then_inc(den_inverted, 1)
                if st.after:
                    dve.wait_ge(x_loaded[1 - st.parity], 16 * ((st.half if st.parity == 0 else st.half + 1) + 1))
                    norm_stats(0, x_sb[1 - st.parity], b + 1)
                if st.before:
                    for c in range(HC):
                        if c == 0:
                            dve.wait_ge(rden_turned, b)
                            dve.wait_ge(qkv_done, HC * b)
                        nc.vector.tensor_tensor(attnT[:, c, :], kvsum[c], psD[:, c, :], ALU.mult).then_inc(attn_done, 1)
                if st.now:
                    phi(b, 0)
                    k_times_v(b, 0)
                if st.before:
                    for h in range(2):
                        if h == 0:
                            dve.wait_ge(residual_loaded, 16 * b)
                        dve.wait_ge(proj_ready, 2 * (b - 1) + h + 1)
                        nc.vector.tensor_tensor(x1_sb[:, 2 * h:2 * h + 2], psD[:, h, :].rearrange("p (j h) -> p j h", h=H),
                                                x1_sb[:, 2 * h:2 * h + 2], ALU.add).then_inc(x1_done, 1)
                    dve.wait_ge(x1_done, 2 * b)
                    norm_stats(1, x1_sb, b - 1)
                if st.after:
                    dve.wait_ge(xn_transposed, HC * b + HC)
                    norm(0, xn, x_sb[1 - st.parity], b + 1, xn_ready)
                if st.now:
                    kv_sum(b, 0)
                prep_out(b, 0)
                if st.before:
                    dve.wait_ge(x1_stored, 16 * b)
                    norm(1, xn2, x1_sb, b - 1, xn2_ready)
                for n in range(1, 6):
                    prep_out(b, n)
                if st.now:
                    phi(b, 1)
                    k_times_v(b, 1)
                    kv_sum(b, 1)
                if st.before:
                    dve.wait_ge(logits_ready, TS * b)
                    nc.vector.scalar_tensor_tensor(logits[:, :, :], psD[:, 0, 0:TS * E].rearrange("p (j e) -> p j e", e=E), 1 / WS,
                                                   rb[:, :].unsqueeze(1).to_broadcast([P, TS, E]), ALU.mult, ALU.add).then_inc(logits_done, 1)
                for n in range(6, 9):
                    prep_out(b, n)
                if st.before:
                    wait_apart(dve, logits_done, b + 1)
                    for j in range(TS):
                        nc.vector.max(top8[:, j], logits[:, j]).then_inc(top_done, 1)
                    wait_apart(dve, top_done, TS * b)
                    for j in range(TS):
                        nc.vector.max_index(idx8[:, j], top8[:, j], logits[:, j]).then_inc(topi_done, 1)
                    dve.wait_ge(topi_done, (TS + 2) * (b - 1) + TS)
                    nc.vector.tensor_copy(topv[:, bass.ds(TS * (b - 1), TS), :], top8[:, :, 0:K]).then_inc(topi_done, 1)
                    nc.vector.tensor_copy(topi[:, bass.ds(TS * (b - 1), TS), :], idx8[:, :, 0:K]).then_inc(topi_done, 1)

            links = [0]

            def link(instruction):
                links[0] += 1
                instruction.then_inc(chain, 1)
                dve.wait_ge(chain, links[0])

            def dispatch():
                v = nc.vector
                dve.wait_ge(route_made, 9)
                dve.wait_ge(x1_stored, 16 * NB)
                dve.wait_ge(xn2_stored, 16 * NB)
                dve.wait_ge(topi_done, (TS + 2) * NB)
                link(v.tensor_copy(share_sum[:, :], topv[:, :, 0]))
                v.tensor_tensor(share[:, :, :], topv[:, :, :], share_sum[:, :].unsqueeze(2).to_broadcast([P, NT, K]), ALU.subtract).then_inc(share_shifted, 1)
                for k in range(K):
                    v.tensor_tensor(chosen[k].rearrange("p (e j) -> p e j", e=E), topi[:, :, k].unsqueeze(1).to_broadcast([P, E, NT]),
                                    iota_e[:, :].unsqueeze(2).to_broadcast([P, E, NT]), ALU.is_equal).then_inc(chosen_done, 1)
                dve.wait_ge(ranks_ready, 1)
                link(v.tensor_tensor_scan(dest, one[:, :].to_broadcast([P, E * NT]), psD[:, :, :].rearrange("p a b -> p (a b)"), 0.0, ALU.mult, ALU.add))
                dest_v = dest.rearrange("p (e j) -> p e j", e=E)
                v.memset(seen[:, 0:1], 0.0)
                link(v.tensor_copy(seen[:, 1:E], dest_v[:, 0:E - 1, NT - 1]))
                link(v.tensor_tensor(counts[:, :], dest_v[:, :, NT - 1], seen[:, :], ALU.subtract))
                link(v.tensor_scalar(counts_i[:, :], counts[:, :], float(P - 1), None, ALU.add))
                link(v.tensor_scalar(counts_i[:, :], counts_i[:, :], P.bit_length() - 1, None, ALU.arith_shift_right))
                link(v.tensor_copy(counts[:, :], counts_i[:, :]))
                link(v.tensor_tensor_scan(tile_end[:, :], one[:, :].to_broadcast([P, E]), counts[:, :], 0.0, ALU.mult, ALU.add))
                link(v.tensor_tensor(shift[:, :], tile_end[:, :], counts[:, :], ALU.subtract))
                link(v.scalar_tensor_tensor(shift[:, :], shift[:, :], float(P), seen[:, :], ALU.mult, ALU.subtract))
                half = E * NT // 2
                for n, bank in enumerate((psK, psQ)):
                    last = v.tensor_tensor(dest[:, n * half:(n + 1) * half], bank[:, :], dest[:, n * half:(n + 1) * half], ALU.add)
                link(last)
                link(v.tensor_tensor(dest_v, dest_v, shift[:, :].unsqueeze(2).to_broadcast([P, E, NT]), ALU.add))
                for k in range(K):
                    link(v.tensor_tensor(picked, chosen[k], dest, ALU.mult))
                    link(v.tensor_reduce(slot[:, k, :], picked.rearrange("p (e j) -> p j e", e=E), AX.X, ALU.add))
                flat = slot[:, :, :].rearrange("p k j -> p (k j)")
                hi, lo = slot_hi[:, :, :].rearrange("p k j -> p (k j)"), slot_lo[:, :, :].rearrange("p k j -> p (k j)")
                link(v.tensor_copy(slot_i, flat))
                link(v.tensor_scalar(slot_i, slot_i, P.bit_length() - 1, None, ALU.arith_shift_right))
                link(v.tensor_copy(hi, slot_i))
                link(v.scalar_tensor_tensor(lo, hi, -float(P), flat, ALU.mult, ALU.add))
                v.tensor_scalar(rest[:, 0:K * NT], hi, -1.0, None, ALU.mult).then_inc(slots_ready, 1)
                v.tensor_scalar(minus_number, number[:, :], -1.0, None, ALU.mult).then_inc(slots_ready, 1)
                for n in range(2):
                    v.tensor_scalar((counts, shift)[n][:, :], tile_end[:, :], row[:, n:n + 1], None, ALU.is_le, ALU.add, accum_out=owner[:, n:n + 1]).then_inc(owner_done, 1)
                dve.wait_ge(owner_turned, 1)
                v.memset(owner_i[:, 0:2], 0)
                v.tensor_scalar(owner_i[:, 2:], psD[0:1, 0, 0:ROUTED], float(E - 1), float(EW), ALU.min, ALU.mult).then_inc(owner_ready, 1)

                def hot(j, parity, first):
                    col = bass.ds(j, 1)
                    if not first:
                        dve.wait_ge(placed, K * j - K)
                    v.tensor_tensor(lo_hot[parity], iota_s[:, 0:P].unsqueeze(1).to_broadcast([P, K, P]),
                                    slot_lo[:, :, col].to_broadcast([P, K, P]), ALU.is_equal)
                    for k in range(DVE_HOT):
                        n = K * j + k
                        if not (first and j == 0):
                            dve.wait_ge(placed, n - K + 1)
                        v.tensor_scalar(hi_hot[k], iota_s[:, :], slot_hi[:, k, col], number[:, bass.ds(n, 1)], ALU.is_equal, ALU.mult).then_inc(hot_done, 1)

                hot(0, 0, True)
                hot(1, 1, True)
                with dve.Fori(1, NT // 2) as i:
                    hot(2 * i, 0, False)
                    hot(2 * i + 1, 1, False)
                dve.wait_ge(placed, K * NT)
                table = psV[:, 0:ROUTED]
                link(v.tensor_scalar(place, table, -float(P), 0.0, ALU.add, ALU.max))
                link(v.tensor_copy(place_i, place))
                v.tensor_scalar(gtab[:, :], place_i, (P * K).bit_length() - 1, P.bit_length() - 1, ALU.arith_shift_right, ALU.logical_shift_left)
                link(v.tensor_scalar(stab[:, :], place_i, P.bit_length() - 1, K - 1, ALU.arith_shift_right, ALU.bitwise_and))
                link(v.tensor_scalar(place_i, place_i, P - 1, None, ALU.bitwise_and))
                link(v.tensor_tensor(gtab[:, :], gtab[:, :], place_i, ALU.add))
                v.tensor_copy(gcur[:, :], gtab[:, 0:ROUND]).then_inc(gcur_done, 1)
                link(v.tensor_scalar(place, iota_s[:, :], float(P), row[:, 2:3], ALU.mult, ALU.add))
                v.scalar_tensor_tensor(place, table, 0.0, place, ALU.is_equal, ALU.mult)
                link(v.tensor_copy(place_i, gtab[:, :]))
                link(v.tensor_scalar(place_i, place_i, K.bit_length() - 1, None, ALU.logical_shift_left))
                link(v.tensor_tensor(stab[:, :], stab[:, :], place_i, ALU.add))
                link(v.tensor_tensor(stab[:, :], stab[:, :], gtab[:, :], ALU.add))
                link(v.tensor_copy(place_i, place))
                v.tensor_tensor(stab[:, :], stab[:, :], place_i, ALU.add).then_inc(tables_done, 1)
                dve.wait_ge(share_exp, 1)
                link(v.tensor_reduce(share_sum[:, :], share[:, :, :], AX.X, ALU.add))
                link(v.reciprocal(share_sum[:, :], share_sum[:, :]))
                v.scalar_tensor_tensor(share[:, :, :], share[:, :, :], SCALE, share_sum[:, :].unsqueeze(2).to_broadcast([P, NT, K]), ALU.mult, ALU.mult).then_inc(share_done, 1)
                dve.wait_ge(share_done, 1)

            def turn_out(tile, c, kind):
                dve.wait_ge(x_turned, tile + 1)
                nc.vector.tensor_copy(xT[c % 2].rearrange("p s c t -> p (s c t)"), psX[c % 2]).then_inc(xT_done, 1)
                if kind_of(tile + ROUND, None, kind) == "routed":
                    nc.vector.tensor_copy(gcur[:, c % ROUND:c % ROUND + 1], gtab[:, bass.ds(tile + ROUND, 1)]).then_inc(gcur_done, 1)

            def dve_round(i, kind):
                if isinstance(i, int) and i == 0:
                    turn_out(0, 0, None)
                for c in range(ROUND):
                    t = ROUND * i + c
                    if kind_of(t + 1, i, kind):
                        turn_out(t + 1, c + 1, kind)
                    if kind_of(t - 2, i, kind) == "shared":
                        j, r = t - 2 - ROUTED, (c - 2) % ROUND
                        dve.wait_ge(terms_added, j + 1)
                        nc.vector.scalar_tensor_tensor(terms[r][:, 0], terms[r][:, 0], share[:, bass.ds(j, 1), 0], terms[r][:, 1], ALU.mult, ALU.add).then_inc(o_started, 1)
                    if kind_of(t, i, kind):
                        dve.wait_ge(silu_done, t + 1)
                        nc.vector.scalar_tensor_tensor(act32[c % 2], psG[c % 2][:, I:GU], 1 / WS, gate[c % 2], ALU.mult, ALU.mult).then_inc(a_done, 1)
                    if kind_of(t - 1, i, kind):
                        u = (c - 1) % 2
                        dve.wait_ge(aT_hi_done, 2 * t)
                        nc.vector.tensor_tensor(aT_lo[u], psA[u][:, 0:P], aT_hi[u], ALU.subtract)
                        nc.vector.tensor_tensor(aT_tail[u][IC:P], psA[u][0:IC, P:2 * P], aT_tail[u][0:IC], ALU.subtract).then_inc(aT_lo_done, 1)
                    if kind_of(t - 2, i, kind) == "shared":
                        j, r = t - 2 - ROUTED, (c - 2) % ROUND
                        if kind or j >= ROUND:
                            dve.wait_ge(out_stored[r], 16 * ((i if c >= 2 else i - 1) - R_ROUNDS))
                        dve.wait_ge(o_started, j + 1)
                        dve.wait_ge(y_ready, t - 1)
                        nc.vector.scalar_tensor_tensor(o_sb[r], psY[c % 2], 1 / WS, terms[r][:, 0], ALU.mult, ALU.add).then_inc(o_done, 1)

            norm(0, xn, x_sb[0], 0, xn_ready)
            steps(dve, step)
            dispatch()
            rounds(dve, dve_round)

        @block.tensor
        def _(pe):
            pe.wait_ge(consts_made, 7)
            pe.wait_ge(consts_loaded, 48)
            for c in range(HC):
                nc.tensor.matmul(psK[:, c:c + 1], headsel[:, c * P:(c + 1) * P], decay_in[:, :], start=True, stop=True)
            nc.tensor.matmul(psQ[:, 0:P], headsel[:, 0:P], headsel[:, 0:P], start=True, stop=True)
            nc.tensor.matmul(psV[:, 0:E], ones_row, rb_row[:, :], start=True, stop=True)
            for c in range(HC):
                last = nc.tensor.transpose(psD[:, 0, c * E:(c + 1) * E], rw_nat[:, c * P:(c + 1) * P], ident32[0:E, 0:E])
            last.then_inc(setup_mm, 1)

            def xn_in(b):
                pe.wait_ge(xn_ready, TS * b + TS)
                for c in range(HC):
                    for j in range(TS):
                        last = nc.tensor.transpose(bank_of("xn", c)[:, j * P:(j + 1) * P], xn[:, j, c * P:(c + 1) * P], ident32[:, :])
                    last.then_inc(xn_transposed, 1)

            def prep_in(st, n, late=False):
                if n == 0:
                    pe.wait_ge(wstage_loaded, staged(st.b))
                if n == 2:
                    pe.wait_ge(tail_doubled, st.b + 1)
                if not late:
                    wait_bank(pe, "prep", n, st)
                elif not (st.b == LATE_STEPS[0] and n < 3):
                    pe.wait_ge(prep_hi, 9 * st.b + n - 2)
                bank, q, part = psT[n % 3] if late else bank_of("prep", n), n // 3, n % 3
                if part < HC:
                    for m in range(3):
                        last = nc.tensor.transpose(bank[:, m * P:(m + 1) * P], gu_nat[:, q, m, part * P:(part + 1) * P], ident32[:, :])
                else:
                    for c in range(HC):
                        nc.tensor.transpose(bank[:, c * P:(c + 1) * P], dn_nat[:, q, c, 0:P], ident32[:, :])
                        last = nc.tensor.transpose(bank[:, H + c * P:H + (c + 1) * P],
                                                   dn_nat[:, q, c, P:I + IC], ident32[:, :])
                last.then_inc(prep_transposed, 1)

            def late_and_dispatch():
                pe.wait_ge(route_made, 9)
                pe.wait_ge(topi_done, (TS + 2) * NB)
                half = E * NT // 2
                for k in range(K):
                    pe.wait_ge(chosen_done, k + 1)
                    for n, bank in enumerate((psK, psQ)):
                        nc.tensor.matmul(bank[:, :], before[:, :], chosen[k][:, n * half:(n + 1) * half], start=(k == 0), stop=(k == K - 1))
                        last = nc.tensor.matmul(psD[:, n, :], ones16[:, :], chosen[k][:, n * half:(n + 1) * half], start=(k == 0), stop=(k == K - 1))
                last.then_inc(ranks_ready, 1)
                pe.wait_ge(xT2_ready, NT)
                for n in range(9):
                    prep_in(Step(LATE_STEPS[0], 0, 0), n, late=True)
                pe.wait_ge(owner_done, 2)
                for w in range(2):
                    last = nc.tensor.transpose(psD[0:1, 0, w * P:(w + 1) * P], owner[:, w:w + 1], ident32[:, :])
                last.then_inc(owner_turned, 1)

                def hot(j, parity, first=False, last=False):
                    for k in range(K):
                        if k < DVE_HOT:
                            pe.wait_ge(hot_done, DVE_HOT * j + k + 1)
                        else:
                            pe.wait_ge(act_hot_done, j + 1)
                        nc.tensor.matmul(psV[:, 0:ROUTED], lo_hot[parity][:, k], hi_hot[k] if k < DVE_HOT else last_hi_hot[parity], start=(first and k == 0), stop=(last and k == K - 1)).then_inc(placed, 1)

                hot(0, 0, first=True)
                assert len(LATE_STEPS) == 2
                for n in range(9):
                    prep_in(Step(LATE_STEPS[1], 0, 0), n, late=True)
                    hot(n + 1, (n + 1) % 2)
                with pe.Fori(5, NT // 2 - 1) as i:
                    hot(2 * i, 0)
                    hot(2 * i + 1, 1)
                hot(NT - 2, 0)
                hot(NT - 1, 1, last=True)
                pe.wait_ge(owner_ready, 1)
                pe.wait_ge(tables_done, 1)
                pe.wait_ge(prep_lo, 9 * (LATE_STEPS[-1] + 1))

            def turn_in(tile, c, i, kind):
                if kind == "routed":
                    pe.wait_ge(xg_loaded[c % ROUND], 16 * (i + 1 + c // ROUND))
                else:
                    pe.wait_ge(xs_loaded[c % ROUND], 16 * (i + 1 + c // ROUND - R_ROUNDS))
                for n in range(2 * HC):
                    last = nc.tensor.transpose(psX[c % 2][:, n * P:(n + 1) * P], xg[c % ROUND][:, n * P:(n + 1) * P], ident16[:, :])
                last.then_inc(x_turned, 1)

            expert_at = [pe.alloc_register(f"expert_at{n}") for n in range(ROUND + 2)]

            def experts_of(i):
                pe.load(expert_at, owner_i[0:1, bass.ds(ROUND * i, ROUND + 2)])
                return [pe.snap(r, min_val=0, max_val=(E - 1) * EW) for r in expert_at]

            last_at = [0] * 2

            def pe_round(i, kind):
                if isinstance(i, int) and i == 0:
                    turn_in(0, 0, 0, "routed")
                routed = kind == "routed" if kind else i < R_ROUNDS
                at_of = experts_of(i) if routed else last_at[-2:] + [E * EW] * ROUND
                last_at[:] = at_of
                for c in range(ROUND):
                    t = ROUND * i + c
                    now, last_kind = kind_of(t, i, kind), kind_of(t - 2, i, kind)
                    if now:
                        at = at_of[c + 2]
                        pe.wait_ge(xT_done, t + 1)
                        n = 0
                        for sx, sw in ((0, 0), (0, 1), (1, 0)):
                            for h in range(HC):
                                last = nc.tensor.matmul(psG[c % 2][:, 0:GU], xT[c % 2][:, sx, h], W[:, bass.ds(at + (2 * h + sw) * GU, GU)],
                                                        start=(n == 0), stop=(n == 3 * HC - 1))
                                n += 1
                        last.then_inc(gu_ready, 1)
                    if kind_of(t + 1, i, kind):
                        turn_in(t + 1, c + 1, i, kind_of(t + 1, i, kind))
                    if kind_of(t - 1, i, kind):
                        u = (c - 1) % 2
                        pe.wait_ge(a_done, t)
                        nc.tensor.transpose(psA[u][:, 0:P], act32[u][:, 0:P], ident32[:, :])
                        nc.tensor.transpose(psA[u][0:IC, P:2 * P], act32[u][:, P:I], ident32[:, :]).then_inc(a_turned, 1)
                    if last_kind:
                        u = c % 2
                        at = at_of[c]
                        pe.wait_ge(aT_lo_done, t - 1)
                        parts = ((aT_hi[u], 0, P), (aT_tail[u], 1, P), (aT_lo[u], 0, P), (aT_hi[u], 2, P), (aT_tail[u], 3, IC))
                        for n, (part, q, rows) in enumerate(parts):
                            last = nc.tensor.matmul(psY[u], part[0:rows], W[0:rows, bass.ds(at + GUW + q * H, H)], start=(n == 0), stop=(n == len(parts) - 1))
                        last.then_inc(y_ready, 1)

            def project(dst, st, c, which, acted, ready):
                n = HC * st.b + c
                if not (isinstance(n, int) and n == 0):
                    pe.wait_ge(acted, n)
                for h in range(HC):
                    last = nc.tensor.matmul(dst[:, :], wqkv_sb[:, h, which * H + c * P:which * H + (c + 1) * P], xnT[:, h, :],
                                            start=(h == 0), stop=(h == HC - 1))
                last.then_inc(ready, 1)

            def step(st):
                b = st.b
                if st.now:
                    pe.wait_ge(xnT_ready, HC * b + HC)
                    project(psK, st, 0, 1, k_acted, k_ready)
                if st.before:
                    den(b)
                if st.now:
                    project(psQ, st, 0, 0, q_acted, q_ready)
                if st.before:
                    pe.wait_ge(rden_spread, b)
                    for c in range(HC):
                        for j in range(TS):
                            last = nc.tensor.transpose(psD[:, c, j * P:(j + 1) * P], rden_rows[:, j, c * P:(c + 1) * P], ident32[:, :])
                    last.then_inc(rden_turned, 1)
                if st.now:
                    project(psV, st, 0, 2, kv_done, v_ready)
                if st.before:
                    pe.wait_ge(attn_done, HC * b)
                    for j in range(TS):
                        for c in range(HC):
                            last = nc.tensor.matmul(psD[:, j // 2, (j % 2) * H:(j % 2 + 1) * H], attnT[:, c, j * P:(j + 1) * P],
                                                    wout_sb[:, c, :], start=(c == 0), stop=(c == HC - 1))
                        if j % 2:
                            last.then_inc(proj_ready, 1)
                if st.now:
                    project(psK, st, 1, 1, k_acted, k_ready)
                prep_in(st, 0)
                if st.now:
                    project(psQ, st, 1, 0, q_acted, q_ready)
                prep_in(st, 1)
                if st.now:
                    project(psV, st, 1, 2, kv_done, v_ready)
                prep_in(st, 2)
                if st.after:
                    for c in range(HC):
                        wait_bank(pe, "xn", c, st)
                    xn_in(b + 1)
                for n in range(3, 6):
                    prep_in(st, n)
                if st.before:
                    for j in range(TS):
                        if j % 2 == 0:
                            pe.wait_ge(split_done, 2 * (b - 1) + j // 2 + 1)
                        wait_bank(pe, "xn2", j, st)
                        bank = bank_of("xn2", j)[:, 0:H].bitcast(f16)
                        for s in range(2):
                            for c in range(HC):
                                last = nc.tensor.transpose(bank[:, (s * HC + c) * P:(s * HC + c + 1) * P],
                                                           xn2_split[:, j, s, c * P:(c + 1) * P], ident16[:, :])
                        last.then_inc(xn2_transposed, 1)
                        if j >= 1:
                            route(b, j - 1)
                    route(b, TS - 1)
                for n in range(6, 9):
                    prep_in(st, n)

            def route(b, j):
                pe.wait_ge(xT2_ready, TS * (b - 1) + j + 1)
                if j == 0:
                    pe.wait_ge(x1_done, 2 * b)
                n = 0
                for sx, sw in ((0, 0), (0, 1), (1, 0)):
                    for c in range(HC):
                        last = nc.tensor.matmul(psD[:, 0, j * E:(j + 1) * E], xT2[j % 2][:, sx, c, :], rwT[:, c, sw, :],
                                                start=(n == 0), stop=(n == 3 * HC - 1))
                        n += 1
                last.then_inc(logits_ready, 1)

            def den(b):
                pe.wait_ge(qks_done, HC * b)
                pe.wait_ge(logits_done, b)
                for c in range(HC):
                    for j in range(TS):
                        n = j * HEADS + c * P // D
                        last = nc.tensor.matmul(psD[:, 0, n:n + P // D], qks[c][:, j * P:(j + 1) * P], head_sums, start=True, stop=True)
                last.then_inc(den_ready, 1)

            pe.wait_ge(setup_dve, 3)
            pe.wait_ge(wattn_loaded, 32)
            xn_in(0)
            steps(pe, step)
            late_and_dispatch()
            rounds(pe, pe_round)


_INS = ['L0_attn_x', 'L0_attn_w_qkv', 'L0_attn_w_out', 'L0_attn_decay_param', 'L0_ffn_router_w', 'L0_ffn_router_b',
        'L0_ffn_gate_w', 'L0_ffn_up_w', 'L0_ffn_down_w', 'L0_ffn_shared_gate_w', 'L0_ffn_shared_up_w', 'L0_ffn_shared_down_w']
_OUTS = [((8, 512, 256), 'float32')]


def kernel(**inputs):
    import numpy as _np
    import concourse.bacc as _bacc
    from concourse import mybir as _mybir
    from concourse.bass_utils import run_bass_kernel_spmd as _run

    nc = _bacc.Bacc("TRN2", target_bir_lowering=False, num_devices=1)
    arrays, args = {}, []
    for name in _INS:
        a = _np.ascontiguousarray(inputs[name])
        arrays[f"in_{name}_dram"] = a
        args.append(nc.dram_tensor(f"in_{name}_dram", a.shape, _mybir.dt.from_np(a.dtype), kind="ExternalInput").ap())
    for i, (shape, dtype) in enumerate(_OUTS):
        dt = _mybir.dt.from_np(_np.dtype(dtype))
        args.append(nc.dram_tensor(f"out_{i}_dram", shape, dt, kind="ExternalOutput").ap())
    moe_block(nc, *args)
    r = _run(nc, [arrays], core_ids=[0])
    got = tuple(r.results[0][f"out_{i}_dram"] for i in range(len(_OUTS)))
    return got[0]
```
